# Optimizing a Trainium2 kernel written in Bass

```python
import numpy as np
import jax
import jax.numpy as jnp

def _softmax(x, axis=-1):
    return jax.nn.softmax(x, axis=axis)

def _gelu(x):
    return jax.nn.gelu(x, approximate=True)

def _silu(x):
    return jax.nn.silu(x)

def _sigmoid(x):
    return jax.nn.sigmoid(x)

def _layernorm(x, axis=-1, eps=1e-05):
    m = jnp.mean(x, axis=axis, keepdims=True)
    v = jnp.var(x, axis=axis, keepdims=True)
    return (x - m) / jnp.sqrt(v + eps)

def _scatter_add(tgt, idx, src, axis=0):
    return tgt.at[idx].add(src)

def _segment_sum(src, seg, n):
    return jax.ops.segment_sum(src, seg, n)
kernel_name = 'mk_xattn_ffn_d1_seqx_r2_6e24f9'

def setup_inputs(seed: int=0):
    np.random.seed(seed)
    _w = jnp.asarray

    def _rec_inputs():
        import jax
        import jax.numpy as jnp
        _rk = jax.random.key(seed)
        x = 7.22e-05 + 1 * jax.random.normal(jax.random.fold_in(_rk, 1), (16, 512, 1024), jnp.float32)
        _lenS = 512 - jax.random.randint(jax.random.fold_in(_rk, 7), (16,), 0, max(1, 512 // 4) + 1, jnp.int32)
        _lenS2 = 512 - jax.random.randint(jax.random.fold_in(_rk, 8), (16,), 0, max(1, 512 // 4) + 1, jnp.int32)
        _ctx_512P = jax.random.normal(jax.random.fold_in(_rk, 11), (16, 16, 256), jnp.float32)
        _ctx_512c = jax.random.dirichlet(jax.random.fold_in(_rk, 511), 0.3 * jnp.ones((16,), jnp.float32), (16, 512))
        _ctx_512t = jnp.einsum('bsk,bkd->bsd', _ctx_512c, _ctx_512P)
        _ctx_512t = _ctx_512t * jax.lax.rsqrt(jnp.mean(jnp.square(_ctx_512t)) + 1e-12) * 0.953939
        ctx_512 = -0.000514642 + 1.00011 * (_ctx_512t + 0.3 * jax.random.normal(jax.random.fold_in(_rk, 611), (16, 512, 256), jnp.float32))
        return (x, ctx_512)
    x, ctx_512 = _rec_inputs()

    def _L0_xattn_setup():
        import jax, jax.numpy as jnp
        import numpy as np
        import math
        D_MODEL = 1024
        N_HEADS = 16
        N_GROUPS = 4
        HEADS_PER_GROUP = N_HEADS // N_GROUPS
        HEAD_DIM = D_MODEL // N_HEADS
        B, S = (2, 1024)
        key = jax.random.key(seed)
        k1, k2, k3, k4, k5 = jax.random.split(key, 5)
        q = jax.random.normal(k1, (B, S, D_MODEL), dtype=jnp.float32)
        k = jax.random.normal(k2, (B, S, N_GROUPS * HEAD_DIM), dtype=jnp.float32)
        v = jax.random.normal(k3, (B, S, N_GROUPS * HEAD_DIM), dtype=jnp.float32)
        lim = 1.0 / math.sqrt(D_MODEL)
        Wc = jax.random.uniform(k4, (D_MODEL, D_MODEL), minval=-lim, maxval=lim, dtype=jnp.float32)
        bc = jax.random.uniform(k5, (D_MODEL,), minval=-lim, maxval=lim, dtype=jnp.float32)
        return {'q': q, 'k': k, 'v': v, 'Wc': Wc, 'bc': bc}
    _L0_xattn_all = _L0_xattn_setup()
    _L0_xattn_in = {k: v for k, v in _L0_xattn_all.items() if k in ('Wc', 'bc')}
    del _L0_xattn_all

    def _L0_ffn_setup():
        import jax, jax.numpy as jnp
        import numpy as np
        TOP_K = 8
        NUM_EXPERTS = 32
        key = jax.random.key(seed)
        k1, k2, k3, k4, k5 = jax.random.split(key, 5)
        B, S, D, M, E = (4, 512, 1024, 384, NUM_EXPERTS)
        return {'hidden_states': jax.random.normal(k1, (B, S, D), dtype=jnp.float32), 'gate_kernel': jax.random.normal(k2, (D, E), dtype=jnp.float32) * 0.02, 'gate_proj': jax.random.normal(k3, (E, D, M), dtype=jnp.float32) * 0.02, 'up_proj': jax.random.normal(k4, (E, D, M), dtype=jnp.float32) * 0.02, 'down_proj': jax.random.normal(k5, (E, M, D), dtype=jnp.float32) * 0.02}
    _L0_ffn_all = _L0_ffn_setup()
    _L0_ffn_in = {k: v for k, v in _L0_ffn_all.items() if k in ('gate_kernel', 'gate_proj', 'up_proj', 'down_proj')}
    del _L0_ffn_all
    return {'x': x, 'ctx_512': ctx_512, 'L0_xattn_Wc': _L0_xattn_in['Wc'], 'L0_xattn_bc': _L0_xattn_in['bc'], 'L0_ffn_gate_kernel': _L0_ffn_in['gate_kernel'], 'L0_ffn_gate_proj': _L0_ffn_in['gate_proj'], 'L0_ffn_up_proj': _L0_ffn_in['up_proj'], 'L0_ffn_down_proj': _L0_ffn_in['down_proj']}

def reference(x, ctx_512, L0_xattn_Wc, L0_xattn_bc, L0_ffn_gate_kernel, L0_ffn_gate_proj, L0_ffn_up_proj, L0_ffn_down_proj):
    import jax
    import jax.numpy as jnp

    def _L0_xattn_ref(q, k, v, Wc, bc):
        import jax, jax.numpy as jnp
        import numpy as np
        import math
        D_MODEL = 1024
        N_HEADS = 16
        N_GROUPS = 4
        HEADS_PER_GROUP = N_HEADS // N_GROUPS
        HEAD_DIM = D_MODEL // N_HEADS
        B, S = (2, 1024)
        b, s, _ = q.shape
        qh = q.reshape(b, s, N_GROUPS, HEADS_PER_GROUP, HEAD_DIM).transpose(0, 2, 3, 1, 4)
        kh = k.reshape(b, s, N_GROUPS, HEAD_DIM).transpose(0, 2, 1, 3)
        vh = v.reshape(b, s, N_GROUPS, HEAD_DIM).transpose(0, 2, 1, 3)
        scale = 1.0 / math.sqrt(HEAD_DIM)
        scores = jnp.einsum('bghsd,bgtd->bghst', qh, kh) * scale
        probs = jax.nn.softmax(scores, axis=-1)
        out = jnp.einsum('bghst,bgtd->bghsd', probs, vh)
        out = out.transpose(0, 3, 1, 2, 4).reshape(b, s, D_MODEL)
        return out @ Wc.T + bc

    def _L0_ffn_ref(hidden_states, gate_kernel, gate_proj, up_proj, down_proj):
        import jax, jax.numpy as jnp
        import numpy as np
        TOP_K = 8
        NUM_EXPERTS = 32
        B, S, D = hidden_states.shape
        T = B * S
        x2d = hidden_states.reshape(T, D)
        router_logits = x2d @ gate_kernel
        routing_weights = jax.nn.softmax(router_logits, axis=-1)
        routing_weights, selected_experts = jax.lax.top_k(routing_weights, TOP_K)
        routing_weights = routing_weights / jnp.sum(routing_weights, axis=-1, keepdims=True)
        flat_experts = selected_experts.reshape(-1)
        sort_idx = jnp.argsort(flat_experts)
        token_rows = sort_idx // TOP_K
        sorted_inputs = jnp.take(x2d, token_rows, axis=0)
        group_sizes = jnp.bincount(flat_experts, length=NUM_EXPERTS).astype(jnp.int32)
        w0 = jax.lax.ragged_dot(sorted_inputs, gate_proj, group_sizes, preferred_element_type=jnp.float32)
        w1 = jax.lax.ragged_dot(sorted_inputs, up_proj, group_sizes, preferred_element_type=jnp.float32)
        inter = jax.nn.silu(w0) * w1
        expert_out = jax.lax.ragged_dot(inter, down_proj, group_sizes, preferred_element_type=jnp.float32)
        unsorted = jnp.take(expert_out, jnp.argsort(sort_idx), axis=0)
        per_token = unsorted.reshape(T, TOP_K, D)
        output = jnp.einsum('BKE,BK->BE', per_token.astype(jnp.float32), routing_weights.astype(jnp.float32))
        return output.reshape(B, S, D)
    x = x + _L0_xattn_ref(_layernorm(x, axis=-1), ctx_512, ctx_512, L0_xattn_Wc, L0_xattn_bc)
    x = x + _L0_ffn_ref(_layernorm(x, axis=-1), L0_ffn_gate_kernel, L0_ffn_gate_proj, L0_ffn_up_proj, L0_ffn_down_proj)
    return x

_drawn_inputs = setup_inputs


def setup_inputs(seed=0):
    import zlib

    import numpy as np

    out = dict(_drawn_inputs(seed))
    spreads = {}
    factors = {'L0_xattn_bc': 3.327}
    for name, (base, spread) in spreads.items():
        noise = np.random.default_rng([zlib.crc32(name.encode()), seed]).standard_normal(out[name].shape)
        drawn = base * np.exp(spread * noise) if base else spread * noise
        out[name] = jnp.asarray(drawn.astype(out[name].dtype))
    for name, factor in factors.items():
        out[name] = (out[name] * factor).astype(out[name].dtype)
    return out
```

```python
import concourse.bass as bass
from concourse import mybir
from contextlib import ExitStack

F32 = mybir.dt.float32
F32R = mybir.dt.float32r
BF16 = mybir.dt.bfloat16
I32 = mybir.dt.int32
U32 = mybir.dt.uint32
ALU = mybir.AluOpType
ACT = mybir.ActivationFunctionType
AX = mybir.AxisListType
P = 128
EPS = 1e-5
TOP_K = 8
HEAD_DIM = 64
GROUP_HEADS = 4
SLOT_ROWS = 512


def wait(eng, sem, value):
    if isinstance(value, int) and value <= 0:
        return
    eng.wait_ge(sem, value)


class Chain:

    def __init__(self, eng, sem, before, each):
        self.eng, self.sem, self.before, self.each, self.n = eng, sem, before, each, 0

    def then(self, instruction):
        instruction.then_inc(self.sem, 1)
        self.n += 1
        self.eng.wait_ge(self.sem, self.before + self.n)

    def done(self):
        assert self.n == self.each, (self.n, self.each)


def moe_block(nc, x, ctx_in, Wc, bc, gate_w, gate_proj, up_proj, down_proj, out):
    B, S, D = x.shape
    CD = ctx_in.shape[2]
    E, _, M = gate_proj.shape
    T = B * S
    DC = D // P
    MC = M // P
    TC = ctx_in.shape[1] // P
    SC = S // P
    H = D // HEAD_DIM
    G = H // GROUP_HEADS
    HALF = 512
    NH = D // HALF
    TILES = T // P
    PAD_ROW = T
    TABLE_PAD = E * T
    TABLE_ROWS = TABLE_PAD + SLOT_ROWS
    QUARTERS = SLOT_ROWS // P
    MOST_TILES = (T * TOP_K + E * (SLOT_ROWS - 1)) // SLOT_ROWS
    SCHED_COLS = (MOST_TILES + 1 + P - 1) // P
    SCHED = SCHED_COLS * P
    assert CD == G * HEAD_DIM and TC * P == 512 and S == 512 and QUARTERS == 4

    x_rows = x.rearrange("b s d -> (b s) d")
    ctx_v = ctx_in.rearrange("b (c p) d -> p b c d", p=P)
    gate_v = gate_proj.rearrange("e (c p) m -> e p c m", p=P)
    up_v = up_proj.rearrange("e (c p) m -> e p c m", p=P)
    down_v = down_proj.rearrange("e (c p) d -> e p c d", p=P)

    xn_dram = nc.dram_tensor("xn_rows", (T + SLOT_ROWS, D), F32, kind="Internal").ap()
    table = nc.dram_tensor("slot_table", (TABLE_ROWS, 2), I32, kind="Internal").ap()
    sched_dram = nc.dram_tensor("tile_schedule", (SCHED, 4), I32, kind="Internal").ap()

    top = ExitStack()
    with top:
        def sb(ctx, name, shape, dt):
            return ctx.enter_context(nc.sbuf_tensor(name, shape, dt))

        def sem(name):
            return top.enter_context(nc.semaphore(name))

        banks = [top.enter_context(nc.psum_tensor(f"bank{n}", [P, 512], F32)) for n in range(8)]

        ident = sb(top, "ident", [P, P], F32)
        slot_base = sb(top, "slot_base", [P, E], F32)
        expert_base = sb(top, "expert_base", [P, E], F32)

        attention_mem = ExitStack()
        with attention_mem:
            WcT_hi = sb(attention_mem, "WcT_hi", [P, DC, D], F32R)
            WcT_lo = sb(attention_mem, "WcT_lo", [P, DC, D], F32R)
            ident_r = sb(attention_mem, "ident_r", [P, P], F32R)
            before_bf = sb(attention_mem, "before_bf", [P, P], BF16)
            ones_bf = sb(attention_mem, "ones_bf", [P, P], BF16)
            gate_sb = sb(attention_mem, "gate_sb", [P, DC, E], F32)
            bias_row = sb(attention_mem, "bias_row", [P, D], F32)
            iota_e = sb(attention_mem, "iota_e", [P, E], F32)
            token_id = sb(attention_mem, "token_id", [P, 1], F32)
            eps = sb(attention_mem, "eps", [P, 1], F32)

            setup_stage(nc, sb, sem, banks, Wc, bc, gate_w, xn_dram, table, out, ident, ident_r, before_bf,
                        ones_bf, gate_sb, bias_row, iota_e, token_id, eps, slot_base, expert_base, WcT_hi, WcT_lo,
                        D=D, DC=DC, E=E, T=T, TABLE_ROWS=TABLE_ROWS)

            x_t = [sb(attention_mem, f"x_t{n}", [P, D], F32) for n in range(SC)]
            xn = sb(attention_mem, "xn", [P, D], F32)
            xq = sb(attention_mem, "xq", [P, H, 2, HEAD_DIM], F32R)
            qT = sb(attention_mem, "qT", [P, H, P], F32R)
            ctx_sb = sb(attention_mem, "ctx_sb", [P, TC, CD], F32)
            v_hi = sb(attention_mem, "v_hi", [P, TC, G, P], F32R)
            v_lo = sb(attention_mem, "v_lo", [P, TC, G, P], F32R)
            kT_hi = sb(attention_mem, "kT_hi", [P, G, 512], F32R)
            kT_lo = sb(attention_mem, "kT_lo", [P, G, 512], F32R)
            probs = [sb(attention_mem, f"probs{n}", [P, 512], F32) for n in range(2)]
            pT_hi = [sb(attention_mem, f"pT_hi{n}", [P, TC, GROUP_HEADS, P], F32R) for n in range(2)]
            pT_lo = [sb(attention_mem, f"pT_lo{n}", [P, TC, GROUP_HEADS, P], F32R) for n in range(2)]
            oT_hi = sb(attention_mem, "oT_hi", [P, DC, P], F32R)
            oT_lo = sb(attention_mem, "oT_lo", [P, DC, P], F32R)
            x2 = sb(attention_mem, "x2", [P, D], F32)
            xn2 = sb(attention_mem, "xn2", [P, D], F32)
            xn2T = sb(attention_mem, "xn2T", [P, DC, P], F32)
            neg_max = sb(attention_mem, "neg_max", [P, H], F32)
            row_sum = sb(attention_mem, "row_sum", [P, H], F32)
            row_inv = sb(attention_mem, "row_inv", [P, H], F32)
            bn1 = sb(attention_mem, "bn1", [P, 2, 6], F32)
            mv1 = sb(attention_mem, "mv1", [P, 2], F32)
            ln1 = sb(attention_mem, "ln1", [P, 8], F32)
            bn2 = sb(attention_mem, "bn2", [P, 2, 6], F32)
            mv2 = sb(attention_mem, "mv2", [P, 2], F32)
            ln2 = sb(attention_mem, "ln2", [P, 8], F32)
            LOG, SEED, VAR, SQ, ERR, FIX, SCALE, SHIFT = range(8)
            FACTOR_STEPS = 5
            logits = sb(attention_mem, "logits", [P, E], F32)
            top_v = sb(attention_mem, "top_v", [P, TOP_K], F32)
            top_i = sb(attention_mem, "top_i", [P, TOP_K], U32)
            top_f = sb(attention_mem, "top_f", [P, TOP_K], F32)
            neg_top = sb(attention_mem, "neg_top", [P, 1], F32)
            top_e = sb(attention_mem, "top_e", [P, TOP_K], F32)
            top_s = sb(attention_mem, "top_s", [P, 1], F32)
            top_inv = sb(attention_mem, "top_inv", [P, 1], F32)
            hot = sb(attention_mem, "hot", [P, TOP_K, E], F32)
            hot_pos = sb(attention_mem, "hot_pos", [P, TOP_K, E], F32)
            chosen = sb(attention_mem, "chosen", [P, E], BF16)
            pos = sb(attention_mem, "pos", [P, E], F32)
            slot_i = sb(attention_mem, "slot_i", [P, TOP_K], I32)
            entry = sb(attention_mem, "entry", [P, TOP_K, 2], I32)

            S_BANK, PT_BANK, O_BANK, MISC = banks[0:2], banks[2:4], banks[4:6], banks[6:8]

            x_in = [sem(f"x_in{s}") for s in range(SC)]
            ctx_loaded = sem("ctx_loaded")
            x2_stored = sem("x2_stored")
            xn2_stored = sem("xn2_stored")
            table_written = sem("table_written")
            ln1_chain, stats1, pool1_chain, ln1_ready = sem("ln1_chain"), sem("stats1"), sem("pool1_chain"), sem("ln1_ready")
            log1_ready, seed1_ready, log2_ready, seed2_ready = sem("log1_ready"), sem("seed1_ready"), sem("log2_ready"), sem("seed2_ready")
            xn_ready, xq_hi_ready, xq_ready, xbias_ready = sem("xn_ready"), sem("xq_hi_ready"), sem("xq_ready"), sem("xbias_ready")
            qt_done, qt_copied = sem("qt_done"), sem("qt_copied")
            vhi_ready, vlo_ready, kt_done = sem("vhi_ready"), sem("vlo_ready"), sem("kt_done")
            kthi_copied, ktlo_copied = sem("kthi_copied"), sem("ktlo_copied")
            scores_done, max_ready, exp_ready, probs_ready = sem("scores_done"), sem("max_ready"), sem("exp_ready"), sem("probs_ready")
            inverse_ready = sem("inverse_ready")
            pt_done, pthi_copied, ptlo_copied = sem("pt_done"), sem("pthi_copied"), sem("ptlo_copied")
            pv_done, othi_copied, otlo_copied = sem("pv_done"), sem("othi_copied"), sem("otlo_copied")
            wo_done, x2_ready, back_chain, stats2 = sem("wo_done"), sem("x2_ready"), sem("back_chain"), sem("stats2")
            pool2_chain, ln2_ready, xn2_ready = sem("pool2_chain"), sem("ln2_ready"), sem("xn2_ready")
            xt2_done, xt2_copied, router_done, logits_copied = sem("xt2_done"), sem("xt2_copied"), sem("router_done"), sem("logits_copied")
            top_ready, topexp_ready, chosen_ready, rank_done = sem("top_ready"), sem("topexp_ready"), sem("chosen_ready"), sem("rank_done")
            rank_copied, entry_ready = sem("rank_copied"), sem("entry_ready")
            fence = {n: sem(f"fence_{n}") for n in ("dve", "pool")}

            BACK_STEPS = 14
            COPY_OUT = (8, 9, 12)

            def tiles_of_a_batch(b, body):
                for s in range(SC):
                    body(b, s, b * SC + s, not (isinstance(b, int) and b == 0 and s == 0))

            block = attention_mem.enter_context(nc.Block())

            @block.sync
            def _(sp):
                def store(j):
                    sp.wait_ge(x2_ready, 2 * j + 2)
                    sp.dma_start(out[bass.ds(j * P, P), :], x2[:, :]).then_inc(x2_stored, 16)
                    sp.wait_ge(xn2_ready, j + 1)
                    sp.dma_start(xn_dram[bass.ds(j * P, P), :], xn2[:, :]).then_inc(xn2_stored, 16)

                def batch(b):
                    wait(sp, vhi_ready, b)
                    wait(sp, vlo_ready, b)
                    sp.dma_start(ctx_sb[:, :, :], ctx_v[:, bass.ds(b, 1), :, :].rearrange("p b c d -> p (b c) d")
                                 ).then_inc(ctx_loaded, 16)

                    def tile(b, s, i, _):
                        wait(sp, x2_ready, 2 * (i - SC) + 2)
                        sp.dma_start(x_t[s][:, :], x_rows[bass.ds(i * P, P), :]).then_inc(x_in[s], 16)
                        if not (isinstance(b, int) and b == 0 and s < 2):
                            store(i - 2)
                    tiles_of_a_batch(b, tile)

                batch(0)
                with sp.Fori(1, B) as b:
                    batch(b)
                store(TILES - 2)
                store(TILES - 1)
                sp.wait_ge(x2_stored, 16 * TILES)
                sp.wait_ge(xn2_stored, 16 * TILES)

            @block.gpsimd
            def _(pool):
                def hold(semaphore, value):
                    if isinstance(value, int) and value <= 0:
                        return
                    pool.wait_ge(semaphore, value)
                    pool.sem_inc(fence["pool"], 1)

                def factors(f, mv, scale, chain, before, signal):
                    pool.tensor_scalar(f[:, VAR:VAR + 1], mv[:, 1:2], EPS, None, ALU.add).then_inc(chain, 1)
                    pool.tensor_tensor(f[:, SQ:SQ + 1], f[:, SEED:SEED + 1], f[:, SEED:SEED + 1], ALU.mult).then_inc(chain, 1)
                    hold(chain, before + 2)
                    pool.tensor_tensor(f[:, ERR:ERR + 1], f[:, SQ:SQ + 1], f[:, VAR:VAR + 1], ALU.mult).then_inc(chain, 1)
                    hold(chain, before + 3)
                    pool.tensor_scalar(f[:, FIX:FIX + 1], f[:, ERR:ERR + 1], -0.5, 1.5, ALU.mult, ALU.add).then_inc(chain, 1)
                    hold(chain, before + 4)
                    pool.tensor_scalar(f[:, SCALE:SCALE + 1], f[:, FIX:FIX + 1], f[:, SEED:SEED + 1], scale,
                                       ALU.mult, ALU.mult).then_inc(chain, 1)
                    hold(chain, before + FACTOR_STEPS)
                    pool.tensor_scalar(f[:, SHIFT:SHIFT + 1], mv[:, 0:1], f[:, SCALE:SCALE + 1], -1.0, ALU.mult, ALU.mult
                                       ).then_inc(signal, 1)

                def factors1(i):
                    hold(seed1_ready, i + 1)
                    hold(xn_ready, i)
                    factors(ln1, mv1, HEAD_DIM ** -0.5, pool1_chain, FACTOR_STEPS * i, ln1_ready)

                def queries(i, s):
                    hold(xn_ready, i + 1)
                    hold(qt_done, 4 * i)
                    heads = xn[:, :].rearrange("p (h d) -> p h d", d=HEAD_DIM)
                    pool.tensor_copy(xq[:, :, 0, :], heads).then_inc(xq_hi_ready, 1)
                    hold(xq_hi_ready, i + 1)
                    pool.tensor_tensor(xq[:, :, 1, :], heads, xq[:, :, 0, :].bitcast(F32), ALU.subtract).then_inc(xq_ready, 1)
                    pool.tensor_tensor(x_t[s][:, :], x_t[s][:, :], bias_row[:, :], ALU.add).then_inc(xbias_ready, 1)

                def factors2(j):
                    hold(seed2_ready, j + 1)
                    hold(xn2_ready, j)
                    factors(ln2, mv2, 1.0, pool2_chain, FACTOR_STEPS * j, ln2_ready)

                def scatter(j):
                    hold(entry_ready, j + 1)
                    for k in range(TOP_K):
                        pool.indirect_dma_start(
                            out=table, out_offset=bass.IndirectOffsetOnAxis(ap=slot_i[:, k:k + 1], axis=0),
                            in_=entry[:, k, :], in_offset=None, bounds_check=TABLE_ROWS - 1, oob_is_err=True,
                        ).then_inc(table_written, 16)

                def batch(b):
                    def tile(b, s, i, back):
                        if s == 0:
                            factors1(i)
                            queries(i, s)
                        if s < SC - 1:
                            factors1(i + 1)
                        if back:
                            factors2(i - 1)
                        if s < SC - 1:
                            queries(i + 1, s + 1)
                        if back:
                            scatter(i - 1)
                    tiles_of_a_batch(b, tile)

                batch(0)
                with pool.Fori(1, B) as b:
                    batch(b)
                factors2(TILES - 1)
                scatter(TILES - 1)
                pool.wait_ge(table_written, 16 * TOP_K * TILES)

            @block.scalar
            def _(act):
                def seed(i, f, mv, stats, log_ready, ready, taken):
                    act.wait_ge(stats, i + 1)
                    wait(act, taken, i)
                    act.activation(f[:, LOG:LOG + 1], mv[:, 1:2], ACT.Ln, bias=eps[:, :]).then_inc(log_ready, 1)
                    act.wait_ge(log_ready, i + 1)
                    act.activation(f[:, SEED:SEED + 1], f[:, LOG:LOG + 1], ACT.Exp, scale=-0.5).then_inc(ready, 1)

                def seed1(i):
                    seed(i, ln1, mv1, stats1, log1_ready, seed1_ready, ln1_ready)

                def seed2(j):
                    seed(j, ln2, mv2, stats2, log2_ready, seed2_ready, ln2_ready)

                def normalise1(i, s):
                    act.wait_ge(ln1_ready, i + 1)
                    wait(act, xq_ready, i)
                    act.activation(xn[:, :], x_t[s][:, :], ACT.Identity, bias=ln1[:, SHIFT:SHIFT + 1], scale=ln1[:, SCALE:SCALE + 1]
                                   ).then_inc(xn_ready, 1)

                def copy_queries(i):
                    for n in range(4):
                        act.wait_ge(qt_done, 4 * i + n + 1)
                        act.activation(qT[:, 4 * n:4 * n + 4, :], MISC[n % 2][:, :].rearrange("p (h t) -> p h t", h=4),
                                       ACT.Copy).then_inc(qt_copied, 1)

                def values_hi(b):
                    act.wait_ge(ctx_loaded, 16 * b + 16)
                    wait(act, pv_done, G * SC * b)
                    src = ctx_sb[:, :, :].rearrange("p c (g d) -> p (c g) d", d=HEAD_DIM)
                    act.activation(v_hi[:, :, :, :].rearrange("p c g (two d) -> p (c g) two d", two=2),
                                   src.unsqueeze(2).to_broadcast([P, TC * G, 2, HEAD_DIM]), ACT.Copy).then_inc(vhi_ready, 1)

                def copy_keys_hi(b):
                    for g in range(G):
                        act.wait_ge(kt_done, 2 * G * b + 2 * g + 1)
                        act.activation(kT_hi[:, g, :], MISC[0][:, :], ACT.Copy).then_inc(kthi_copied, 1)

                def exponent(i, h):
                    act.wait_ge(max_ready, H * i + h + 1)
                    wait(act, pt_done, H * i + h - 1)
                    act.activation(probs[h % 2][:, :], S_BANK[h % 2][:, :], ACT.Exp, bias=neg_max[:, h:h + 1],
                                   accum_out=row_sum[:, h:h + 1]).then_inc(exp_ready, 1)

                def copy_probs_hi(i, h):
                    g, k = divmod(h, GROUP_HEADS)
                    act.wait_ge(pt_done, H * i + h + 1)
                    if k == 0:
                        wait(act, pv_done, G * i + g - 1)
                    act.activation(pT_hi[g % 2][:, :, k, :], PT_BANK[h % 2][:, :].rearrange("p (c t) -> p c t", c=TC),
                                   ACT.Copy).then_inc(pthi_copied, 1)

                def copy_out_hi(i, g):
                    act.wait_ge(pv_done, G * i + g + 1)
                    if g == 0:
                        wait(act, wo_done, NH * i)
                    for r in range(2):
                        rows = slice(HEAD_DIM * r, HEAD_DIM * (r + 1))
                        act.activation(oT_hi[rows, 2 * g:2 * g + 2, :],
                                       O_BANK[g % 2][rows, :].rearrange("p (a two t) -> p a two t", two=2, t=P)[:, :, r, :],
                                       ACT.Copy).then_inc(othi_copied, 1)

                def normalise2(j):
                    act.wait_ge(ln2_ready, j + 1)
                    wait(act, xn2_stored, 16 * j)
                    wait(act, xt2_done, 2 * j)
                    act.activation(xn2[:, :], x2[:, :], ACT.Identity, bias=ln2[:, SHIFT:SHIFT + 1], scale=ln2[:, SCALE:SCALE + 1]
                                   ).then_inc(xn2_ready, 1)

                def copy_xn2(j):
                    for n in range(2):
                        act.wait_ge(xt2_done, 2 * j + n + 1)
                        if n == 0:
                            wait(act, router_done, j)
                        act.activation(xn2T[:, 4 * n:4 * n + 4, :], MISC[n][:, :].rearrange("p (c t) -> p c t", c=4),
                                       ACT.Copy).then_inc(xt2_copied, 1)

                def top_exponent(j):
                    act.wait_ge(top_ready, j + 1)
                    wait(act, entry_ready, j)
                    act.activation(top_e[:, :], top_v[:, :], ACT.Exp, bias=neg_top[:, :], accum_out=top_s[:, :]
                                   ).then_inc(topexp_ready, 1)

                def batch(b):
                    def tile(b, s, i, back):
                        if s == 0:
                            seed1(i)
                            if back:
                                copy_out_hi(i - 1, G - 1)
                            values_hi(b)
                            normalise1(i, s)
                            if back:
                                seed2(i - 1)
                            copy_queries(i)
                            copy_keys_hi(b)
                        exponent(i, 0)
                        exponent(i, 1)
                        if s > 0:
                            copy_out_hi(i - 1, G - 1)
                        for h in range(H):
                            copy_probs_hi(i, h)
                            if h + 2 < H:
                                exponent(i, h + 2)
                            if h in COPY_OUT:
                                copy_out_hi(i, COPY_OUT.index(h))
                            if h == 6 and s < SC - 1:
                                seed1(i + 1)
                            if h == 8 and s > 0:
                                seed2(i - 1)
                            if h == 7 and s < SC - 1:
                                normalise1(i + 1, s + 1)
                            if h == 9 and back:
                                normalise2(i - 1)
                            if h == 11 and back:
                                copy_xn2(i - 1)
                            if h == 13 and back:
                                top_exponent(i - 1)
                        if s < SC - 1:
                            copy_queries(i + 1)
                    tiles_of_a_batch(b, tile)

                batch(0)
                with act.Fori(1, B) as b:
                    batch(b)
                copy_out_hi(TILES - 1, G - 1)
                seed2(TILES - 1)
                normalise2(TILES - 1)
                copy_xn2(TILES - 1)
                top_exponent(TILES - 1)

            @block.vector
            def _(dve):
                def statistics(chain, bn, mv, rows, signal):
                    dve.bn_stats(bn[:, 0, :], rows[:, 0:512]).then_inc(chain.sem, 1)
                    dve.bn_stats(bn[:, 1, :], rows[:, 512:1024]).then_inc(chain.sem, 1)
                    chain.n += 2
                    dve.wait_ge(chain.sem, chain.before + chain.n)
                    dve.sem_inc(fence["dve"], 1)
                    dve.bn_aggr(mv[:, :], bn[:, :, :]).then_inc(signal, 1)

                def statistics1(i, s):
                    chain = Chain(dve, ln1_chain, 2 * i, 2)
                    dve.wait_ge(x_in[s], (i - s) * (16 // SC) + 16)
                    wait(dve, ln1_ready, i)
                    statistics(chain, bn1, mv1, x_t[s], stats1)
                    chain.done()

                def values_lo(b):
                    dve.wait_ge(vhi_ready, b + 1)
                    src = ctx_sb[:, :, :].rearrange("p c (g d) -> p (c g) d", d=HEAD_DIM)
                    hi = v_hi[:, :, :, :].rearrange("p c g (two d) -> p (c g) two d", two=2)
                    lo = v_lo[:, :, :, :].rearrange("p c g (two d) -> p (c g) two d", two=2)
                    dve.tensor_tensor(lo, src.unsqueeze(2).to_broadcast([P, TC * G, 2, HEAD_DIM]), hi.bitcast(F32),
                                      ALU.subtract).then_inc(vlo_ready, 1)

                def copy_keys_lo(b):
                    for g in range(G):
                        dve.wait_ge(kt_done, 2 * G * b + 2 * g + 2)
                        dve.tensor_copy(kT_lo[:, g, :], MISC[1][:, :]).then_inc(ktlo_copied, 1)

                def maximum(i, h):
                    dve.wait_ge(scores_done, H * i + h + 1)
                    dve.tensor_reduce(neg_max[:, h:h + 1], S_BANK[h % 2][:, :], AX.X, ALU.max, negate=True
                                      ).then_inc(max_ready, 1)

                def normalise_probs(i, h):
                    dve.wait_ge(exp_ready, H * i + h + 1)
                    dve.reciprocal(row_inv[:, h:h + 1], row_sum[:, h:h + 1]).then_inc(inverse_ready, 1)
                    dve.wait_ge(inverse_ready, H * i + h + 1)
                    dve.tensor_scalar(probs[h % 2][:, :], probs[h % 2][:, :], row_inv[:, h:h + 1], None, ALU.mult
                                      ).then_inc(probs_ready, 1)

                def copy_probs_lo(i, h):
                    g, k = divmod(h, GROUP_HEADS)
                    dve.wait_ge(pthi_copied, H * i + h + 1)
                    dve.tensor_tensor(pT_lo[g % 2][:, :, k, :], PT_BANK[h % 2][:, :].rearrange("p (c t) -> p c t", c=TC),
                                      pT_hi[g % 2][:, :, k, :].bitcast(F32), ALU.subtract).then_inc(ptlo_copied, 1)

                def copy_out_lo(i, g):
                    dve.wait_ge(othi_copied, 2 * (G * i + g) + 2)
                    for r in range(2):
                        rows = slice(HEAD_DIM * r, HEAD_DIM * (r + 1))
                        dve.tensor_tensor(oT_lo[rows, 2 * g:2 * g + 2, :],
                                          O_BANK[g % 2][rows, :].rearrange("p (a two t) -> p a two t", two=2, t=P)[:, :, r, :],
                                          oT_hi[rows, 2 * g:2 * g + 2, :].bitcast(F32), ALU.subtract).then_inc(otlo_copied, 1)

                def residual(j, n, s):
                    cols = slice(n * HALF, (n + 1) * HALF)
                    dve.wait_ge(wo_done, NH * j + n + 1)
                    if n == 0:
                        dve.wait_ge(xbias_ready, j + 1)
                        wait(dve, x2_stored, 16 * j)
                        wait(dve, xn2_ready, j)
                    dve.tensor_tensor(x2[:, cols], MISC[n][:, :], x_t[s][:, cols], ALU.add).then_inc(x2_ready, 1)

                def statistics2(j):
                    dve.wait_ge(x2_ready, 2 * j + 2)
                    wait(dve, ln2_ready, j)
                    statistics(Chain(dve, back_chain, BACK_STEPS * j, 0), bn2, mv2, x2, stats2)

                def choose(j):
                    chain = Chain(dve, back_chain, BACK_STEPS * j + 2, 0)
                    dve.wait_ge(router_done, j + 1)
                    dve.tensor_copy(logits[:, :], MISC[0][:, 0:E]).then_inc(logits_copied, 1)
                    dve.wait_ge(logits_copied, j + 1)
                    dve.sem_inc(fence["dve"], 1)
                    chain.then(dve.max(top_v[:, :], logits[:, :]))
                    dve.tensor_scalar(neg_top[:, :], top_v[:, 0:1], -1.0, None, ALU.mult).then_inc(top_ready, 1)
                    chain.then(dve.max_index(top_i[:, :], top_v[:, :], logits[:, :]))
                    chain.then(dve.tensor_copy(top_f[:, :], top_i[:, :]))
                    chain.then(dve.tensor_tensor(hot[:, :, :], top_f[:, :].unsqueeze(2).to_broadcast([P, TOP_K, E]),
                                                 iota_e[:, :].unsqueeze(1).to_broadcast([P, TOP_K, E]), ALU.is_equal))
                    with nc.allow_low_precision(reason="a sum of one 1 at most"):
                        dve.tensor_reduce(chosen[:, :], hot[:, :, :].rearrange("p k e -> p e k"), AX.X, ALU.add
                                          ).then_inc(chosen_ready, 1)
                    assert chain.n == 4

                def place(j):
                    chain = Chain(dve, back_chain, BACK_STEPS * j + 6, 0)
                    dve.wait_ge(rank_done, j + 1)
                    chain.then(dve.tensor_tensor(pos[:, :], MISC[1][:, 0:E], slot_base[:, :], ALU.add))
                    chain.then(dve.tensor_tensor(slot_base[:, :], MISC[1][:, E:2 * E], slot_base[:, :], ALU.add))
                    dve.sem_inc(rank_copied, 1)
                    chain.then(dve.tensor_tensor(hot_pos[:, :, :], hot[:, :, :],
                                                 pos[:, :].unsqueeze(1).to_broadcast([P, TOP_K, E]), ALU.mult))
                    wait(dve, table_written, 16 * TOP_K * j)
                    with nc.allow_low_precision(reason="one whole number below 2 ** 24 and zeros, summed in float32"):
                        chain.then(dve.tensor_reduce(slot_i[:, :], hot_pos[:, :, :], AX.X, ALU.add))
                    chain.then(dve.tensor_copy(entry[:, :, 0], token_id[:, :].to_broadcast([P, TOP_K])))
                    chain.then(dve.tensor_scalar(token_id[:, :], token_id[:, :], float(P), None, ALU.add))
                    dve.wait_ge(topexp_ready, j + 1)
                    chain.then(dve.reciprocal(top_inv[:, :], top_s[:, :]))
                    chain.then(dve.tensor_scalar(entry[:, :, 1].bitcast(F32), top_e[:, :], top_inv[:, :], None, ALU.mult))
                    dve.sem_inc(entry_ready, 1)
                    assert chain.n == 8

                def batch(b):
                    def tile(b, s, i, back):
                        if s == 0:
                            statistics1(i, s)
                            if back:
                                copy_out_lo(i - 1, G - 1)
                            values_lo(b)
                            if back:
                                residual(i - 1, 0, SC - 1)
                                residual(i - 1, 1, SC - 1)
                                statistics2(i - 1)
                            copy_keys_lo(b)
                        maximum(i, 0)
                        maximum(i, 1)
                        if s > 0:
                            copy_out_lo(i - 1, G - 1)
                        for h in range(H):
                            normalise_probs(i, h)
                            copy_probs_lo(i, h)
                            if h + 2 < H:
                                maximum(i, h + 2)
                            if h - 1 in COPY_OUT:
                                copy_out_lo(i, COPY_OUT.index(h - 1))
                            if s > 0 and h == 4:
                                residual(i - 1, 0, s - 1)
                            if s > 0 and h == 8:
                                residual(i - 1, 1, s - 1)
                                statistics2(i - 1)
                            if h == 6 and s < SC - 1:
                                statistics1(i + 1, s + 1)
                            if h == 12 and back:
                                choose(i - 1)
                            if h == 14 and back:
                                place(i - 1)
                    tiles_of_a_batch(b, tile)

                batch(0)
                with dve.Fori(1, B) as b:
                    batch(b)
                copy_out_lo(TILES - 1, G - 1)
                residual(TILES - 1, 0, SC - 1)
                residual(TILES - 1, 1, SC - 1)
                statistics2(TILES - 1)
                choose(TILES - 1)
                place(TILES - 1)

            @block.tensor
            def _(pe):
                def transpose_queries(i, s):
                    pe.wait_ge(xq_ready, i + 1)
                    for n in range(4):
                        if n >= 2:
                            pe.wait_ge(qt_copied, 4 * i + n - 1)
                        elif s == 0:
                            wait(pe, x2_ready, 2 * (i - 1) + n + 1)
                        elif n == 0:
                            wait(pe, logits_copied, i - 1)
                        else:
                            wait(pe, rank_copied, i - 1)
                            if isinstance(i, int) and i == 1:
                                pe.wait_ge(ktlo_copied, G)
                        if n == 0 and isinstance(i, int) and i == 1:
                            pe.wait_ge(kthi_copied, G)
                        for k in range(4):
                            last = nc.tensor.transpose(MISC[n % 2][:, k * P:(k + 1) * P].bitcast(F32R),
                                                       xq[:, 4 * n + k, :, :].rearrange("p two d -> p (two d)"), ident_r[:, :])
                        last.then_inc(qt_done, 1)

                def transpose_keys(b, i):
                    pe.wait_ge(vlo_ready, b + 1)
                    pe.wait_ge(qt_copied, 4 * i + 4)
                    for g in range(G):
                        for n, v in enumerate((v_hi, v_lo)):
                            if g:
                                pe.wait_ge((kthi_copied, ktlo_copied)[n], G * b + g)
                            for c in range(TC):
                                last = nc.tensor.transpose(MISC[n][:, c * P:(c + 1) * P].bitcast(F32R), v[:, c, g, :],
                                                           ident_r[:, :])
                            last.then_inc(kt_done, 1)

                def scores(b, i, h):
                    if h == 0:
                        pe.wait_ge(qt_copied, 4 * i + 4)
                        pe.wait_ge(kthi_copied, G * b + G)
                        pe.wait_ge(ktlo_copied, G * b + G)
                    wait(pe, exp_ready, H * i + h - 1)
                    g = h // GROUP_HEADS
                    nc.tensor.matmul(S_BANK[h % 2][:, :], qT[:, h, :], kT_hi[:, g, :], start=True, stop=False)
                    nc.tensor.matmul(S_BANK[h % 2][:, :], qT[:, h, :], kT_lo[:, g, :], start=False, stop=True
                                     ).then_inc(scores_done, 1)

                def transpose_probs(i, h):
                    pe.wait_ge(probs_ready, H * i + h + 1)
                    wait(pe, ptlo_copied, H * i + h - 1)
                    for c in range(TC):
                        last = nc.tensor.transpose(PT_BANK[h % 2][:, c * P:(c + 1) * P], probs[h % 2][:, c * P:(c + 1) * P],
                                                   ident[:, :])
                    last.then_inc(pt_done, 1)

                def values(i, g):
                    pe.wait_ge(ptlo_copied, H * i + GROUP_HEADS * (g + 1))
                    wait(pe, otlo_copied, 2 * (G * i + g - 1))
                    for c in range(TC):
                        for v, p in ((v_hi, pT_hi), (v_hi, pT_lo), (v_lo, pT_hi)):
                            last = nc.tensor.matmul(O_BANK[g % 2][:, :], v[:, c, g, :],
                                                    p[g % 2][:, c, :, :].rearrange("p h t -> p (h t)"),
                                                    start=(c == 0 and v is v_hi and p is pT_hi),
                                                    stop=(c == TC - 1 and v is v_lo))
                    last.then_inc(pv_done, 1)

                def project(j, n, cs, s):
                    if cs[0] == 0:
                        if n == 0:
                            pe.wait_ge(otlo_copied, 2 * G * (j + 1))
                        if s == 0:
                            wait(pe, (logits_copied, rank_copied)[n], j)
                        else:
                            pe.wait_ge(qt_copied, 4 * (j + 1) + 3 + n)
                    for c in cs:
                        for o, w in ((oT_hi, WcT_hi), (oT_hi, WcT_lo), (oT_lo, WcT_hi)):
                            last = nc.tensor.matmul(MISC[n][:, :], o[:, c, :], w[:, c, n * HALF:(n + 1) * HALF],
                                                    start=(c == 0 and w is WcT_hi and o is oT_hi),
                                                    stop=(c == DC - 1 and o is oT_lo))
                    if cs[-1] == DC - 1:
                        last.then_inc(wo_done, 1)

                def transpose_xn2(j, b, s):
                    pe.wait_ge(xn2_ready, j + 1)
                    if s == 0:
                        pe.wait_ge(kthi_copied, G * b + G)
                        pe.wait_ge(ktlo_copied, G * b + G)
                    for n in range(2):
                        for k in range(4):
                            c = 4 * n + k
                            last = nc.tensor.transpose(MISC[n][:, k * P:(k + 1) * P], xn2[:, c * P:(c + 1) * P], ident[:, :])
                        last.then_inc(xt2_done, 1)

                def router(j):
                    pe.wait_ge(xt2_copied, 2 * j + 2)
                    for c in range(DC):
                        last = nc.tensor.matmul(MISC[0][:, 0:E], xn2T[:, c, :], gate_sb[:, c, :], start=(c == 0), stop=(c == DC - 1))
                    last.then_inc(router_done, 1)

                def ranks(j):
                    pe.wait_ge(chosen_ready, j + 1)
                    nc.tensor.matmul(MISC[1][:, 0:E], before_bf[:, :], chosen[:, :], start=True, stop=True)
                    nc.tensor.matmul(MISC[1][:, E:2 * E], ones_bf[:, :], chosen[:, :], start=True, stop=True
                                     ).then_inc(rank_done, 1)

                def batch(b):
                    def tile(b, s, i, back):
                        if s == 0:
                            if back:
                                values(i - 1, G - 1)
                                project(i - 1, 0, list(range(DC)), 0)
                                project(i - 1, 1, list(range(DC)), 0)
                            transpose_queries(i, s)
                            transpose_keys(b, i)
                        scores(b, i, 0)
                        scores(b, i, 1)
                        if s > 0:
                            values(i - 1, G - 1)
                        for h in range(H):
                            if h + 2 < H:
                                scores(b, i, h + 2)
                            transpose_probs(i, h)
                            if h % 4 == 0 and h > 0:
                                values(i, h // 4 - 1)
                            if s > 0 and h < 8:
                                project(i - 1, h // 4, [2 * (h % 4), 2 * (h % 4) + 1], s)
                            if h == 11 and back:
                                transpose_xn2(i - 1, b, s)
                            if h == 12 and back:
                                router(i - 1)
                            if h == 14 and back:
                                ranks(i - 1)
                            if h == 15 and s < SC - 1:
                                transpose_queries(i + 1, s + 1)
                    tiles_of_a_batch(b, tile)

                batch(0)
                with pe.Fori(1, B) as b:
                    batch(b)
                values(TILES - 1, G - 1)
                project(TILES - 1, 0, list(range(DC)), 0)
                project(TILES - 1, 1, list(range(DC)), 0)
                transpose_xn2(TILES - 1, B - 1, 1)
                router(TILES - 1)
                ranks(TILES - 1)


        schedule_stage(nc, sb, sem, ident, slot_base, expert_base, sched_dram, T=T, E=E, SCHED_COLS=SCHED_COLS,
                       TABLE_PAD=TABLE_PAD, top=top, experts=lambda row, used: experts_stage(
                           nc, sb, sem, banks, ident, row, used, xn_dram, table, gate_v, up_v, down_v, out,
                           T=T, D=D, DC=DC, M=M, MC=MC, E=E, TABLE_PAD=TABLE_PAD, MOST_TILES=MOST_TILES))


def setup_stage(nc, sb, sem, banks, Wc, bc, gate_w, xn_dram, table, out, ident, ident_r, before_bf, ones_bf, gate_sb,
                bias_row, iota_e, token_id, eps, slot_base, expert_base, WcT_hi, WcT_lo, *, D, DC, E, T, TABLE_ROWS):
    ROWS = TABLE_ROWS // P
    assert ROWS * P == TABLE_ROWS and T % SLOT_ROWS == 0
    mem = ExitStack()
    with mem:
        Wc_sb = sb(mem, "Wc_sb", [P, DC, D], F32)
        row_i = sb(mem, "row_i", [P, ROWS], I32)
        row_m = sb(mem, "row_m", [P, ROWS], I32)
        empty = sb(mem, "empty", [P, ROWS, 2], I32)
        zeros = sb(mem, "zeros", [P, D], F32)
        before_f = sb(mem, "before_f", [P, P], F32)
        wc_loaded, small_loaded, stored = sem("wc_loaded"), sem("small_loaded"), sem("setup_stored")
        made, ident_made, ident_r_made, empty_made = sem("made"), sem("ident_made"), sem("ident_r_made"), sem("empty_made")
        wct_done, wct_hi, wct_lo = sem("wct_done"), sem("wct_hi"), sem("wct_lo")
        block = mem.enter_context(nc.Block())
        GROUPS = [(c, n) for c in range(DC) for n in range(DC // 4)]

        @block.sync
        def _(sp):
            sp.dma_start(Wc_sb[:, :, :], Wc.rearrange("(n p) c -> p n c", p=P)).then_inc(wc_loaded, 16)
            sp.dma_start(gate_sb[:, :, :], gate_w.rearrange("(c p) e -> p c e", p=P)).then_inc(small_loaded, 16)
            sp.dma_start(bias_row[:, :], bc.unsqueeze(0).to_broadcast([P, D])).then_inc(small_loaded, 16)
            sp.wait_ge(empty_made, 2)
            sp.dma_start(table.rearrange("(p r) two -> p (r two)", p=P), empty[:, :, :].rearrange("p r two -> p (r two)")
                         ).then_inc(stored, 16)
            for rows in (xn_dram[T:T + SLOT_ROWS, :], out[T:T + SLOT_ROWS, :]):
                for q in range(SLOT_ROWS // P):
                    sp.dma_start(rows[q * P:(q + 1) * P, :], zeros[:, :]).then_inc(stored, 16)
            sp.wait_ge(small_loaded, 32)
            sp.wait_ge(stored, 16 * (1 + 2 * SLOT_ROWS // P))

        @block.gpsimd
        def _(pool):
            pool.memset(ident[:, :], 0.0).then_inc(made, 1)
            pool.memset(before_f[:, :], 1.0).then_inc(made, 1)
            pool.wait_ge(made, 2)
            pool.affine_select(out=ident[:, :], in_=ident[:, :], compare_op=ALU.not_equal, fill=1.0, base=0,
                               pattern=[[-1, P]], channel_multiplier=1).then_inc(ident_made, 1)
            pool.affine_select(out=before_f[:, :], in_=before_f[:, :], compare_op=ALU.is_gt, fill=0.0, base=0,
                               pattern=[[1, P]], channel_multiplier=-1).then_inc(made, 1)
            pool.memset(ones_bf[:, :], 1.0)
            pool.memset(eps[:, :], EPS)
            pool.iota(iota_e[:, :], [[1, E]], base=0, channel_multiplier=0, allow_small_or_imprecise_dtypes=True)
            pool.iota(token_id[:, :], [[0, 1]], base=0, channel_multiplier=1, allow_small_or_imprecise_dtypes=True)
            pool.iota(slot_base[:, :], [[T, E]], base=0, channel_multiplier=0, allow_small_or_imprecise_dtypes=True)
            pool.iota(expert_base[:, :], [[T, E]], base=0, channel_multiplier=0, allow_small_or_imprecise_dtypes=True)
            pool.iota(row_i[:, :], [[1, ROWS]], base=0, channel_multiplier=ROWS % SLOT_ROWS).then_inc(made, 1)
            pool.wait_ge(made, 4)
            pool.tensor_copy(before_bf[:, :], before_f[:, :])

        @block.vector
        def _(dve):
            dve.memset(zeros[:, :], 0.0).then_inc(empty_made, 1)
            dve.memset(empty[:, :, 1], 0)
            dve.wait_ge(ident_made, 1)
            dve.tensor_copy(ident_r[:, :], ident[:, :]).then_inc(ident_r_made, 1)
            dve.wait_ge(made, 4)
            dve.tensor_single_scalar(row_m[:, :], row_i[:, :], SLOT_ROWS - 1, ALU.bitwise_and).then_inc(ident_r_made, 1)
            dve.wait_ge(ident_r_made, 2)
            dve.tensor_scalar(empty[:, :, 0], row_m[:, :], float(T), None, ALU.add).then_inc(empty_made, 1)
            for k, (c, n) in enumerate(GROUPS):
                dve.wait_ge(wct_hi, k + 1)
                dve.tensor_tensor(WcT_lo[:, c, n * 512:(n + 1) * 512], banks[k % 2][:, :],
                                  WcT_hi[:, c, n * 512:(n + 1) * 512].bitcast(F32), ALU.subtract).then_inc(wct_lo, 1)

        @block.scalar
        def _(act):
            for k, (c, n) in enumerate(GROUPS):
                act.wait_ge(wct_done, k + 1)
                act.activation(WcT_hi[:, c, n * 512:(n + 1) * 512], banks[k % 2][:, :], ACT.Copy).then_inc(wct_hi, 1)

        @block.tensor
        def _(pe):
            pe.wait_ge(ident_made, 1)
            pe.wait_ge(wc_loaded, 16)
            for k, (c, n) in enumerate(GROUPS):
                if k >= 2:
                    pe.wait_ge(wct_lo, k - 1)
                for m in range(4):
                    last = nc.tensor.transpose(banks[k % 2][:, m * P:(m + 1) * P], Wc_sb[:, 4 * n + m, c * P:(c + 1) * P],
                                               ident[:, :])
                last.then_inc(wct_done, 1)


def schedule_stage(nc, sb, sem, ident, slot_base, expert_base, sched_dram, *, T, E, SCHED_COLS, TABLE_PAD, top, experts):
    SIZES = T // SLOT_ROWS
    SCHED = SCHED_COLS * P
    row = sb(top, "sched_row", [1, SCHED * 4], I32)
    used = sb(top, "tiles_used", [P, 1], I32)
    mem = ExitStack()
    with mem:
        steps = sb(mem, "steps", [P, SIZES], F32)
        upto = sb(mem, "upto", [P, E, E], F32)
        tile_no = sb(mem, "tile_no", [P, 2, SCHED_COLS], F32)
        count = sb(mem, "count", [P, E], F32)
        more = sb(mem, "more", [P, E, SIZES], F32)
        tiles = sb(mem, "tiles", [P, E], F32)
        part = sb(mem, "part", [P, E, E], F32)
        ends = sb(mem, "ends", [P, E], F32)
        passed = sb(mem, "passed", [P, 2 * SCHED_COLS, E], F32)
        expert = sb(mem, "expert", [P, 2, SCHED_COLS], F32)
        taken = sb(mem, "taken", [P, SCHED_COLS, E], F32)
        first = sb(mem, "first", [P, SCHED_COLS], F32)
        offset = sb(mem, "offset", [P, SCHED_COLS], F32)
        offset2 = sb(mem, "offset2", [P, SCHED_COLS], F32)
        clamped = sb(mem, "clamped", [P, 2, SCHED_COLS], F32)
        sched = sb(mem, "sched", [P, SCHED_COLS, 4], I32)
        consts, chain_sem, ready, stored = sem("sched_consts"), sem("sched_chain"), sem("sched_ready"), sem("sched_stored")
        block = mem.enter_context(nc.Block())

        @block.gpsimd
        def _(pool):
            pool.iota(steps[:, :], [[SLOT_ROWS, SIZES]], base=0, channel_multiplier=0,
                      allow_small_or_imprecise_dtypes=True).then_inc(consts, 1)
            pool.iota(tile_no[:, :, :], [[-1, 2], [P, SCHED_COLS]], base=0, channel_multiplier=1,
                      allow_small_or_imprecise_dtypes=True).then_inc(consts, 1)
            pool.memset(upto[:, :, :], 1.0).then_inc(consts, 1)
            pool.wait_ge(consts, 3)
            pool.affine_select(out=upto[:, :, :], in_=upto[:, :, :], compare_op=ALU.is_ge, fill=0.0, base=0,
                               pattern=[[1, E], [-1, E]], channel_multiplier=0).then_inc(consts, 1)

        @block.vector
        def _(dve):
            chain = Chain(dve, chain_sem, 0, 0)
            do = chain.then
            do(dve.memset(sched[:, :, 3], 0))
            do(dve.tensor_tensor(count[:, :], slot_base[:, :], expert_base[:, :], ALU.subtract))
            dve.wait_ge(consts, 4)
            do(dve.tensor_tensor(more[:, :, :], count[:, :].unsqueeze(2).to_broadcast([P, E, SIZES]),
                                 steps[:, :].unsqueeze(1).to_broadcast([P, E, SIZES]), ALU.is_gt))
            do(dve.tensor_reduce(tiles[:, :], more[:, :, :], AX.X, ALU.add))
            do(dve.tensor_tensor(part[:, :, :], upto[:, :, :], tiles[:, :].unsqueeze(1).to_broadcast([P, E, E]), ALU.mult))
            do(dve.tensor_reduce(ends[:, :], part[:, :, :], AX.X, ALU.add))
            do(dve.tensor_copy(used[:, :], ends[:, E - 1:E]))
            do(dve.tensor_tensor(passed[:, :, :],
                                 tile_no[:, :, :].rearrange("p a c -> p (a c)").unsqueeze(2).to_broadcast([P, 2 * SCHED_COLS, E]),
                                 ends[:, :].unsqueeze(1).to_broadcast([P, 2 * SCHED_COLS, E]), ALU.is_ge))
            do(dve.tensor_reduce(expert[:, :, :].rearrange("p a c -> p (a c)"), passed[:, :, :], AX.X, ALU.add))
            do(dve.tensor_tensor(taken[:, :, :], passed[:, 0:SCHED_COLS, :],
                                 tiles[:, :].unsqueeze(1).to_broadcast([P, SCHED_COLS, E]), ALU.mult))
            do(dve.tensor_reduce(first[:, :], taken[:, :, :], AX.X, ALU.add))
            do(dve.tensor_tensor(offset[:, :], tile_no[:, 0, :], first[:, :], ALU.subtract))
            do(dve.tensor_scalar(offset2[:, :], offset[:, :], float(SLOT_ROWS), None, ALU.mult))
            do(dve.scalar_tensor_tensor(out=offset[:, :], in0=expert[:, 0, :], scalar=float(T), in1=offset2[:, :],
                                        op0=ALU.mult, op1=ALU.add))
            do(dve.tensor_scalar(sched[:, :, 0], offset[:, :], float(TABLE_PAD), None, ALU.min))
            do(dve.tensor_scalar(clamped[:, :, :], expert[:, :, :], float(E - 1), None, ALU.min))
            do(dve.tensor_copy(sched[:, :, 1], clamped[:, 0, :]))
            do(dve.tensor_tensor(sched[:, :, 2], clamped[:, 0, :], clamped[:, 1, :], ALU.not_equal))
            dve.sem_inc(ready, 1)

        @block.sync
        def _(sp):
            sp.wait_ge(ready, 1)
            sp.dma_start(sched_dram.rearrange("(c p) k -> p c k", p=P), sched[:, :, :]).then_inc(stored, 16)
            sp.wait_ge(stored, 16)
            sp.dma_start(row[:, :], sched_dram.rearrange("t k -> (t k)").unsqueeze(0)).then_inc(stored, 16)
            sp.wait_ge(stored, 32)

    experts(row, used)


def experts_stage(nc, sb, sem, banks, ident, sched_row, tiles_used, xn_dram, table, gate_v, up_v, down_v, out, *,
                  T, D, DC, M, MC, E, TABLE_PAD, MOST_TILES):
    Q = SLOT_ROWS // P
    NH = D // 512
    OUT_GROUPS = Q * NH
    mem = ExitStack()
    with mem:
        gu_raw = sb(mem, "gu_raw", [P, 2, DC, M], F32)
        d_raw = sb(mem, "d_raw", [P, MC, D], F32)
        gu_hi = sb(mem, "gu_hi", [P, DC, 2, M], F32R)
        gu_lo = sb(mem, "gu_lo", [P, DC, 2, M], F32R)
        d_hi = sb(mem, "d_hi", [P, MC, D], F32R)
        d_lo = sb(mem, "d_lo", [P, MC, D], F32R)
        xg = sb(mem, "xg", [P, Q, D], F32)
        xT_hi = sb(mem, "xT_hi", [P, DC, SLOT_ROWS], F32R)
        xT_lo = sb(mem, "xT_lo", [P, DC, SLOT_ROWS], F32R)
        gated = [sb(mem, f"gated{n}", [P, SLOT_ROWS], F32) for n in range(2)]
        h = sb(mem, "h", [P, SLOT_ROWS], F32)
        h_hi = sb(mem, "h_hi", [P, MC, SLOT_ROWS], F32R)
        h_lo = sb(mem, "h_lo", [P, MC, SLOT_ROWS], F32R)
        rows_out = sb(mem, "rows_out", [P, Q, D], F32)
        entry_in = sb(mem, "entry_in", [P, Q, 2], I32)
        entry_now = sb(mem, "entry_now", [P, Q, 2], I32)
        G_BANK, U_BANK, X_BANK, D_BANK = (banks[0], banks[2]), (banks[1], banks[3]), banks[4:6], banks[6:8]

        gu_loaded, d_loaded, entry_loaded = sem("gu_loaded"), sem("d_loaded"), sem("entry_loaded")
        gathered, scattered = sem("gathered"), sem("scattered")
        entry_taken = sem("entry_taken")
        xt_done, xt_hi, xt_lo = sem("xt_done"), sem("xt_hi"), sem("xt_lo")
        guhi_ready, gulo_ready, dhi_ready, dlo_ready = sem("guhi_ready"), sem("gulo_ready"), sem("dhi_ready"), sem("dlo_ready")
        gu_done, silu_ready, h_ready, hhi_ready, hlo_ready = sem("gu_done"), sem("silu_ready"), sem("h_ready"), sem("hhi_ready"), sem("hlo_ready")
        down_done, rows_ready = sem("down_done"), sem("rows_ready")
        fence = {n: sem(f"fence2_{n}") for n in ("pool", "sp")}

        def all_tiles(eng, tile):
            used = eng.value_load(tiles_used[0:1, 0:1], min_val=1, max_val=MOST_TILES)
            tile(0)
            with eng.Fori(1, MOST_TILES) as t:
                with eng.If(t < used):
                    tile(t)

        block = mem.enter_context(nc.Block())

        @block.sync
        def _(sp):
            def load(t):
                first_row = sp.value_load(sched_row[0:1, bass.ds(4 * t, 1)], min_val=0, max_val=TABLE_PAD)
                e = sp.value_load(sched_row[0:1, bass.ds(4 * t + 1, 1)], min_val=0, max_val=E - 1)
                new = None if isinstance(t, int) and t == 0 else sp.value_load(
                    sched_row[0:1, bass.ds(4 * t + 2, 1)], min_val=0, max_val=1)
                only = {} if new is None else {"cond": new}
                wait(sp, entry_taken, t)
                sp.dma_start(entry_in[:, :, :], table[bass.ds(first_row, SLOT_ROWS), :].rearrange("(p q) k -> p q k", q=Q)
                             ).then_inc(entry_loaded, 16)
                wait(sp, gulo_ready, DC * t)
                for n, w in enumerate((gate_v, up_v)):
                    sp.dma_start(gu_raw[:, n, :, :], w[bass.ds(e, 1), :, :, :].rearrange("e p c m -> p (e c) m"), **only
                                 ).then_inc(gu_loaded, 16)
                wait(sp, dlo_ready, MC * t)
                sp.dma_start(d_raw[:, :, :], down_v[bass.ds(e, 1), :, :, :].rearrange("e p c d -> p (e c) d"), **only
                             ).then_inc(d_loaded, 16)

            def tile(t):
                load(t + 1)
                sp.wait_ge(d_loaded, 16 * (t + 2))
                sp.sem_inc(fence["sp"], 1)

            load(0)
            all_tiles(sp, tile)

        @block.gpsimd
        def _(pool):
            def hold(semaphore, value):
                if isinstance(value, int) and value <= 0:
                    return
                pool.wait_ge(semaphore, value)
                pool.sem_inc(fence["pool"], 1)

            def gather(t):
                hold(entry_loaded, 16 * (t + 1))
                hold(xt_done, DC * t)
                for q in range(Q):
                    pool.indirect_dma_start(
                        out=xg[:, q, :], out_offset=None, in_=xn_dram,
                        in_offset=bass.IndirectOffsetOnAxis(ap=entry_in[:, q, 0:1], axis=0),
                        bounds_check=T + SLOT_ROWS - 1, oob_is_err=True).then_inc(gathered, 16)

            def tile(t):
                hold(gathered, 16 * Q * (t + 1))
                pool.tensor_copy(entry_now[:, :, :], entry_in[:, :, :]).then_inc(entry_taken, 1)
                gather(t + 1)
                for q in range(Q):
                    hold(rows_ready, OUT_GROUPS * t + NH * (q + 1))
                    pool.indirect_dma_start(
                        out=out, out_offset=bass.IndirectOffsetOnAxis(ap=entry_now[:, q, 0:1], axis=0),
                        in_=rows_out[:, q, :], in_offset=None, bounds_check=T + SLOT_ROWS - 1, oob_is_err=True,
                        compute_op=ALU.add).then_inc(scattered, 16)
                hold(scattered, 16 * Q * (t + 1))

            gather(0)
            all_tiles(pool, tile)

        @block.scalar
        def _(act):
            def x_hi(t, c):
                act.wait_ge(xt_done, DC * t + c + 1)
                act.activation(xT_hi[:, c, :], X_BANK[c % 2][:, :], ACT.Copy).then_inc(xt_hi, 1)

            def gate_up_hi(t, c):
                act.wait_ge(gu_loaded, 32 * (t + 1))
                act.activation(gu_hi[:, c, :, :], gu_raw[:, :, c, :], ACT.Copy).then_inc(guhi_ready, 1)

            def down_hi(t, k):
                act.wait_ge(d_loaded, 16 * (t + 1))
                wait(act, down_done, OUT_GROUPS * t)
                act.activation(d_hi[:, k, :], d_raw[:, k, :], ACT.Copy).then_inc(dhi_ready, 1)

            def silu(t, j):
                act.wait_ge(gu_done, MC * t + j + 1)
                wait(act, h_ready, MC * t + j - 1)
                act.activation(gated[j % 2][:, :],
                               G_BANK[j % 2][:, :], ACT.Silu).then_inc(silu_ready, 1)

            def weighted_rows(t, g):
                q, n = divmod(g, NH)
                act.wait_ge(down_done, OUT_GROUPS * t + g + 1)
                if g == 0:
                    act.wait_ge(entry_taken, t + 1)
                    wait(act, scattered, 16 * Q * t)
                act.activation(rows_out[:, q, n * 512:(n + 1) * 512], D_BANK[g % 2][:, :], ACT.Copy,
                               scale=entry_now[:, q, 1:2].bitcast(F32)).then_inc(rows_ready, 1)

            def tile(t):
                for k in range(MC):
                    down_hi(t, k)
                    silu(t, k)
                for c in range(DC):
                    x_hi(t + 1, c)
                    gate_up_hi(t + 1, c)
                    if c == 1:
                        weighted_rows(t, 0)
                    if c >= 1:
                        weighted_rows(t, c)

            for c in range(DC):
                x_hi(0, c)
                gate_up_hi(0, c)
            all_tiles(act, tile)

        @block.vector
        def _(dve):
            def x_lo(t, c):
                dve.wait_ge(xt_hi, DC * t + c + 1)
                dve.tensor_tensor(xT_lo[:, c, :], X_BANK[c % 2][:, :], xT_hi[:, c, :].bitcast(F32), ALU.subtract
                                  ).then_inc(xt_lo, 1)

            def gate_up_lo(t, c):
                dve.wait_ge(guhi_ready, DC * t + c + 1)
                dve.tensor_tensor(gu_lo[:, c, :, :], gu_raw[:, :, c, :], gu_hi[:, c, :, :].bitcast(F32), ALU.subtract
                                  ).then_inc(gulo_ready, 1)

            def down_lo(t, k):
                dve.wait_ge(dhi_ready, MC * t + k + 1)
                dve.tensor_tensor(d_lo[:, k, :], d_raw[:, k, :], d_hi[:, k, :].bitcast(F32), ALU.subtract
                                  ).then_inc(dlo_ready, 1)

            def hidden(t, j):
                dve.wait_ge(silu_ready, MC * t + j + 1)
                wait(dve, hlo_ready, MC * t + j)
                dve.tensor_tensor(h[:, :], U_BANK[j % 2][:, :], gated[j % 2][:, :], ALU.mult).then_inc(h_ready, 1)
                dve.wait_ge(h_ready, MC * t + j + 1)
                wait(dve, down_done, OUT_GROUPS * t)
                dve.tensor_copy(h_hi[:, j, :], h[:, :]).then_inc(hhi_ready, 1)
                dve.wait_ge(hhi_ready, MC * t + j + 1)
                dve.tensor_tensor(h_lo[:, j, :], h[:, :], h_hi[:, j, :].bitcast(F32), ALU.subtract).then_inc(hlo_ready, 1)

            def tile(t):
                for k in range(MC):
                    down_lo(t, k)
                    hidden(t, k)
                for c in range(DC):
                    x_lo(t + 1, c)
                    gate_up_lo(t + 1, c)

            for c in range(DC):
                x_lo(0, c)
                gate_up_lo(0, c)
            all_tiles(dve, tile)

        @block.tensor
        def _(pe):
            def transpose_rows(t, c):
                if c == 0:
                    pe.wait_ge(gathered, 16 * Q * (t + 1))
                wait(pe, xt_lo, DC * t + c - 1)
                for q in range(Q):
                    last = nc.tensor.transpose(X_BANK[c % 2][:, q * P:(q + 1) * P], xg[:, q, c * P:(c + 1) * P], ident[:, :])
                last.then_inc(xt_done, 1)

            def gate_up(t, j):
                if j == 0:
                    pe.wait_ge(xt_lo, DC * (t + 1))
                    pe.wait_ge(gulo_ready, DC * (t + 1))
                wait(pe, h_ready, MC * t + (0, -1, 1)[j])
                for n, bank in enumerate((G_BANK[j % 2], U_BANK[j % 2])):
                    for c in range(DC):
                        for w, v in ((gu_hi, xT_hi), (gu_hi, xT_lo), (gu_lo, xT_hi)):
                            last = nc.tensor.matmul(bank[:, :], w[:, c, n, j * P:(j + 1) * P], v[:, c, :],
                                                    start=(c == 0 and w is gu_hi and v is xT_hi),
                                                    stop=(c == DC - 1 and w is gu_lo))
                last.then_inc(gu_done, 1)

            def down(t, g, ks):
                q, n = divmod(g, NH)
                if ks[0] == 0:
                    wait(pe, rows_ready, OUT_GROUPS * t + g - 1)
                for k in ks:
                    if g == 0 or k == MC - 1:
                        pe.wait_ge(hlo_ready, MC * t + k + 1)
                    if g == 0:
                        pe.wait_ge(dlo_ready, MC * t + k + 1)
                    for v, w in ((h_hi, d_hi), (h_hi, d_lo), (h_lo, d_hi)):
                        last = nc.tensor.matmul(D_BANK[g % 2][:, :], v[:, k, q * P:(q + 1) * P],
                                                w[:, k, n * 512:(n + 1) * 512],
                                                start=(k == 0 and v is h_hi and w is d_hi),
                                                stop=(k == MC - 1 and v is h_lo))
                if ks[-1] == MC - 1:
                    last.then_inc(down_done, 1)

            def tile(t):
                for j in range(MC):
                    gate_up(t, j)
                early, late = list(range(MC - 1)), [MC - 1]
                transpose_rows(t + 1, 0)
                down(t, 0, early)
                transpose_rows(t + 1, 1)
                down(t, 1, early)
                down(t, 0, late)
                down(t, 1, late)
                for c in range(2, DC):
                    transpose_rows(t + 1, c)
                    down(t, c, early + late)

            for c in range(DC):
                transpose_rows(0, c)
            all_tiles(pe, tile)


_INS = ["x", "ctx_512", "L0_xattn_Wc", "L0_xattn_bc", "L0_ffn_gate_kernel", "L0_ffn_gate_proj", "L0_ffn_up_proj",
        "L0_ffn_down_proj"]


def kernel(**inputs):
    import numpy as _np
    import concourse.bacc as _bacc
    from concourse import mybir as _mybir
    from concourse.bass_utils import run_bass_kernel_spmd as _run

    nc = _bacc.Bacc("TRN2", target_bir_lowering=False, num_devices=1)
    arrays, args = {}, []
    for name in _INS:
        a = _np.ascontiguousarray(inputs[name])
        arrays[f"in_{name}"] = a
        args.append(nc.dram_tensor(f"in_{name}", a.shape, _mybir.dt.from_np(a.dtype), kind="ExternalInput").ap())
    B, S, D = inputs["x"].shape
    out = nc.dram_tensor("out_rows", (B * S + SLOT_ROWS, D), F32, kind="ExternalOutput").ap()
    moe_block(nc, *args, out)
    r = _run(nc, [arrays], core_ids=[0])
    return r.results[0]["out_rows"][:B * S].reshape(B, S, D)
```

```python
import concourse.bass as bass
from concourse import mybir
from contextlib import ExitStack

F32 = mybir.dt.float32
F32R = mybir.dt.float32r
BF16 = mybir.dt.bfloat16
I32 = mybir.dt.int32
U32 = mybir.dt.uint32
ALU = mybir.AluOpType
ACT = mybir.ActivationFunctionType
AX = mybir.AxisListType
P = 128
EPS = 1e-5
TOP_K = 8
HEAD_DIM = 64
GROUP_HEADS = 4
SLOT_ROWS = 512
DMA_RING = 8192


def wait(eng, sem, value):
    if isinstance(value, int) and value <= 0:
        return
    eng.wait_ge(sem, value)


class Chain:

    def __init__(self, eng, sem, before, each):
        self.eng, self.sem, self.before, self.each, self.n = eng, sem, before, each, 0

    def then(self, instruction):
        instruction.then_inc(self.sem, 1)
        self.n += 1
        self.eng.wait_ge(self.sem, self.before + self.n)

    def done(self):
        assert self.n == self.each, (self.n, self.each)


def moe_block(nc, x, ctx_in, Wc, bc, gate_w, gate_proj, up_proj, down_proj, out):
    B, S, D = x.shape
    CD = ctx_in.shape[2]
    E, _, M = gate_proj.shape
    T = B * S
    DC = D // P
    MC = M // P
    TC = ctx_in.shape[1] // P
    SC = S // P
    H = D // HEAD_DIM
    G = H // GROUP_HEADS
    HALF = 512
    NH = D // HALF
    TILES = T // P
    PAD_ROW = T
    TABLE_PAD = E * T
    TABLE_ROWS = TABLE_PAD + SLOT_ROWS
    QUARTERS = SLOT_ROWS // P
    MOST_TILES = (T * TOP_K + E * (SLOT_ROWS - 1)) // SLOT_ROWS
    SCHED_COLS = (MOST_TILES + 2 + P - 1) // P
    SCHED = SCHED_COLS * P
    assert CD == G * HEAD_DIM and TC * P == 512 and S == 512 and QUARTERS == 4

    x_rows = x.rearrange("b s d -> (b s) d")
    ctx_v = ctx_in.rearrange("b (c p) d -> p b c d", p=P)
    down_v = down_proj.rearrange("e (c p) d -> e p c d", p=P)

    xn_dram = nc.dram_tensor("xn_rows", (T + SLOT_ROWS, D), F32, kind="Internal").ap()
    table = nc.dram_tensor("slot_table", (TABLE_ROWS, 2), I32, kind="Internal").ap()
    sched_dram = nc.dram_tensor("tile_schedule", (SCHED, 4), I32, kind="Internal").ap()

    top = ExitStack()
    with top:
        def sb(ctx, name, shape, dt):
            return ctx.enter_context(nc.sbuf_tensor(name, shape, dt))

        def sem(name):
            return top.enter_context(nc.semaphore(name))

        banks = [top.enter_context(nc.psum_tensor(f"bank{n}", [P, 512], F32)) for n in range(8)]

        ident = sb(top, "ident", [P, P], F32)
        slot_base = sb(top, "slot_base", [P, E], F32)
        expert_base = sb(top, "expert_base", [P, E], F32)

        attention_mem = ExitStack()
        with attention_mem:
            WcT_hi = sb(attention_mem, "WcT_hi", [P, DC, D], F32R)
            WcT_lo = sb(attention_mem, "WcT_lo", [P, DC, D], F32R)
            ident_r = sb(attention_mem, "ident_r", [P, P], F32R)
            before_bf = sb(attention_mem, "before_bf", [P, P], BF16)
            ones_bf = sb(attention_mem, "ones_bf", [P, P], BF16)
            gate_sb = sb(attention_mem, "gate_sb", [P, DC, E], F32)
            bias_row = sb(attention_mem, "bias_row", [P, D], F32)
            iota_e = sb(attention_mem, "iota_e", [P, E], F32)
            token_id = sb(attention_mem, "token_id", [P, 1], F32)
            eps = sb(attention_mem, "eps", [P, 1], F32)

            setup_stage(nc, sb, sem, banks, Wc, bc, gate_w, xn_dram, table, out, ident, ident_r, before_bf,
                        ones_bf, gate_sb, bias_row, iota_e, token_id, eps, slot_base, expert_base, WcT_hi, WcT_lo,
                        D=D, DC=DC, E=E, T=T, TABLE_ROWS=TABLE_ROWS)

            x_t = [sb(attention_mem, f"x_t{n}", [P, D], F32) for n in range(SC)]
            xn = sb(attention_mem, "xn", [P, D], F32)
            xq = sb(attention_mem, "xq", [P, H, 2, HEAD_DIM], F32R)
            qT = [sb(attention_mem, f"qT{n}", [P, H, P], F32R) for n in range(2)]
            ctx_sb = sb(attention_mem, "ctx_sb", [P, TC, CD], F32)
            v_hi = sb(attention_mem, "v_hi", [P, TC, G, P], F32R)
            v_lo = sb(attention_mem, "v_lo", [P, TC, G, P], F32R)
            kT_hi = sb(attention_mem, "kT_hi", [P, G, 512], F32R)
            kT_lo = sb(attention_mem, "kT_lo", [P, G, 512], F32R)
            probs = [sb(attention_mem, f"probs{n}", [P, 512], F32) for n in range(4)]
            pT_hi = [sb(attention_mem, f"pT_hi{n}", [P, TC, GROUP_HEADS, P], F32R) for n in range(2)]
            pT_lo = [sb(attention_mem, f"pT_lo{n}", [P, TC, GROUP_HEADS, P], F32R) for n in range(2)]
            oT_hi = sb(attention_mem, "oT_hi", [P, DC, P], F32R)
            oT_lo = sb(attention_mem, "oT_lo", [P, DC, P], F32R)
            x2 = sb(attention_mem, "x2", [P, D], F32)
            xn2 = sb(attention_mem, "xn2", [P, D], F32)
            xn2T = sb(attention_mem, "xn2T", [P, DC, P], F32)
            neg_max = sb(attention_mem, "neg_max", [P, H], F32)
            row_sum = sb(attention_mem, "row_sum", [P, H], F32)
            row_inv = sb(attention_mem, "row_inv", [P, H], F32)
            bn1 = sb(attention_mem, "bn1", [P, 2, 6], F32)
            mv1 = sb(attention_mem, "mv1", [P, 2], F32)
            ln1 = sb(attention_mem, "ln1", [P, 8], F32)
            bn2 = sb(attention_mem, "bn2", [P, 2, 6], F32)
            mv2 = sb(attention_mem, "mv2", [P, 2], F32)
            ln2 = sb(attention_mem, "ln2", [P, 8], F32)
            LOG, SEED, VAR, SQ, ERR, FIX, SCALE, SHIFT = range(8)
            FACTOR_STEPS = 5
            logits = sb(attention_mem, "logits", [P, E], F32)
            top_v = sb(attention_mem, "top_v", [P, TOP_K], F32)
            top_i = sb(attention_mem, "top_i", [P, TOP_K], U32)
            top_f = sb(attention_mem, "top_f", [P, TOP_K], F32)
            neg_top = sb(attention_mem, "neg_top", [P, 1], F32)
            top_e = sb(attention_mem, "top_e", [P, TOP_K], F32)
            top_s = sb(attention_mem, "top_s", [P, 1], F32)
            top_inv = sb(attention_mem, "top_inv", [P, 1], F32)
            hot = sb(attention_mem, "hot", [P, TOP_K, E], F32)
            hot_pos = sb(attention_mem, "hot_pos", [P, TOP_K, E], F32)
            chosen = sb(attention_mem, "chosen", [P, E], BF16)
            pos = sb(attention_mem, "pos", [P, E], F32)
            slot_i = sb(attention_mem, "slot_i", [P, TOP_K], I32)
            entry = sb(attention_mem, "entry", [P, TOP_K, 2], I32)

            S_BANK, PT_BANK, O_BANK, MISC = banks[0:2], banks[2:4], banks[4:6], banks[6:8]

            x_in = [sem(f"x_in{s}") for s in range(SC)]
            ctx_loaded = sem("ctx_loaded")
            x2_stored = sem("x2_stored")
            xn2_stored = sem("xn2_stored")
            table_written = sem("table_written")
            ln1_chain, stats1, pool1_chain, ln1_ready = sem("ln1_chain"), sem("stats1"), sem("pool1_chain"), sem("ln1_ready")
            log1_ready, seed1_ready, log2_ready, seed2_ready = sem("log1_ready"), sem("seed1_ready"), sem("log2_ready"), sem("seed2_ready")
            xn_ready, xq_hi_ready, xq_ready, xbias_ready = sem("xn_ready"), sem("xq_hi_ready"), sem("xq_ready"), sem("xbias_ready")
            qt_done, qt_copied = sem("qt_done"), sem("qt_copied")
            vhi_ready, vlo_ready, kt_done = sem("vhi_ready"), sem("vlo_ready"), sem("kt_done")
            kthi_copied, ktlo_copied = sem("kthi_copied"), sem("ktlo_copied")
            scores_done, max_ready, exp_ready, probs_ready = sem("scores_done"), sem("max_ready"), sem("exp_ready"), sem("probs_ready")
            inverse_ready = sem("inverse_ready")
            pt_done, pthi_copied, ptlo_copied = sem("pt_done"), sem("pthi_copied"), sem("ptlo_copied")
            pv_done, othi_copied, otlo_copied = sem("pv_done"), sem("othi_copied"), sem("otlo_copied")
            wo_done, x2_ready, back_chain, stats2 = sem("wo_done"), sem("x2_ready"), sem("back_chain"), sem("stats2")
            pool2_chain, ln2_ready, xn2_ready = sem("pool2_chain"), sem("ln2_ready"), sem("xn2_ready")
            xt2_done, xt2_copied, router_done, logits_copied = sem("xt2_done"), sem("xt2_copied"), sem("router_done"), sem("logits_copied")
            top_ready, topexp_ready, chosen_ready, rank_done = sem("top_ready"), sem("topexp_ready"), sem("chosen_ready"), sem("rank_done")
            rank_copied, entry_ready = sem("rank_copied"), sem("entry_ready")
            fence = {n: sem(f"fence_{n}") for n in ("dve", "pool")}

            BACK_STEPS = 14
            AHEAD = 3
            PROJECT = {1: ((0, 0, 2),), 2: ((0, 2, 4),), 3: ((0, 4, 6),), 4: ((1, 0, 2),), 5: ((0, 6, 8),),
                       6: ((1, 2, 5),), 7: ((1, 5, 8),)}
            NEXT_STATS, NEXT_NORM, NEXT_QUERIES = 2, 3, (9, 10)
            RESIDUAL, NORM2, TRANSPOSE2, ROUTER, CHOOSE, PLACE = (6, 8), 10, 11, 12, 13, 15

            def tiles_of_a_batch(b, body):
                for s in range(SC):
                    body(b, s, b * SC + s, not (isinstance(b, int) and b == 0 and s == 0))

            block = attention_mem.enter_context(nc.Block())

            @block.sync
            def _(sp):
                def store(j):
                    sp.wait_ge(x2_ready, 2 * j + 2)
                    sp.dma_start(out[bass.ds(j * P, P), :], x2[:, :]).then_inc(x2_stored, 16)
                    sp.wait_ge(xn2_ready, j + 1)
                    sp.dma_start(xn_dram[bass.ds(j * P, P), :], xn2[:, :]).then_inc(xn2_stored, 16)

                def batch(b):
                    wait(sp, vhi_ready, b)
                    wait(sp, vlo_ready, b)
                    sp.dma_start(ctx_sb[:, :, :], ctx_v[:, bass.ds(b, 1), :, :].rearrange("p b c d -> p (b c) d")
                                 ).then_inc(ctx_loaded, 16)

                    def tile(b, s, i, _):
                        wait(sp, x2_ready, 2 * (i - SC) + 2)
                        sp.dma_start(x_t[s][:, :], x_rows[bass.ds(i * P, P), :]).then_inc(x_in[s], 16)
                        if not (isinstance(b, int) and b == 0 and s < 2):
                            store(i - 2)
                    tiles_of_a_batch(b, tile)

                batch(0)
                with sp.Fori(1, B) as b:
                    batch(b)
                store(TILES - 2)
                store(TILES - 1)
                sp.wait_ge(x2_stored, 16 * TILES)
                sp.wait_ge(xn2_stored, 16 * TILES)

            @block.gpsimd
            def _(pool):
                def hold(semaphore, value):
                    if isinstance(value, int) and value <= 0:
                        return
                    pool.wait_ge(semaphore, value)
                    pool.sem_inc(fence["pool"], 1)

                def factors(f, mv, scale, chain, before, signal):
                    pool.tensor_scalar(f[:, VAR:VAR + 1], mv[:, 1:2], EPS, None, ALU.add).then_inc(chain, 1)
                    pool.tensor_tensor(f[:, SQ:SQ + 1], f[:, SEED:SEED + 1], f[:, SEED:SEED + 1], ALU.mult).then_inc(chain, 1)
                    hold(chain, before + 2)
                    pool.tensor_tensor(f[:, ERR:ERR + 1], f[:, SQ:SQ + 1], f[:, VAR:VAR + 1], ALU.mult).then_inc(chain, 1)
                    hold(chain, before + 3)
                    pool.tensor_scalar(f[:, FIX:FIX + 1], f[:, ERR:ERR + 1], -0.5, 1.5, ALU.mult, ALU.add).then_inc(chain, 1)
                    hold(chain, before + 4)
                    pool.tensor_scalar(f[:, SCALE:SCALE + 1], f[:, FIX:FIX + 1], f[:, SEED:SEED + 1], scale,
                                       ALU.mult, ALU.mult).then_inc(chain, 1)
                    hold(chain, before + FACTOR_STEPS)
                    pool.tensor_scalar(f[:, SHIFT:SHIFT + 1], mv[:, 0:1], f[:, SCALE:SCALE + 1], -1.0, ALU.mult, ALU.mult
                                       ).then_inc(signal, 1)

                def factors1(i):
                    hold(seed1_ready, i + 1)
                    hold(xn_ready, i)
                    factors(ln1, mv1, HEAD_DIM ** -0.5, pool1_chain, FACTOR_STEPS * i, ln1_ready)

                def queries(i, s):
                    hold(xn_ready, i + 1)
                    hold(qt_done, 4 * i)
                    heads = xn[:, :].rearrange("p (h d) -> p h d", d=HEAD_DIM)
                    pool.tensor_copy(xq[:, :, 0, :], heads).then_inc(xq_hi_ready, 1)
                    hold(xq_hi_ready, i + 1)
                    pool.tensor_tensor(xq[:, :, 1, :], heads, xq[:, :, 0, :].bitcast(F32), ALU.subtract).then_inc(xq_ready, 1)
                    pool.tensor_tensor(x_t[s][:, :], x_t[s][:, :], bias_row[:, :], ALU.add).then_inc(xbias_ready, 1)

                def factors2(j):
                    hold(seed2_ready, j + 1)
                    hold(xn2_ready, j)
                    factors(ln2, mv2, 1.0, pool2_chain, FACTOR_STEPS * j, ln2_ready)

                def scatter(j):
                    hold(entry_ready, j + 1)
                    for k in range(TOP_K):
                        pool.indirect_dma_start(
                            out=table, out_offset=bass.IndirectOffsetOnAxis(ap=slot_i[:, k:k + 1], axis=0),
                            in_=entry[:, k, :], in_offset=None, bounds_check=TABLE_ROWS - 1, oob_is_err=True,
                        ).then_inc(table_written, 16)

                def batch(b):
                    def tile(b, s, i, back):
                        if s == 0:
                            factors1(i)
                            queries(i, s)
                        if s < SC - 1:
                            factors1(i + 1)
                            queries(i + 1, s + 1)
                        if back:
                            factors2(i - 1)
                            scatter(i - 1)
                    tiles_of_a_batch(b, tile)

                batch(0)
                with pool.Fori(1, B) as b:
                    batch(b)
                factors2(TILES - 1)
                scatter(TILES - 1)
                pool.wait_ge(table_written, 16 * TOP_K * TILES)

            @block.scalar
            def _(act):
                def seed(i, f, mv, stats, log_ready, ready, taken):
                    act.wait_ge(stats, i + 1)
                    wait(act, taken, i)
                    act.activation(f[:, LOG:LOG + 1], mv[:, 1:2], ACT.Ln, bias=eps[:, :]).then_inc(log_ready, 1)
                    act.wait_ge(log_ready, i + 1)
                    act.activation(f[:, SEED:SEED + 1], f[:, LOG:LOG + 1], ACT.Exp, scale=-0.5).then_inc(ready, 1)

                def seed1(i):
                    seed(i, ln1, mv1, stats1, log1_ready, seed1_ready, ln1_ready)

                def seed2(j):
                    seed(j, ln2, mv2, stats2, log2_ready, seed2_ready, ln2_ready)

                def normalise1(i, s):
                    act.wait_ge(ln1_ready, i + 1)
                    wait(act, xq_ready, i)
                    act.activation(xn[:, :], x_t[s][:, :], ACT.Identity, bias=ln1[:, SHIFT:SHIFT + 1], scale=ln1[:, SCALE:SCALE + 1]
                                   ).then_inc(xn_ready, 1)

                def copy_queries(i, s, ns):
                    for n in ns:
                        act.wait_ge(qt_done, 4 * i + n + 1)
                        act.activation(qT[s % 2][:, 4 * n:4 * n + 4, :], MISC[n % 2][:, :].rearrange("p (h t) -> p h t", h=4),
                                       ACT.Copy).then_inc(qt_copied, 1)

                def values_hi(b):
                    act.wait_ge(ctx_loaded, 16 * b + 16)
                    wait(act, pv_done, G * SC * b)
                    src = ctx_sb[:, :, :].rearrange("p c (g d) -> p (c g) d", d=HEAD_DIM)
                    act.activation(v_hi[:, :, :, :].rearrange("p c g (two d) -> p (c g) two d", two=2),
                                   src.unsqueeze(2).to_broadcast([P, TC * G, 2, HEAD_DIM]), ACT.Copy).then_inc(vhi_ready, 1)

                def copy_keys_hi(b):
                    for g in range(G):
                        act.wait_ge(kt_done, 2 * G * b + 2 * g + 1)
                        act.activation(kT_hi[:, g, :], MISC[0][:, :], ACT.Copy).then_inc(kthi_copied, 1)

                def exponent(i, h):
                    act.wait_ge(max_ready, H * i + h + 1)
                    wait(act, pt_done, H * i + h - 3)
                    act.activation(probs[h % 4][:, :], S_BANK[h % 2][:, :], ACT.Exp, bias=neg_max[:, h:h + 1],
                                   accum_out=row_sum[:, h:h + 1]).then_inc(exp_ready, 1)

                def copy_probs_hi(i, h):
                    g, k = divmod(h, GROUP_HEADS)
                    act.wait_ge(pt_done, H * i + h + 1)
                    if k == 0:
                        wait(act, pv_done, G * i + g - 1)
                    act.activation(pT_hi[g % 2][:, :, k, :], PT_BANK[h % 2][:, :].rearrange("p (c t) -> p c t", c=TC),
                                   ACT.Copy).then_inc(pthi_copied, 1)

                def copy_out_hi(i, g):
                    act.wait_ge(pv_done, G * i + g + 1)
                    if g == 0:
                        wait(act, wo_done, NH * i)
                    for r in range(2):
                        rows = slice(HEAD_DIM * r, HEAD_DIM * (r + 1))
                        act.activation(oT_hi[rows, 2 * g:2 * g + 2, :],
                                       O_BANK[g % 2][rows, :].rearrange("p (a two t) -> p a two t", two=2, t=P)[:, :, r, :],
                                       ACT.Copy).then_inc(othi_copied, 1)

                def normalise2(j):
                    act.wait_ge(ln2_ready, j + 1)
                    wait(act, xn2_stored, 16 * j)
                    wait(act, xt2_done, 2 * j)
                    act.activation(xn2[:, :], x2[:, :], ACT.Identity, bias=ln2[:, SHIFT:SHIFT + 1], scale=ln2[:, SCALE:SCALE + 1]
                                   ).then_inc(xn2_ready, 1)

                def copy_xn2(j):
                    for n in range(2):
                        act.wait_ge(xt2_done, 2 * j + n + 1)
                        if n == 0:
                            wait(act, router_done, j)
                        act.activation(xn2T[:, 4 * n:4 * n + 4, :], MISC[n][:, :].rearrange("p (c t) -> p c t", c=4),
                                       ACT.Copy).then_inc(xt2_copied, 1)

                def top_exponent(j):
                    act.wait_ge(top_ready, j + 1)
                    wait(act, entry_ready, j)
                    act.activation(top_e[:, :], top_v[:, :], ACT.Exp, bias=neg_top[:, :], accum_out=top_s[:, :]
                                   ).then_inc(topexp_ready, 1)

                def batch(b):
                    def tile(b, s, i, back):
                        if s == 0:
                            seed1(i)
                            if back:
                                copy_out_hi(i - 1, G - 2)
                                copy_out_hi(i - 1, G - 1)
                            values_hi(b)
                            normalise1(i, s)
                            if back:
                                seed2(i - 1)
                            copy_queries(i, s, range(4))
                            copy_keys_hi(b)
                            for h in range(AHEAD):
                                exponent(i, h)
                        for h in range(H):
                            copy_probs_hi(i, h)
                            if h + AHEAD < H:
                                exponent(i, h + AHEAD)
                            elif s < SC - 1:
                                exponent(i + 1, h + AHEAD - H)
                            if h in (0, 4) and s > 0:
                                copy_out_hi(i - 1, 2 + h // 4)
                            if h in (8, 12):
                                copy_out_hi(i, h // 4 - 2)
                            if h == NEXT_STATS and s < SC - 1:
                                seed1(i + 1)
                            if h == NEXT_NORM and s < SC - 1:
                                normalise1(i + 1, s + 1)
                            if h == RESIDUAL[1] and s > 0:
                                seed2(i - 1)
                            if h == NORM2 and back:
                                normalise2(i - 1)
                            if h == TRANSPOSE2 and back:
                                copy_xn2(i - 1)
                            if h in NEXT_QUERIES and s < SC - 1:
                                n = 2 * NEXT_QUERIES.index(h)
                                copy_queries(i + 1, s + 1, (n, n + 1))
                            if h == CHOOSE and back:
                                top_exponent(i - 1)
                    tiles_of_a_batch(b, tile)

                batch(0)
                with act.Fori(1, B) as b:
                    batch(b)
                copy_out_hi(TILES - 1, G - 2)
                copy_out_hi(TILES - 1, G - 1)
                seed2(TILES - 1)
                normalise2(TILES - 1)
                copy_xn2(TILES - 1)
                top_exponent(TILES - 1)

            @block.vector
            def _(dve):
                def statistics(chain, bn, mv, rows, signal):
                    dve.bn_stats(bn[:, 0, :], rows[:, 0:512]).then_inc(chain.sem, 1)
                    dve.bn_stats(bn[:, 1, :], rows[:, 512:1024]).then_inc(chain.sem, 1)
                    chain.n += 2
                    dve.wait_ge(chain.sem, chain.before + chain.n)
                    dve.sem_inc(fence["dve"], 1)
                    dve.bn_aggr(mv[:, :], bn[:, :, :]).then_inc(signal, 1)

                def statistics1(i, s):
                    chain = Chain(dve, ln1_chain, 2 * i, 2)
                    dve.wait_ge(x_in[s], (i - s) * (16 // SC) + 16)
                    wait(dve, ln1_ready, i)
                    statistics(chain, bn1, mv1, x_t[s], stats1)
                    chain.done()

                def values_lo(b):
                    dve.wait_ge(vhi_ready, b + 1)
                    src = ctx_sb[:, :, :].rearrange("p c (g d) -> p (c g) d", d=HEAD_DIM)
                    hi = v_hi[:, :, :, :].rearrange("p c g (two d) -> p (c g) two d", two=2)
                    lo = v_lo[:, :, :, :].rearrange("p c g (two d) -> p (c g) two d", two=2)
                    dve.tensor_tensor(lo, src.unsqueeze(2).to_broadcast([P, TC * G, 2, HEAD_DIM]), hi.bitcast(F32),
                                      ALU.subtract).then_inc(vlo_ready, 1)

                def copy_keys_lo(b):
                    for g in range(G):
                        dve.wait_ge(kt_done, 2 * G * b + 2 * g + 2)
                        dve.tensor_copy(kT_lo[:, g, :], MISC[1][:, :]).then_inc(ktlo_copied, 1)

                def maximum(i, h):
                    dve.wait_ge(scores_done, H * i + h + 1)
                    dve.tensor_reduce(neg_max[:, h:h + 1], S_BANK[h % 2][:, :], AX.X, ALU.max, negate=True
                                      ).then_inc(max_ready, 1)

                def normalise_probs(i, h):
                    dve.wait_ge(exp_ready, H * i + h + 1)
                    dve.reciprocal(row_inv[:, h:h + 1], row_sum[:, h:h + 1]).then_inc(inverse_ready, 1)
                    dve.wait_ge(inverse_ready, H * i + h + 1)
                    dve.tensor_scalar(probs[h % 4][:, :], probs[h % 4][:, :], row_inv[:, h:h + 1], None, ALU.mult
                                      ).then_inc(probs_ready, 1)

                def copy_probs_lo(i, h):
                    g, k = divmod(h, GROUP_HEADS)
                    dve.wait_ge(pthi_copied, H * i + h + 1)
                    dve.tensor_tensor(pT_lo[g % 2][:, :, k, :], PT_BANK[h % 2][:, :].rearrange("p (c t) -> p c t", c=TC),
                                      pT_hi[g % 2][:, :, k, :].bitcast(F32), ALU.subtract).then_inc(ptlo_copied, 1)

                def copy_out_lo(i, g):
                    dve.wait_ge(othi_copied, 2 * (G * i + g) + 2)
                    for r in range(2):
                        rows = slice(HEAD_DIM * r, HEAD_DIM * (r + 1))
                        dve.tensor_tensor(oT_lo[rows, 2 * g:2 * g + 2, :],
                                          O_BANK[g % 2][rows, :].rearrange("p (a two t) -> p a two t", two=2, t=P)[:, :, r, :],
                                          oT_hi[rows, 2 * g:2 * g + 2, :].bitcast(F32), ALU.subtract).then_inc(otlo_copied, 1)

                def residual(j, n, s):
                    cols = slice(n * HALF, (n + 1) * HALF)
                    dve.wait_ge(wo_done, NH * j + n + 1)
                    if n == 0:
                        dve.wait_ge(xbias_ready, j + 1)
                        wait(dve, x2_stored, 16 * j)
                        wait(dve, xn2_ready, j)
                    dve.tensor_tensor(x2[:, cols], MISC[n][:, :], x_t[s][:, cols], ALU.add).then_inc(x2_ready, 1)

                def statistics2(j):
                    dve.wait_ge(x2_ready, 2 * j + 2)
                    wait(dve, ln2_ready, j)
                    statistics(Chain(dve, back_chain, BACK_STEPS * j, 0), bn2, mv2, x2, stats2)

                def choose(j):
                    chain = Chain(dve, back_chain, BACK_STEPS * j + 2, 0)
                    dve.wait_ge(router_done, j + 1)
                    dve.tensor_copy(logits[:, :], MISC[0][:, 0:E]).then_inc(logits_copied, 1)
                    dve.wait_ge(logits_copied, j + 1)
                    dve.sem_inc(fence["dve"], 1)
                    chain.then(dve.max(top_v[:, :], logits[:, :]))
                    dve.tensor_scalar(neg_top[:, :], top_v[:, 0:1], -1.0, None, ALU.mult).then_inc(top_ready, 1)
                    chain.then(dve.max_index(top_i[:, :], top_v[:, :], logits[:, :]))
                    chain.then(dve.tensor_copy(top_f[:, :], top_i[:, :]))
                    chain.then(dve.tensor_tensor(hot[:, :, :], top_f[:, :].unsqueeze(2).to_broadcast([P, TOP_K, E]),
                                                 iota_e[:, :].unsqueeze(1).to_broadcast([P, TOP_K, E]), ALU.is_equal))
                    with nc.allow_low_precision(reason="a sum of one 1 at most"):
                        dve.tensor_reduce(chosen[:, :], hot[:, :, :].rearrange("p k e -> p e k"), AX.X, ALU.add
                                          ).then_inc(chosen_ready, 1)
                    assert chain.n == 4

                def place(j):
                    chain = Chain(dve, back_chain, BACK_STEPS * j + 6, 0)
                    dve.wait_ge(rank_done, j + 1)
                    chain.then(dve.tensor_tensor(pos[:, :], MISC[1][:, 0:E], slot_base[:, :], ALU.add))
                    chain.then(dve.tensor_tensor(slot_base[:, :], MISC[1][:, E:2 * E], slot_base[:, :], ALU.add))
                    dve.sem_inc(rank_copied, 1)
                    chain.then(dve.tensor_tensor(hot_pos[:, :, :], hot[:, :, :],
                                                 pos[:, :].unsqueeze(1).to_broadcast([P, TOP_K, E]), ALU.mult))
                    wait(dve, table_written, 16 * TOP_K * j)
                    with nc.allow_low_precision(reason="one whole number below 2 ** 24 and zeros, summed in float32"):
                        chain.then(dve.tensor_reduce(slot_i[:, :], hot_pos[:, :, :], AX.X, ALU.add))
                    chain.then(dve.tensor_copy(entry[:, :, 0], token_id[:, :].to_broadcast([P, TOP_K])))
                    chain.then(dve.tensor_scalar(token_id[:, :], token_id[:, :], float(P), None, ALU.add))
                    dve.wait_ge(topexp_ready, j + 1)
                    chain.then(dve.reciprocal(top_inv[:, :], top_s[:, :]))
                    chain.then(dve.tensor_scalar(entry[:, :, 1].bitcast(F32), top_e[:, :], top_inv[:, :], None, ALU.mult))
                    dve.sem_inc(entry_ready, 1)
                    assert chain.n == 8

                def batch(b):
                    def tile(b, s, i, back):
                        if s == 0:
                            statistics1(i, s)
                            if back:
                                copy_out_lo(i - 1, G - 2)
                                copy_out_lo(i - 1, G - 1)
                            values_lo(b)
                            if back:
                                residual(i - 1, 0, SC - 1)
                                residual(i - 1, 1, SC - 1)
                                statistics2(i - 1)
                            copy_keys_lo(b)
                            for h in range(AHEAD):
                                maximum(i, h)
                            normalise_probs(i, 0)
                        for h in range(H):
                            if h + AHEAD < H:
                                maximum(i, h + AHEAD)
                            elif s < SC - 1:
                                maximum(i + 1, h + AHEAD - H)
                            if h + 1 < H:
                                normalise_probs(i, h + 1)
                            elif s < SC - 1:
                                normalise_probs(i + 1, 0)
                            copy_probs_lo(i, h)
                            if h in (0, 4) and s > 0:
                                copy_out_lo(i - 1, 2 + h // 4)
                            if h in (8, 12):
                                copy_out_lo(i, h // 4 - 2)
                            if h == NEXT_STATS and s < SC - 1:
                                statistics1(i + 1, s + 1)
                            if s > 0 and h in RESIDUAL:
                                residual(i - 1, RESIDUAL.index(h), s - 1)
                            if s > 0 and h == RESIDUAL[1]:
                                statistics2(i - 1)
                            if h == CHOOSE and back:
                                choose(i - 1)
                            if h == PLACE and back:
                                place(i - 1)
                    tiles_of_a_batch(b, tile)

                batch(0)
                with dve.Fori(1, B) as b:
                    batch(b)
                copy_out_lo(TILES - 1, G - 2)
                copy_out_lo(TILES - 1, G - 1)
                residual(TILES - 1, 0, SC - 1)
                residual(TILES - 1, 1, SC - 1)
                statistics2(TILES - 1)
                choose(TILES - 1)
                place(TILES - 1)

            @block.tensor
            def _(pe):
                def transpose_queries(i, s, ns):
                    pe.wait_ge(xq_ready, i + 1)
                    for n in ns:
                        if n >= 2:
                            pe.wait_ge(qt_copied, 4 * i + n - 1)
                        elif s == 1:
                            pe.wait_ge((kthi_copied, ktlo_copied)[n], (i - 1) * (G // SC) + G)
                            wait(pe, x2_ready, 2 * (i - 2) + n + 1)
                        else:
                            wait(pe, x2_ready, 2 * (i - (1 if s == 0 else 2)) + n + 1)
                        for k in range(4):
                            last = nc.tensor.transpose(MISC[n % 2][:, k * P:(k + 1) * P].bitcast(F32R),
                                                       xq[:, 4 * n + k, :, :].rearrange("p two d -> p (two d)"), ident_r[:, :])
                        last.then_inc(qt_done, 1)

                def transpose_keys(b, i):
                    pe.wait_ge(vlo_ready, b + 1)
                    pe.wait_ge(qt_copied, 4 * i + 4)
                    for g in range(G):
                        for n, v in enumerate((v_hi, v_lo)):
                            if g:
                                pe.wait_ge((kthi_copied, ktlo_copied)[n], G * b + g)
                            for c in range(TC):
                                last = nc.tensor.transpose(MISC[n][:, c * P:(c + 1) * P].bitcast(F32R), v[:, c, g, :],
                                                           ident_r[:, :])
                            last.then_inc(kt_done, 1)

                def scores(b, s, i, h):
                    if h % 4 == 0:
                        pe.wait_ge(qt_copied, 4 * i + h // 4 + 1)
                    if h == 0:
                        pe.wait_ge(kthi_copied, G * b + G)
                        pe.wait_ge(ktlo_copied, G * b + G)
                    wait(pe, exp_ready, H * i + h - 1)
                    g = h // GROUP_HEADS
                    nc.tensor.matmul(S_BANK[h % 2][:, :], qT[s % 2][:, h, :], kT_hi[:, g, :], start=True, stop=False)
                    nc.tensor.matmul(S_BANK[h % 2][:, :], qT[s % 2][:, h, :], kT_lo[:, g, :], start=False, stop=True
                                     ).then_inc(scores_done, 1)

                def transpose_probs(i, h):
                    pe.wait_ge(probs_ready, H * i + h + 1)
                    wait(pe, ptlo_copied, H * i + h - 1)
                    for c in range(TC):
                        last = nc.tensor.transpose(PT_BANK[h % 2][:, c * P:(c + 1) * P], probs[h % 4][:, c * P:(c + 1) * P],
                                                   ident[:, :])
                    last.then_inc(pt_done, 1)

                def values(i, g, cs):
                    if cs[0] == 0:
                        pe.wait_ge(ptlo_copied, H * i + GROUP_HEADS * (g + 1))
                        wait(pe, otlo_copied, 2 * (G * i + g - 1))
                    for c in cs:
                        for v, p in ((v_hi, pT_hi), (v_hi, pT_lo), (v_lo, pT_hi)):
                            last = nc.tensor.matmul(O_BANK[g % 2][:, :], v[:, c, g, :],
                                                    p[g % 2][:, c, :, :].rearrange("p h t -> p (h t)"),
                                                    start=(c == 0 and v is v_hi and p is pT_hi),
                                                    stop=(c == TC - 1 and v is v_lo))
                    if cs[-1] == TC - 1:
                        last.then_inc(pv_done, 1)

                def project(j, n, cs, s):
                    if cs[0] == 0:
                        if s > 0:
                            pe.wait_ge(qt_copied, 4 * (j + 1) + 3 + n)
                        wait(pe, (logits_copied, rank_copied)[n], j)
                    for c in cs:
                        if c % 2 == 0 and n == 0:
                            pe.wait_ge(otlo_copied, 2 * G * j + c + 2)
                        for o, w in ((oT_hi, WcT_hi), (oT_hi, WcT_lo), (oT_lo, WcT_hi)):
                            last = nc.tensor.matmul(MISC[n][:, :], o[:, c, :], w[:, c, n * HALF:(n + 1) * HALF],
                                                    start=(c == 0 and w is WcT_hi and o is oT_hi),
                                                    stop=(c == DC - 1 and o is oT_lo))
                    if cs[-1] == DC - 1:
                        last.then_inc(wo_done, 1)

                def transpose_xn2(j, s):
                    pe.wait_ge(xn2_ready, j + 1)
                    if s < SC - 1:
                        pe.wait_ge(qt_copied, 4 * (j + 2) + 4)
                    for n in range(2):
                        for k in range(4):
                            c = 4 * n + k
                            last = nc.tensor.transpose(MISC[n][:, k * P:(k + 1) * P], xn2[:, c * P:(c + 1) * P], ident[:, :])
                        last.then_inc(xt2_done, 1)

                def router(j):
                    pe.wait_ge(xt2_copied, 2 * j + 2)
                    for c in range(DC):
                        last = nc.tensor.matmul(MISC[0][:, 0:E], xn2T[:, c, :], gate_sb[:, c, :], start=(c == 0), stop=(c == DC - 1))
                    last.then_inc(router_done, 1)

                def ranks(j):
                    pe.wait_ge(chosen_ready, j + 1)
                    nc.tensor.matmul(MISC[1][:, 0:E], before_bf[:, :], chosen[:, :], start=True, stop=True)
                    nc.tensor.matmul(MISC[1][:, E:2 * E], ones_bf[:, :], chosen[:, :], start=True, stop=True
                                     ).then_inc(rank_done, 1)

                def batch(b):
                    def tile(b, s, i, back):
                        if s == 0:
                            if back:
                                values(i - 1, G - 1, range(TC))
                                project(i - 1, 0, list(range(DC)), 0)
                                project(i - 1, 1, list(range(DC)), 0)
                            transpose_queries(i, s, range(4))
                            transpose_keys(b, i)
                            for h in range(AHEAD):
                                scores(b, s, i, h)
                        for h in range(H):
                            if h + AHEAD < H:
                                scores(b, s, i, h + AHEAD)
                            elif s < SC - 1:
                                scores(b, s + 1, i + 1, h + AHEAD - H)
                            transpose_probs(i, h)
                            if h >= 4:
                                values(i, h // 4 - 1, (h % 4,))
                            elif s > 0:
                                values(i - 1, G - 1, (h,))
                            if s > 0:
                                for n, c0, c1 in PROJECT.get(h, ()):
                                    project(i - 1, n, list(range(c0, c1)), s)
                            if h == TRANSPOSE2 and back:
                                transpose_xn2(i - 1, s)
                            if h == ROUTER and back:
                                router(i - 1)
                            if h in NEXT_QUERIES and s < SC - 1:
                                n = 2 * NEXT_QUERIES.index(h)
                                transpose_queries(i + 1, s + 1, (n, n + 1))
                            if h == PLACE and back:
                                ranks(i - 1)
                    tiles_of_a_batch(b, tile)

                batch(0)
                with pe.Fori(1, B) as b:
                    batch(b)
                values(TILES - 1, G - 1, range(TC))
                project(TILES - 1, 0, list(range(DC)), 0)
                project(TILES - 1, 1, list(range(DC)), 0)
                transpose_xn2(TILES - 1, SC - 1)
                router(TILES - 1)
                ranks(TILES - 1)


        schedule_stage(nc, sb, sem, ident, slot_base, expert_base, sched_dram, T=T, E=E, SCHED_COLS=SCHED_COLS,
                       TABLE_PAD=TABLE_PAD, top=top, experts=lambda row, used: experts_stage(
                           nc, sb, sem, banks, row, used, xn_dram, table, gate_proj, up_proj, down_v, out,
                           T=T, D=D, DC=DC, M=M, MC=MC, E=E, TABLE_PAD=TABLE_PAD, MOST_TILES=MOST_TILES))


def setup_stage(nc, sb, sem, banks, Wc, bc, gate_w, xn_dram, table, out, ident, ident_r, before_bf, ones_bf, gate_sb,
                bias_row, iota_e, token_id, eps, slot_base, expert_base, WcT_hi, WcT_lo, *, D, DC, E, T, TABLE_ROWS):
    ROWS = TABLE_ROWS // P
    assert ROWS * P == TABLE_ROWS and T % SLOT_ROWS == 0
    mem = ExitStack()
    with mem:
        Wc_sb = sb(mem, "Wc_sb", [P, DC, D], F32)
        row_i = sb(mem, "row_i", [P, ROWS], I32)
        row_m = sb(mem, "row_m", [P, ROWS], I32)
        empty = sb(mem, "empty", [P, ROWS, 2], I32)
        zeros = sb(mem, "zeros", [P, D], F32)
        before_f = sb(mem, "before_f", [P, P], F32)
        wc_loaded, small_loaded, stored = sem("wc_loaded"), sem("small_loaded"), sem("setup_stored")
        made, ident_made, ident_r_made, empty_made = sem("made"), sem("ident_made"), sem("ident_r_made"), sem("empty_made")
        wct_done, wct_hi, wct_lo = sem("wct_done"), sem("wct_hi"), sem("wct_lo")
        block = mem.enter_context(nc.Block())
        GROUPS = [(c, n) for c in range(DC) for n in range(DC // 4)]

        @block.sync
        def _(sp):
            sp.dma_start(Wc_sb[:, :, :], Wc.rearrange("(n p) c -> p n c", p=P)).then_inc(wc_loaded, 16)
            sp.dma_start(gate_sb[:, :, :], gate_w.rearrange("(c p) e -> p c e", p=P)).then_inc(small_loaded, 16)
            sp.dma_start(bias_row[:, :], bc.unsqueeze(0).to_broadcast([P, D])).then_inc(small_loaded, 16)
            sp.wait_ge(empty_made, 2)
            sp.dma_start(table.rearrange("(p r) two -> p (r two)", p=P), empty[:, :, :].rearrange("p r two -> p (r two)")
                         ).then_inc(stored, 16)
            for rows in (xn_dram[T:T + SLOT_ROWS, :], out[T:T + SLOT_ROWS, :]):
                for q in range(SLOT_ROWS // P):
                    sp.dma_start(rows[q * P:(q + 1) * P, :], zeros[:, :]).then_inc(stored, 16)
            sp.wait_ge(small_loaded, 32)
            sp.wait_ge(stored, 16 * (1 + 2 * SLOT_ROWS // P))

        @block.gpsimd
        def _(pool):
            pool.memset(ident[:, :], 0.0).then_inc(made, 1)
            pool.memset(before_f[:, :], 1.0).then_inc(made, 1)
            pool.wait_ge(made, 2)
            pool.affine_select(out=ident[:, :], in_=ident[:, :], compare_op=ALU.not_equal, fill=1.0, base=0,
                               pattern=[[-1, P]], channel_multiplier=1).then_inc(ident_made, 1)
            pool.affine_select(out=before_f[:, :], in_=before_f[:, :], compare_op=ALU.is_gt, fill=0.0, base=0,
                               pattern=[[1, P]], channel_multiplier=-1).then_inc(made, 1)
            pool.memset(ones_bf[:, :], 1.0)
            pool.memset(eps[:, :], EPS)
            pool.iota(iota_e[:, :], [[1, E]], base=0, channel_multiplier=0, allow_small_or_imprecise_dtypes=True)
            pool.iota(token_id[:, :], [[0, 1]], base=0, channel_multiplier=1, allow_small_or_imprecise_dtypes=True)
            pool.iota(slot_base[:, :], [[T, E]], base=0, channel_multiplier=0, allow_small_or_imprecise_dtypes=True)
            pool.iota(expert_base[:, :], [[T, E]], base=0, channel_multiplier=0, allow_small_or_imprecise_dtypes=True)
            pool.iota(row_i[:, :], [[1, ROWS]], base=0, channel_multiplier=ROWS % SLOT_ROWS).then_inc(made, 1)
            pool.wait_ge(made, 4)
            pool.tensor_copy(before_bf[:, :], before_f[:, :])

        @block.vector
        def _(dve):
            dve.memset(zeros[:, :], 0.0).then_inc(empty_made, 1)
            dve.memset(empty[:, :, 1], 0)
            dve.wait_ge(ident_made, 1)
            dve.tensor_copy(ident_r[:, :], ident[:, :]).then_inc(ident_r_made, 1)
            dve.wait_ge(made, 4)
            dve.tensor_single_scalar(row_m[:, :], row_i[:, :], SLOT_ROWS - 1, ALU.bitwise_and).then_inc(ident_r_made, 1)
            dve.wait_ge(ident_r_made, 2)
            dve.tensor_scalar(empty[:, :, 0], row_m[:, :], float(T), None, ALU.add).then_inc(empty_made, 1)
            for k, (c, n) in enumerate(GROUPS):
                dve.wait_ge(wct_hi, k + 1)
                dve.tensor_tensor(WcT_lo[:, c, n * 512:(n + 1) * 512], banks[k % 2][:, :],
                                  WcT_hi[:, c, n * 512:(n + 1) * 512].bitcast(F32), ALU.subtract).then_inc(wct_lo, 1)

        @block.scalar
        def _(act):
            for k, (c, n) in enumerate(GROUPS):
                act.wait_ge(wct_done, k + 1)
                act.activation(WcT_hi[:, c, n * 512:(n + 1) * 512], banks[k % 2][:, :], ACT.Copy).then_inc(wct_hi, 1)

        @block.tensor
        def _(pe):
            pe.wait_ge(ident_made, 1)
            pe.wait_ge(wc_loaded, 16)
            for k, (c, n) in enumerate(GROUPS):
                if k >= 2:
                    pe.wait_ge(wct_lo, k - 1)
                for m in range(4):
                    last = nc.tensor.transpose(banks[k % 2][:, m * P:(m + 1) * P], Wc_sb[:, 4 * n + m, c * P:(c + 1) * P],
                                               ident[:, :])
                last.then_inc(wct_done, 1)


def schedule_stage(nc, sb, sem, ident, slot_base, expert_base, sched_dram, *, T, E, SCHED_COLS, TABLE_PAD, top, experts):
    SIZES = T // SLOT_ROWS
    SCHED = SCHED_COLS * P
    row = sb(top, "sched_row", [1, SCHED * 4], I32)
    used = sb(top, "tiles_used", [P, 1], I32)
    mem = ExitStack()
    with mem:
        steps = sb(mem, "steps", [P, SIZES], F32)
        upto = sb(mem, "upto", [P, E, E], F32)
        tile_no = sb(mem, "tile_no", [P, 2, SCHED_COLS], F32)
        count = sb(mem, "count", [P, E], F32)
        more = sb(mem, "more", [P, E, SIZES], F32)
        tiles = sb(mem, "tiles", [P, E], F32)
        part = sb(mem, "part", [P, E, E], F32)
        ends = sb(mem, "ends", [P, E], F32)
        passed = sb(mem, "passed", [P, 2 * SCHED_COLS, E], F32)
        expert = sb(mem, "expert", [P, 2, SCHED_COLS], F32)
        taken = sb(mem, "taken", [P, SCHED_COLS, E], F32)
        first = sb(mem, "first", [P, SCHED_COLS], F32)
        offset = sb(mem, "offset", [P, SCHED_COLS], F32)
        offset2 = sb(mem, "offset2", [P, SCHED_COLS], F32)
        clamped = sb(mem, "clamped", [P, 2, SCHED_COLS], F32)
        expert_no = sb(mem, "expert_no", [P, E], F32)
        own = sb(mem, "own", [P, SCHED_COLS, E], F32)
        own_count = sb(mem, "own_count", [P, SCHED_COLS, E], F32)
        rows = sb(mem, "rows", [P, SCHED_COLS], F32)
        left = sb(mem, "left", [P, SCHED_COLS], F32)
        sched = sb(mem, "sched", [P, SCHED_COLS, 4], I32)
        consts, chain_sem, ready, stored = sem("sched_consts"), sem("sched_chain"), sem("sched_ready"), sem("sched_stored")
        block = mem.enter_context(nc.Block())

        @block.gpsimd
        def _(pool):
            pool.iota(steps[:, :], [[SLOT_ROWS, SIZES]], base=0, channel_multiplier=0,
                      allow_small_or_imprecise_dtypes=True).then_inc(consts, 1)
            pool.iota(tile_no[:, :, :], [[-1, 2], [P, SCHED_COLS]], base=0, channel_multiplier=1,
                      allow_small_or_imprecise_dtypes=True).then_inc(consts, 1)
            pool.iota(expert_no[:, :], [[1, E]], base=0, channel_multiplier=0,
                      allow_small_or_imprecise_dtypes=True).then_inc(consts, 1)
            pool.memset(upto[:, :, :], 1.0).then_inc(consts, 1)
            pool.wait_ge(consts, 4)
            pool.affine_select(out=upto[:, :, :], in_=upto[:, :, :], compare_op=ALU.is_ge, fill=0.0, base=0,
                               pattern=[[1, E], [-1, E]], channel_multiplier=0).then_inc(consts, 1)

        @block.vector
        def _(dve):
            chain = Chain(dve, chain_sem, 0, 0)
            do = chain.then
            do(dve.tensor_tensor(count[:, :], slot_base[:, :], expert_base[:, :], ALU.subtract))
            dve.wait_ge(consts, 5)
            do(dve.tensor_tensor(more[:, :, :], count[:, :].unsqueeze(2).to_broadcast([P, E, SIZES]),
                                 steps[:, :].unsqueeze(1).to_broadcast([P, E, SIZES]), ALU.is_gt))
            do(dve.tensor_reduce(tiles[:, :], more[:, :, :], AX.X, ALU.add))
            do(dve.tensor_tensor(part[:, :, :], upto[:, :, :], tiles[:, :].unsqueeze(1).to_broadcast([P, E, E]), ALU.mult))
            do(dve.tensor_reduce(ends[:, :], part[:, :, :], AX.X, ALU.add))
            do(dve.tensor_copy(used[:, :], ends[:, E - 1:E]))
            do(dve.tensor_tensor(passed[:, :, :],
                                 tile_no[:, :, :].rearrange("p a c -> p (a c)").unsqueeze(2).to_broadcast([P, 2 * SCHED_COLS, E]),
                                 ends[:, :].unsqueeze(1).to_broadcast([P, 2 * SCHED_COLS, E]), ALU.is_ge))
            do(dve.tensor_reduce(expert[:, :, :].rearrange("p a c -> p (a c)"), passed[:, :, :], AX.X, ALU.add))
            do(dve.tensor_tensor(taken[:, :, :], passed[:, 0:SCHED_COLS, :],
                                 tiles[:, :].unsqueeze(1).to_broadcast([P, SCHED_COLS, E]), ALU.mult))
            do(dve.tensor_reduce(first[:, :], taken[:, :, :], AX.X, ALU.add))
            do(dve.tensor_tensor(offset[:, :], tile_no[:, 0, :], first[:, :], ALU.subtract))
            do(dve.tensor_scalar(offset2[:, :], offset[:, :], float(SLOT_ROWS), None, ALU.mult))
            do(dve.scalar_tensor_tensor(out=offset[:, :], in0=expert[:, 0, :], scalar=float(T), in1=offset2[:, :],
                                        op0=ALU.mult, op1=ALU.add))
            do(dve.tensor_tensor(own[:, :, :], expert[:, 0, :].unsqueeze(2).to_broadcast([P, SCHED_COLS, E]),
                                 expert_no[:, :].unsqueeze(1).to_broadcast([P, SCHED_COLS, E]), ALU.is_equal))
            do(dve.tensor_tensor(own_count[:, :, :], own[:, :, :],
                                 count[:, :].unsqueeze(1).to_broadcast([P, SCHED_COLS, E]), ALU.mult))
            do(dve.tensor_reduce(rows[:, :], own_count[:, :, :], AX.X, ALU.add))
            do(dve.tensor_tensor(left[:, :], rows[:, :], offset2[:, :], ALU.subtract))
            do(dve.tensor_scalar(sched[:, :, 3], left[:, :], float(SLOT_ROWS // 2), None, ALU.is_le))
            do(dve.tensor_scalar(sched[:, :, 0], offset[:, :], float(TABLE_PAD), None, ALU.min))
            do(dve.tensor_scalar(clamped[:, :, :], expert[:, :, :], float(E - 1), None, ALU.min))
            do(dve.tensor_copy(sched[:, :, 1], clamped[:, 0, :]))
            do(dve.tensor_tensor(sched[:, :, 2], clamped[:, 0, :], clamped[:, 1, :], ALU.not_equal))
            dve.sem_inc(ready, 1)

        @block.sync
        def _(sp):
            sp.wait_ge(ready, 1)
            sp.dma_start(sched_dram.rearrange("(c p) k -> p c k", p=P), sched[:, :, :]).then_inc(stored, 16)
            sp.wait_ge(stored, 16)
            sp.dma_start(row[:, :], sched_dram.rearrange("t k -> (t k)").unsqueeze(0)).then_inc(stored, 16)
            sp.wait_ge(stored, 32)

    experts(row, used)


def experts_stage(nc, sb, sem, banks, sched_row, tiles_used, xn_dram, table, gate_proj, up_proj, down_v, out, *,
                  T, D, DC, M, MC, E, TABLE_PAD, MOST_TILES):
    Q = SLOT_ROWS // P
    NH = D // 512
    OUT_GROUPS = Q * NH
    QUAD = 32
    KQ = P // QUAD
    RUNS = SLOT_ROWS // QUAD
    QUARTER_ROW = D // KQ
    assert QUARTER_ROW == DC * QUAD
    quarter_rows = xn_dram.rearrange("t (k d) -> (t k) d", k=KQ)
    weights_v = [w.rearrange("e (k c r) m -> e k r c m", k=KQ, r=QUAD) for w in (gate_proj, up_proj)]

    mem = ExitStack()
    with mem:
        gu_raw = sb(mem, "gu_raw", [P, 2, DC, M], F32)
        d_raw = sb(mem, "d_raw", [P, MC, D], F32)
        gu_hi = sb(mem, "gu_hi", [P, DC, 2, M], F32R)
        gu_lo = sb(mem, "gu_lo", [P, DC, 2, M], F32R)
        d_hi = sb(mem, "d_hi", [P, MC, D], F32R)
        d_lo = sb(mem, "d_lo", [P, MC, D], F32R)
        xg = sb(mem, "xg", [P, RUNS, QUARTER_ROW], F32)
        xT = sb(mem, "xT", [P, DC, SLOT_ROWS], F32)
        xT_hi = sb(mem, "xT_hi", [P, DC, SLOT_ROWS], F32R)
        xT_lo = sb(mem, "xT_lo", [P, DC, SLOT_ROWS], F32R)
        gated = [sb(mem, f"gated{n}", [P, SLOT_ROWS], F32) for n in range(2)]
        h = sb(mem, "h", [P, SLOT_ROWS], F32)
        h_hi = sb(mem, "h_hi", [P, MC, SLOT_ROWS], F32R)
        h_lo = sb(mem, "h_lo", [P, MC, SLOT_ROWS], F32R)
        rows_out = sb(mem, "rows_out", [P, Q, D], F32)
        entry_in = sb(mem, "entry_in", [P, RUNS, 2], I32)
        entry_next = sb(mem, "entry_next", [P, RUNS, 2], I32)
        entry_now = sb(mem, "entry_now", [P, Q, 2], I32)
        quarter_no = sb(mem, "quarter_no", [P, 1], F32)
        gather_row = sb(mem, "gather_row", [P, RUNS], I32)
        GU_BANK, D_BANK = banks[0:6], banks[6:8]

        gu_loaded, d_loaded, entry_loaded = sem("gu_loaded"), sem("d_loaded"), sem("entry_loaded")
        gathered, scattered = sem("gathered"), sem("scattered")
        quarter_made, rows_made, entry_taken, entry_kept = sem("quarter_made"), sem("rows_made"), sem("entry_taken"), sem("entry_kept")
        xt_ready, xt_hi, xt_lo = sem("xt_ready"), sem("xt_hi"), sem("xt_lo")
        guhi_ready, gulo_ready, dhi_ready, dlo_ready = sem("guhi_ready"), sem("gulo_ready"), sem("dhi_ready"), sem("dlo_ready")
        gu_done, silu_ready, h_ready, hhi_ready, hlo_ready = sem("gu_done"), sem("silu_ready"), sem("h_ready"), sem("hhi_ready"), sem("hlo_ready")
        down_done, left_ready, right_ready = sem("down_done"), sem("left_ready"), sem("right_ready")
        fence = {n: sem(f"fence2_{n}") for n in ("pool", "sp")}

        def all_tiles(eng, tile):
            used = eng.value_load(tiles_used[0:1, 0:1], min_val=1, max_val=MOST_TILES)
            tile(0)
            with eng.Fori(1, MOST_TILES) as t:
                with eng.If(t < used):
                    tile(t)

        block = mem.enter_context(nc.Block())

        @block.sync
        def _(sp):
            def hold(semaphore, value):
                sp.wait_ge(semaphore, value)
                sp.sem_inc(fence["sp"], 1)

            def load_entries(t):
                first_row = sp.value_load(sched_row[0:1, bass.ds(4 * t, 1)], min_val=0, max_val=TABLE_PAD)
                wait(sp, entry_taken, t)
                for k in range(KQ):
                    sp.dma_start(entry_in[k * QUAD:(k + 1) * QUAD, :, :].rearrange("r (a m) two -> r a (m two)", a=2),
                                 table[bass.ds(first_row, SLOT_ROWS), :].rearrange("(a r m) two -> r a (m two)", a=2, r=QUAD)
                                 ).then_inc(entry_loaded, 16)

            def load_weights(t):
                e = sp.value_load(sched_row[0:1, bass.ds(4 * t + 1, 1)], min_val=0, max_val=E - 1)
                first = isinstance(t, int) and t == 0
                only = {} if first else {"cond": sp.value_load(sched_row[0:1, bass.ds(4 * t + 2, 1)], min_val=0, max_val=1)}
                wait(sp, gulo_ready, DC * t)
                for n, w in enumerate(weights_v):
                    for k in range(KQ):
                        sp.dma_start(gu_raw[k * QUAD:(k + 1) * QUAD, n, :, :],
                                     w[bass.ds(e, 1), k, :, :, :].rearrange("e r c m -> r (e c) m"), **only
                                     ).then_inc(gu_loaded, 16)
                wait(sp, dlo_ready, MC * t)
                sp.dma_start(d_raw[:, :, :], down_v[bass.ds(e, 1), :, :, :].rearrange("e p c d -> p (e c) d"), **only
                             ).then_inc(d_loaded, 16)

            def tile(t):
                load_entries(t + 2)
                load_weights(t + 1)
                hold(d_loaded, 16 * (t + 2))

            load_entries(0)
            load_weights(0)
            load_entries(1)
            all_tiles(sp, tile)

        @block.gpsimd
        def _(pool):
            def hold(semaphore, value):
                if isinstance(value, int) and value <= 0:
                    return
                pool.wait_ge(semaphore, value)
                pool.sem_inc(fence["pool"], 1)

            def gather(t):
                hold(entry_loaded, 16 * KQ * (t + 1))
                pool.tensor_scalar(gather_row[:, :], entry_in[:, :, 0], float(KQ), quarter_no[:, :], ALU.mult, ALU.add
                                   ).then_inc(rows_made, 1)
                hold(rows_made, t + 1)
                hold(xt_ready, DC * t)
                for m in range(RUNS):
                    pool.indirect_dma_start(
                        out=xg[:, m, :], out_offset=None, in_=quarter_rows,
                        in_offset=bass.IndirectOffsetOnAxis(ap=gather_row[:, m:m + 1], axis=0),
                        bounds_check=KQ * (T + SLOT_ROWS) - 1, oob_is_err=True).then_inc(gathered, 16)

            def keep(t):
                pool.tensor_copy(entry_next[:, :, :], entry_in[:, :, :]).then_inc(entry_taken, 1)
                hold(entry_taken, t + 1)

            def tile(t):
                for k in range(KQ):
                    quad = slice(k * QUAD, (k + 1) * QUAD)
                    pool.tensor_copy(entry_now[quad, :, :],
                                     entry_next[quad, :, :].rearrange("r (q k) two -> r q k two", k=KQ)[:, :, k, :]
                                     ).then_inc(entry_kept, 1)
                hold(entry_kept, KQ * (t + 1))
                keep(t + 1)
                gather(t + 2)
                for q in range(Q):
                    hold(left_ready, Q * t + q + 1)
                    hold(right_ready, Q * t + q + 1)
                    pool.indirect_dma_start(
                        out=out, out_offset=bass.IndirectOffsetOnAxis(ap=entry_now[:, q, 0:1], axis=0),
                        in_=rows_out[:, q, :], in_offset=None, bounds_check=T + SLOT_ROWS - 1, oob_is_err=True,
                        compute_op=ALU.add).then_inc(scattered, 16)
                hold(gathered, 16 * RUNS * (t + 3))
                hold(scattered, 16 * Q * (t + 1))

            for k in range(KQ):
                pool.memset(quarter_no[k * QUAD:(k + 1) * QUAD, :], float(k)).then_inc(quarter_made, 1)
            pool.wait_ge(quarter_made, KQ)
            gather(0)
            keep(0)
            hold(gathered, 16 * RUNS)
            gather(1)
            hold(gathered, 16 * RUNS * 2)
            all_tiles(pool, tile)

        @block.scalar
        def _(act):
            def x_hi(t, c):
                act.wait_ge(xt_ready, DC * t + c + 1)
                wait(act, gu_done, MC * t)
                act.activation(xT_hi[:, c, :], xT[:, c, :], ACT.Copy).then_inc(xt_hi, 1)

            def gate_up_hi(t, c):
                act.wait_ge(gu_loaded, 16 * 2 * KQ * (t + 1))
                act.activation(gu_hi[:, c, :, :], gu_raw[:, :, c, :], ACT.Copy).then_inc(guhi_ready, 1)

            def down_hi(t, k):
                act.wait_ge(d_loaded, 16 * (t + 1))
                wait(act, down_done, OUT_GROUPS * t)
                act.activation(d_hi[:, k, :], d_raw[:, k, :], ACT.Copy).then_inc(dhi_ready, 1)

            def silu(t, j):
                act.wait_ge(gu_done, MC * t + j + 1)
                wait(act, h_ready, MC * t + j - (1 if j else 2 - MC % 2))
                act.activation(gated[j % 2][:, :], GU_BANK[2 * j][:, :], ACT.Silu).then_inc(silu_ready, 1)

            def left_rows(t, q):
                act.wait_ge(down_done, OUT_GROUPS * t + NH * q + 1)
                if q == 0:
                    act.wait_ge(entry_kept, KQ * (t + 1))
                    wait(act, scattered, 16 * Q * t)
                act.activation(rows_out[:, q, 0:512], D_BANK[0][:, :], ACT.Copy,
                               scale=entry_now[:, q, 1:2].bitcast(F32)).then_inc(left_ready, 1)

            def tile(t):
                for k in range(MC):
                    down_hi(t, k)
                    silu(t, k)
                for c in range(DC):
                    x_hi(t + 1, c)
                    gate_up_hi(t + 1, c)
                    if c % 2 == 1:
                        left_rows(t, c // 2)

            for c in range(DC):
                x_hi(0, c)
                gate_up_hi(0, c)
            all_tiles(act, tile)

        @block.vector
        def _(dve):
            def transpose_rows(t, c):
                if c == 0:
                    dve.wait_ge(gathered, 16 * RUNS * (t + 1))
                    wait(dve, xt_lo, DC * t)
                dve.transpose(xT[:, c, :].rearrange("p (m r) -> p m r", r=QUAD), xg[:, :, c * QUAD:(c + 1) * QUAD]
                              ).then_inc(xt_ready, 1)

            def x_lo(t, c):
                dve.wait_ge(xt_hi, DC * t + c + 1)
                dve.tensor_tensor(xT_lo[:, c, :], xT[:, c, :], xT_hi[:, c, :].bitcast(F32), ALU.subtract
                                  ).then_inc(xt_lo, 1)

            def gate_up_lo(t, c):
                dve.wait_ge(guhi_ready, DC * t + c + 1)
                dve.tensor_tensor(gu_lo[:, c, :, :], gu_raw[:, :, c, :], gu_hi[:, c, :, :].bitcast(F32), ALU.subtract
                                  ).then_inc(gulo_ready, 1)

            def down_lo(t, k):
                dve.wait_ge(dhi_ready, MC * t + k + 1)
                dve.tensor_tensor(d_lo[:, k, :], d_raw[:, k, :], d_hi[:, k, :].bitcast(F32), ALU.subtract
                                  ).then_inc(dlo_ready, 1)

            def hidden(t, j):
                dve.wait_ge(silu_ready, MC * t + j + 1)
                wait(dve, hlo_ready, MC * t + j)
                dve.tensor_tensor(h[:, :], GU_BANK[2 * j + 1][:, :], gated[j % 2][:, :], ALU.mult).then_inc(h_ready, 1)
                dve.wait_ge(h_ready, MC * t + j + 1)
                wait(dve, down_done, OUT_GROUPS * t)
                dve.tensor_copy(h_hi[:, j, :], h[:, :]).then_inc(hhi_ready, 1)
                dve.wait_ge(hhi_ready, MC * t + j + 1)
                dve.tensor_tensor(h_lo[:, j, :], h[:, :], h_hi[:, j, :].bitcast(F32), ALU.subtract).then_inc(hlo_ready, 1)

            def right_rows(t, q):
                dve.wait_ge(down_done, OUT_GROUPS * t + NH * q + 2)
                if q == 0:
                    dve.wait_ge(entry_kept, KQ * (t + 1))
                    wait(dve, scattered, 16 * Q * t)
                dve.tensor_scalar(rows_out[:, q, 512:1024], D_BANK[1][:, :], entry_now[:, q, 1:2].bitcast(F32), None,
                                  ALU.mult).then_inc(right_ready, 1)

            def tile(t):
                for k in range(MC):
                    down_lo(t, k)
                    hidden(t, k)
                    for c in ((0, 1, 2, 3), (4, 5, 6, 7), ())[k]:
                        transpose_rows(t + 1, c)
                for c in range(DC):
                    x_lo(t + 1, c)
                    gate_up_lo(t + 1, c)
                    if c % 2 == 1:
                        right_rows(t, c // 2)

            for c in range(DC):
                transpose_rows(0, c)
                x_lo(0, c)
                gate_up_lo(0, c)
            all_tiles(dve, tile)

        @block.tensor
        def _(pe):
            def gate_up(t, j, cols):
                wait(pe, h_ready, MC * (t - 1) + j + 1)
                for n, bank in enumerate(GU_BANK[2 * j:2 * j + 2]):
                    for c in range(DC):
                        if j == 0 and n == 0:
                            pe.wait_ge(xt_lo, DC * t + c + 1)
                            pe.wait_ge(gulo_ready, DC * t + c + 1)
                        for w, v in ((gu_hi, xT_hi), (gu_hi, xT_lo), (gu_lo, xT_hi)):
                            last = nc.tensor.matmul(bank[:, 0:cols], w[:, c, n, j * P:(j + 1) * P], v[:, c, 0:cols],
                                                    start=(c == 0 and w is gu_hi and v is xT_hi),
                                                    stop=(c == DC - 1 and w is gu_lo))
                last.then_inc(gu_done, 1)

            def down(t, g, ks, cols=512):
                q, n = divmod(g, NH)
                if ks[0] == 0:
                    wait(pe, (left_ready, right_ready)[n], Q * t + q)
                for k in ks:
                    if g == 0:
                        pe.wait_ge(dlo_ready, MC * t + k + 1)
                        pe.wait_ge(hlo_ready, MC * t + k + 1)
                    for v, w in ((h_hi, d_hi), (h_hi, d_lo), (h_lo, d_hi)):
                        last = nc.tensor.matmul(D_BANK[n][:, 0:cols], v[:, k, q * P:(q + 1) * P],
                                                w[:, k, n * 512:n * 512 + cols],
                                                start=(k == ks[0] == 0 and v is h_hi and w is d_hi),
                                                stop=(k == MC - 1 and v is h_lo))
                if ks[-1] == MC - 1:
                    last.then_inc(down_done, 1)

            def products(t, cols):
                for j in range(MC):
                    gate_up(t, j, cols)
                early, late = list(range(MC - 1)), [MC - 1]
                down(t, 0, early)
                down(t, 1, early)
                down(t, 0, late)
                down(t, 1, late)
                for g in range(2, OUT_GROUPS):
                    if g // NH * P < cols:
                        down(t, g, early + late)
                    else:
                        empty_group(t, g)

            def empty_group(t, g):
                q, n = divmod(g, NH)
                wait(pe, (left_ready, right_ready)[n], Q * t + q)
                nc.tensor.matmul(D_BANK[n][:, 0:P], h_hi[:, 0, 0:P], d_hi[:, 0, 0:P], start=True, stop=True
                                 ).then_inc(down_done, 1)

            def tile(t):
                half = pe.value_load(sched_row[0:1, bass.ds(4 * t + 3, 1)], min_val=0, max_val=1)
                with pe.If(half > 0):
                    products(t, SLOT_ROWS // 2)
                with pe.Else():
                    products(t, SLOT_ROWS)

            all_tiles(pe, tile)


_INS = ["x", "ctx_512", "L0_xattn_Wc", "L0_xattn_bc", "L0_ffn_gate_kernel", "L0_ffn_gate_proj", "L0_ffn_up_proj",
        "L0_ffn_down_proj"]


def kernel(**inputs):
    import numpy as _np
    import concourse.bacc as _bacc
    from concourse import mybir as _mybir
    from concourse.bass_utils import run_bass_kernel_spmd as _run

    nc = _bacc.Bacc("TRN2", target_bir_lowering=False, num_devices=1, dynamic_dma_scratch_size=DMA_RING)
    arrays, args = {}, []
    for name in _INS:
        a = _np.ascontiguousarray(inputs[name])
        arrays[f"in_{name}"] = a
        args.append(nc.dram_tensor(f"in_{name}", a.shape, _mybir.dt.from_np(a.dtype), kind="ExternalInput").ap())
    B, S, D = inputs["x"].shape
    out = nc.dram_tensor("out_rows", (B * S + SLOT_ROWS, D), F32, kind="ExternalOutput").ap()
    moe_block(nc, *args, out)
    r = _run(nc, [arrays], core_ids=[0])
    return r.results[0]["out_rows"][:B * S].reshape(B, S, D)
```

```python
import concourse.bass as bass
from concourse import mybir
from contextlib import ExitStack

F32 = mybir.dt.float32
F32R = mybir.dt.float32r
BF16 = mybir.dt.bfloat16
I32 = mybir.dt.int32
U32 = mybir.dt.uint32
ALU = mybir.AluOpType
ACT = mybir.ActivationFunctionType
AX = mybir.AxisListType
P = 128
EPS = 1e-5
TOP_K = 8
HEAD_DIM = 64
GROUP_HEADS = 4
SLOT_ROWS = 512
SHORT, HALF_TILE = 384, 256
DMA_RING = 8192


def wait(eng, sem, value):
    if isinstance(value, int) and value <= 0:
        return
    eng.wait_ge(sem, value)


class Chain:

    def __init__(self, eng, sem, before):
        self.eng, self.sem, self.before, self.n = eng, sem, before, 0

    def then(self, instruction):
        instruction.then_inc(self.sem, 1)
        self.n += 1
        self.eng.wait_ge(self.sem, self.before + self.n)


def moe_block(nc, x, ctx_in, Wc, bc, gate_w, gate_proj, up_proj, down_proj, out):
    B, S, D = x.shape
    CD = ctx_in.shape[2]
    E, _, M = gate_proj.shape
    T = B * S
    DC = D // P
    MC = M // P
    TC = ctx_in.shape[1] // P
    SC = S // P
    H = D // HEAD_DIM
    G = H // GROUP_HEADS
    HALF = 512
    NH = D // HALF
    TILES = T // P
    PAD_ROW = T
    TABLE_PAD = E * T
    TABLE_ROWS = TABLE_PAD + SLOT_ROWS
    QUARTERS = SLOT_ROWS // P
    MOST_TILES = (T * TOP_K + E * (SLOT_ROWS - 1)) // SLOT_ROWS
    SCHED_COLS = (MOST_TILES + 2 + P - 1) // P
    SCHED = SCHED_COLS * P
    assert CD == G * HEAD_DIM and TC * P == 512 and S == 512 and QUARTERS == 4

    x_rows = x.rearrange("b s d -> (b s) d")
    ctx_v = ctx_in.rearrange("b (c p) d -> p b c d", p=P)
    down_v = down_proj.rearrange("e (c p) d -> e p c d", p=P)

    xn_dram = nc.dram_tensor("xn_rows", (T + SLOT_ROWS, D), F32, kind="Internal").ap()
    table = nc.dram_tensor("slot_table", (TABLE_ROWS, 2), I32, kind="Internal").ap()
    sched_dram = nc.dram_tensor("tile_schedule", (SCHED, 4), I32, kind="Internal").ap()

    top = ExitStack()
    with top:
        def sb(ctx, name, shape, dt):
            return ctx.enter_context(nc.sbuf_tensor(name, shape, dt))

        def sem(name):
            return top.enter_context(nc.semaphore(name))

        banks = [top.enter_context(nc.psum_tensor(f"bank{n}", [P, 512], F32)) for n in range(8)]

        ident = sb(top, "ident", [P, P], F32)
        slot_base = sb(top, "slot_base", [P, E], F32)
        expert_base = sb(top, "expert_base", [P, E], F32)

        attention_mem = ExitStack()
        with attention_mem:
            WcT_hi = sb(attention_mem, "WcT_hi", [P, DC, D], F32R)
            WcT_lo = sb(attention_mem, "WcT_lo", [P, DC, D], F32R)
            ident_r = sb(attention_mem, "ident_r", [P, P], F32R)
            before_bf = sb(attention_mem, "before_bf", [P, P], BF16)
            ones_bf = sb(attention_mem, "ones_bf", [P, P], BF16)
            gate_sb = sb(attention_mem, "gate_sb", [P, DC, E], F32)
            bias_row = sb(attention_mem, "bias_row", [P, D], F32)
            iota_e = sb(attention_mem, "iota_e", [P, E], F32)
            token_id = sb(attention_mem, "token_id", [P, 1], F32)

            setup_stage(nc, sb, sem, banks, Wc, bc, gate_w, xn_dram, table, out, ident, ident_r, before_bf,
                        ones_bf, gate_sb, bias_row, iota_e, token_id, slot_base, expert_base, WcT_hi, WcT_lo,
                        D=D, DC=DC, E=E, T=T, TABLE_ROWS=TABLE_ROWS)

            x_t = [sb(attention_mem, f"x_t{n}", [P, D], F32) for n in range(SC)]
            xn = sb(attention_mem, "xn", [P, D], F32)
            xq = sb(attention_mem, "xq", [P, H, 2, HEAD_DIM], F32R)
            qT = [sb(attention_mem, f"qT{n}", [P, H, P], F32R) for n in range(2)]
            ctx_sb = sb(attention_mem, "ctx_sb", [P, TC, CD], F32)
            v = sb(attention_mem, "v", [P, TC, G, 2, HEAD_DIM], F32R)
            kT = sb(attention_mem, "kT", [P, G, 512], F32R)
            kT_swapped = sb(attention_mem, "kT_swapped", [P, G, 512], F32R)
            probs = [sb(attention_mem, f"probs{n}", [P, 512], F32) for n in range(4)]
            pT_hi = [sb(attention_mem, f"pT_hi{n}", [P, TC, GROUP_HEADS, P], F32R) for n in range(2)]
            pT_lo = [sb(attention_mem, f"pT_lo{n}", [P, TC, GROUP_HEADS, P], F32R) for n in range(2)]
            oT_hi = sb(attention_mem, "oT_hi", [P, DC, P], F32R)
            oT_lo = sb(attention_mem, "oT_lo", [P, DC, P], F32R)
            o_low = sb(attention_mem, "o_low", [HEAD_DIM, 512], F32)
            o_sum = sb(attention_mem, "o_sum", [P, 2, P], F32)
            x2 = sb(attention_mem, "x2", [P, D], F32)
            xn2 = sb(attention_mem, "xn2", [P, D], F32)
            xn2T = sb(attention_mem, "xn2T", [P, DC, P], F32)
            neg_max = sb(attention_mem, "neg_max", [P, H], F32)
            row_sum = sb(attention_mem, "row_sum", [P, H], F32)
            row_inv = sb(attention_mem, "row_inv", [P, H], F32)
            bn1 = sb(attention_mem, "bn1", [P, 2, 6], F32)
            mv1 = sb(attention_mem, "mv1", [P, 2], F32)
            ln1 = sb(attention_mem, "ln1", [P, 8], F32)
            bn2 = sb(attention_mem, "bn2", [P, 2, 6], F32)
            mv2 = sb(attention_mem, "mv2", [P, 2], F32)
            ln2 = sb(attention_mem, "ln2", [P, 8], F32)
            VAR, ROOT, ERR, FIX, SCALE, SHIFT = range(6)
            NEWTON_STEPS = 3
            FACTOR_STEPS = 2 + 3 * NEWTON_STEPS
            ROOT_SEED = float(0x5f3759df)
            logits = sb(attention_mem, "logits", [P, E], F32)
            top_v = sb(attention_mem, "top_v", [P, TOP_K], F32)
            top_i = sb(attention_mem, "top_i", [P, TOP_K], U32)
            top_f = sb(attention_mem, "top_f", [P, TOP_K], F32)
            neg_top = sb(attention_mem, "neg_top", [P, 1], F32)
            top_e = sb(attention_mem, "top_e", [P, TOP_K], F32)
            top_s = sb(attention_mem, "top_s", [P, 1], F32)
            top_inv = sb(attention_mem, "top_inv", [P, 1], F32)
            hot = sb(attention_mem, "hot", [P, TOP_K, E], F32)
            hot_pos = sb(attention_mem, "hot_pos", [P, TOP_K, E], F32)
            chosen = sb(attention_mem, "chosen", [P, E], BF16)
            pos = sb(attention_mem, "pos", [P, E], F32)
            slot_i = sb(attention_mem, "slot_i", [P, TOP_K], I32)
            entry = sb(attention_mem, "entry", [P, TOP_K, 2], I32)

            S_BANK, PT_BANK, O_BANK, MISC = banks[0:2], banks[2:4], banks[4:6], banks[6:8]

            x_in = [sem(f"x_in{s}") for s in range(SC)]
            ctx_loaded = sem("ctx_loaded")
            x2_stored = sem("x2_stored")
            xn2_stored = sem("xn2_stored")
            table_written = sem("table_written")
            ln1_chain, stats1, pool1_chain, ln1_ready = sem("ln1_chain"), sem("stats1"), sem("pool1_chain"), sem("ln1_ready")
            xn_ready, xq_hi_ready, xq_ready, xbias_ready = sem("xn_ready"), sem("xq_hi_ready"), sem("xq_ready"), sem("xbias_ready")
            qt_done, qt_copied = sem("qt_done"), sem("qt_copied")
            vhi_ready, vlo_ready, kt_done = sem("vhi_ready"), sem("vlo_ready"), sem("kt_done")
            kt_copied, kts_copied = sem("kt_copied"), sem("kts_copied")
            scores_done, max_ready, exp_ready, probs_ready = sem("scores_done"), sem("max_ready"), sem("exp_ready"), sem("probs_ready")
            probs_ready_act = sem("probs_ready_act")
            inverse_ready = sem("inverse_ready")
            pt_done, pthi_copied, ptlo_copied = sem("pt_done"), sem("pthi_copied"), sem("ptlo_copied")
            pv_done, olow_copied, osum_ready = sem("pv_done"), sem("olow_copied"), sem("osum_ready")
            othi_ready, otlo_ready = sem("othi_ready"), sem("otlo_ready")
            wo_done, x2_ready, back_chain, stats2 = sem("wo_done"), sem("x2_ready"), sem("back_chain"), sem("stats2")
            ln2_chain = sem("ln2_chain")
            pool2_chain, ln2_ready, xn2_ready = sem("pool2_chain"), sem("ln2_ready"), sem("xn2_ready")
            xt2_done, xt2_copied, router_done, logits_copied = sem("xt2_done"), sem("xt2_copied"), sem("router_done"), sem("logits_copied")
            top_ready, topexp_ready, chosen_ready, rank_done = sem("top_ready"), sem("topexp_ready"), sem("chosen_ready"), sem("rank_done")
            rank_copied, entry_ready = sem("rank_copied"), sem("entry_ready")
            fence = {n: sem(f"fence_{n}") for n in ("dve", "pool")}

            BACK_STEPS = 12
            AHEAD = 3
            ACT_HEADS = (1, 4, 9, 13)
            OUT_SUM = {0: (1, 2), 4: (1, 3), 8: (0, 0), 12: (0, 1)}
            OUT_SPLIT = {h + 1: back_group for h, back_group in OUT_SUM.items()}
            PROJECT = {1: ((0, 0, 2),), 2: ((0, 2, 4),), 3: ((0, 4, 6),), 4: ((1, 0, 2),), 5: ((1, 2, 5),),
                       6: ((0, 6, 8),), 7: ((1, 5, 8),)}
            NEXT_STATS, NEXT_NORM, NEXT_SPLIT, NEXT_QUERIES = (1, 2), 5, 6, (8, 9, 10, 11)
            RESIDUAL, STATS2, NORM2, TRANSPOSE2, ROUTER = (7, 8), (8, 9), 12, (13, 14), 15
            CHOOSE, RANKS, PLACE = (0, 1), 3, (3, 5)
            FIRST_TILE_VALUES, FIRST_TILE_KEYS = {0: 2, 4: 3}, {2: 2, 6: 3}
            LAST_TILE_VALUES, LAST_TILE_KEYS = {8: 0, 12: 1}, {10: 0, 14: 1}

            class Tile:

                def __init__(self, b, s):
                    self.b, self.s, self.i = b, s, b * SC + s
                    known = isinstance(b, int)
                    self.back1 = not (known and self.i < 1)
                    self.back2 = not (known and self.i < 2)
                    self.next = not (known and self.i == TILES - 1)
                    if s < SC - 1:
                        self.next_b, self.next_s = b, s + 1
                    else:
                        self.next_b, self.next_s = b + 1, 0

            def all_tiles(eng, tile):
                for s in range(SC):
                    tile(Tile(0, s))
                with eng.Fori(1, B - 1) as b:
                    for s in range(SC):
                        tile(Tile(b, s))
                for s in range(SC):
                    tile(Tile(B - 1, s))

            def values_and_keys_at(t, h):
                due = []
                if t.s == 0:
                    due += [(t.b, plan[h], plan is FIRST_TILE_VALUES) for plan in (FIRST_TILE_VALUES, FIRST_TILE_KEYS) if h in plan]
                if t.s == SC - 1 and t.next:
                    due += [(t.b + 1, plan[h], plan is LAST_TILE_VALUES) for plan in (LAST_TILE_VALUES, LAST_TILE_KEYS) if h in plan]
                return due

            block = attention_mem.enter_context(nc.Block())

            @block.sync
            def _(sp):
                def store(j):
                    sp.wait_ge(x2_ready, 2 * j + 2)
                    sp.dma_start(out[bass.ds(j * P, P), :], x2[:, :]).then_inc(x2_stored, 16)
                    sp.wait_ge(xn2_ready, j + 1)
                    sp.dma_start(xn_dram[bass.ds(j * P, P), :], xn2[:, :]).then_inc(xn2_stored, 16)

                def load_ctx(b):
                    wait(sp, vlo_ready, G * b)
                    sp.dma_start(ctx_sb[:, :, :], ctx_v[:, bass.ds(b, 1), :, :].rearrange("p b c d -> p (b c) d")
                                 ).then_inc(ctx_loaded, 16)

                def load_x(t):
                    wait(sp, x2_ready, 2 * (t.i - SC) + 2)
                    sp.dma_start(x_t[t.s][:, :], x_rows[bass.ds(t.i * P, P), :]).then_inc(x_in[t.s], 16)

                def tile(t):
                    load_x(t)
                    if t.back2:
                        store(t.i - 2)
                    if t.s == 2 and not (isinstance(t.b, int) and t.b == B - 1):
                        load_ctx(t.b + 1)

                load_ctx(0)
                all_tiles(sp, tile)
                store(TILES - 2)
                store(TILES - 1)
                sp.wait_ge(x2_stored, 16 * TILES)
                sp.wait_ge(xn2_stored, 16 * TILES)

            @block.gpsimd
            def _(pool):
                def hold(semaphore, value):
                    if isinstance(value, int) and value <= 0:
                        return
                    pool.wait_ge(semaphore, value)
                    pool.sem_inc(fence["pool"], 1)

                def factors(f, mv, scale, chain, before, signal):
                    def column(n):
                        return f[:, n:n + 1]
                    count = before

                    def step(instruction):
                        nonlocal count
                        instruction.then_inc(chain, 1)
                        count += 1
                        hold(chain, count)
                    step(pool.tensor_scalar(column(VAR), mv[:, 1:2], EPS, None, ALU.add))
                    step(pool.tensor_scalar(column(ROOT).bitcast(I32), column(VAR).bitcast(I32), -0.5, ROOT_SEED, ALU.mult, ALU.add))
                    for n in range(NEWTON_STEPS):
                        last = n == NEWTON_STEPS - 1
                        step(pool.tensor_scalar(column(ERR), column(ROOT), column(ROOT), column(VAR), ALU.mult, ALU.mult))
                        step(pool.tensor_scalar(column(FIX), column(ERR), -0.5, 1.5, ALU.mult, ALU.add))
                        step(pool.tensor_scalar(column(SCALE if last else ROOT), column(FIX), column(ROOT),
                                                scale if last else None, ALU.mult, *((ALU.mult,) if last else ())))
                    pool.tensor_scalar(column(SHIFT), mv[:, 0:1], column(SCALE), -1.0, ALU.mult, ALU.mult).then_inc(signal, 1)

                def factors1(i):
                    hold(stats1, i + 1)
                    hold(xn_ready, i)
                    factors(ln1, mv1, HEAD_DIM ** -0.5, pool1_chain, FACTOR_STEPS * i, ln1_ready)

                def queries_lo(i, s):
                    hold(xq_hi_ready, i + 1)
                    pool.tensor_tensor(xq[:, :, 1, :], xn[:, :].rearrange("p (h d) -> p h d", d=HEAD_DIM),
                                       xq[:, :, 0, :].bitcast(F32), ALU.subtract).then_inc(xq_ready, 1)
                    pool.tensor_tensor(x_t[s][:, :], x_t[s][:, :], bias_row[:, :], ALU.add).then_inc(xbias_ready, 1)

                def factors2(j):
                    hold(stats2, j + 1)
                    hold(xn2_ready, j)
                    factors(ln2, mv2, 1.0, pool2_chain, FACTOR_STEPS * j, ln2_ready)

                def scatter(j):
                    hold(entry_ready, j + 1)
                    for k in range(TOP_K):
                        pool.indirect_dma_start(
                            out=table, out_offset=bass.IndirectOffsetOnAxis(ap=slot_i[:, k:k + 1], axis=0),
                            in_=entry[:, k, :], in_offset=None, bounds_check=TABLE_ROWS - 1, oob_is_err=True,
                        ).then_inc(table_written, 16)

                def tile(t):
                    if t.next:
                        factors1(t.i + 1)
                        queries_lo(t.i + 1, t.next_s)
                    if t.back1:
                        factors2(t.i - 1)
                    if t.back2:
                        scatter(t.i - 2)

                factors1(0)
                queries_lo(0, 0)
                all_tiles(pool, tile)
                factors2(TILES - 1)
                scatter(TILES - 2)
                scatter(TILES - 1)
                pool.wait_ge(table_written, 16 * TOP_K * TILES)

            @block.scalar
            def _(act):
                def normalise1(i, s):
                    act.wait_ge(ln1_ready, i + 1)
                    wait(act, xq_ready, i)
                    act.activation(xn[:, :], x_t[s][:, :], ACT.Identity, bias=ln1[:, SHIFT:SHIFT + 1], scale=ln1[:, SCALE:SCALE + 1]
                                   ).then_inc(xn_ready, 1)

                def queries_hi(i):
                    act.wait_ge(xn_ready, i + 1)
                    wait(act, qt_done, 4 * i)
                    act.activation(xq[:, :, 0, :], xn[:, :].rearrange("p (h d) -> p h d", d=HEAD_DIM), ACT.Copy
                                   ).then_inc(xq_hi_ready, 1)

                def copy_queries(i, s, n):
                    act.wait_ge(qt_done, 4 * i + n + 1)
                    act.activation(qT[s % 2][:, 4 * n:4 * n + 4, :], MISC[n % 2][:, :].rearrange("p (h t) -> p h t", h=4),
                                   ACT.Copy).then_inc(qt_copied, 1)

                def values_hi(b, g):
                    act.wait_ge(ctx_loaded, 16 * b + 16)
                    wait(act, pv_done, G * (SC * b - 1) + g + 1)
                    act.activation(v[:, :, g, 0, :], ctx_sb[:, :, g * HEAD_DIM:(g + 1) * HEAD_DIM], ACT.Copy
                                   ).then_inc(vhi_ready, 1)

                def copy_keys(b, g):
                    act.wait_ge(kt_done, G * b + g + 1)
                    act.activation(kT[:, g, :], O_BANK[g % 2][:, :], ACT.Copy).then_inc(kt_copied, 1)

                def exponent(i, h):
                    act.wait_ge(max_ready, H * i + h + 1)
                    wait(act, pt_done, H * i + h - 3)
                    act.activation(probs[h % 4][:, :], S_BANK[h % 2][:, :], ACT.Exp, bias=neg_max[:, h:h + 1],
                                   accum_out=row_sum[:, h:h + 1]).then_inc(exp_ready, 1)

                def normalise_probs(i, h):
                    act.wait_ge(inverse_ready, H * i + h + 1)
                    act.activation(probs[h % 4][:, :], probs[h % 4][:, :], ACT.Copy, scale=row_inv[:, h:h + 1]
                                   ).then_inc(probs_ready_act, 1)

                def copy_probs_hi(i, h):
                    g, k = divmod(h, GROUP_HEADS)
                    act.wait_ge(pt_done, H * i + h + 1)
                    if k == 0:
                        wait(act, pv_done, G * i + g - 1)
                    act.activation(pT_hi[g % 2][:, :, k, :], PT_BANK[h % 2][:, :].rearrange("p (c t) -> p c t", c=TC),
                                   ACT.Copy).then_inc(pthi_copied, 1)

                def copy_out_low(i, g):
                    act.wait_ge(pv_done, G * i + g + 1)
                    wait(act, osum_ready, 2 * (G * i + g))
                    act.activation(o_low[:, :], O_BANK[g % 2][HEAD_DIM:P, :], ACT.Copy).then_inc(olow_copied, 1)

                def split_out_hi(i, g):
                    act.wait_ge(osum_ready, 2 * (G * i + g) + 2)
                    if g == 0:
                        wait(act, wo_done, NH * i)
                    act.activation(oT_hi[:, 2 * g:2 * g + 2, :], o_sum[:, :, :], ACT.Copy).then_inc(othi_ready, 1)

                def normalise2(j):
                    act.wait_ge(ln2_ready, j + 1)
                    wait(act, xn2_stored, 16 * j)
                    wait(act, xt2_done, 2 * j)
                    act.activation(xn2[:, :], x2[:, :], ACT.Identity, bias=ln2[:, SHIFT:SHIFT + 1], scale=ln2[:, SCALE:SCALE + 1]
                                   ).then_inc(xn2_ready, 1)

                def copy_xn2(j, n):
                    act.wait_ge(xt2_done, 2 * j + n + 1)
                    if n == 0:
                        wait(act, router_done, j)
                    act.activation(xn2T[:, 4 * n:4 * n + 4, :], MISC[n][:, :].rearrange("p (c t) -> p c t", c=4),
                                   ACT.Copy).then_inc(xt2_copied, 1)

                def top_exponent(j):
                    act.wait_ge(top_ready, j + 1)
                    wait(act, entry_ready, j)
                    act.activation(top_e[:, :], top_v[:, :], ACT.Exp, bias=neg_top[:, :], accum_out=top_s[:, :]
                                   ).then_inc(topexp_ready, 1)

                def tile(t):
                    i = t.i
                    for h in range(H):
                        if h + 1 in ACT_HEADS:
                            normalise_probs(i, h + 1)
                        copy_probs_hi(i, h)
                        if h + AHEAD < H:
                            exponent(i, h + AHEAD)
                        elif t.next:
                            exponent(i + 1, h + AHEAD - H)
                        if h in OUT_SUM and (t.back1 or not OUT_SUM[h][0]):
                            copy_out_low(i - OUT_SUM[h][0], OUT_SUM[h][1])
                        if h in OUT_SPLIT and (t.back1 or not OUT_SPLIT[h][0]):
                            split_out_hi(i - OUT_SPLIT[h][0], OUT_SPLIT[h][1])
                        for b, g, is_values in values_and_keys_at(t, h):
                            if is_values:
                                values_hi(b, g)
                            else:
                                copy_keys(b, g)
                        if h == CHOOSE[0] and t.back2:
                            top_exponent(i - 2)
                        if h == NEXT_NORM and t.next:
                            normalise1(i + 1, t.next_s)
                        if h == NEXT_SPLIT and t.next:
                            queries_hi(i + 1)
                        if h in NEXT_QUERIES and t.next:
                            copy_queries(i + 1, t.next_s, NEXT_QUERIES.index(h))
                        if h == NORM2 and t.back1:
                            normalise2(i - 1)
                        if h in TRANSPOSE2 and t.back1:
                            copy_xn2(i - 1, TRANSPOSE2.index(h))

                values_hi(0, 0)
                values_hi(0, 1)
                normalise1(0, 0)
                queries_hi(0)
                copy_keys(0, 0)
                copy_keys(0, 1)
                for n in range(4):
                    copy_queries(0, 0, n)
                for h in range(AHEAD):
                    exponent(0, h)
                all_tiles(act, tile)
                top_exponent(TILES - 2)
                for g in (G - 2, G - 1):
                    copy_out_low(TILES - 1, g)
                    split_out_hi(TILES - 1, g)
                normalise2(TILES - 1)
                for n in range(2):
                    copy_xn2(TILES - 1, n)
                top_exponent(TILES - 1)

            @block.vector
            def _(dve):
                def statistics(n, sum_chain, before, bn, mv, rows, signal):
                    dve.bn_stats(bn[:, n, :], rows[:, n * HALF:(n + 1) * HALF]).then_inc(sum_chain, 1)
                    if n == 1:
                        dve.wait_ge(sum_chain, before + 2)
                        dve.sem_inc(fence["dve"], 1)
                        dve.bn_aggr(mv[:, :], bn[:, :, :]).then_inc(signal, 1)

                def statistics1(i, s, n):
                    if n == 0:
                        dve.wait_ge(x_in[s], (i - s) * (16 // SC) + 16)
                        wait(dve, ln1_ready, i)
                    statistics(n, ln1_chain, 2 * i, bn1, mv1, x_t[s], stats1)

                def values_lo(b, g):
                    dve.wait_ge(vhi_ready, G * b + g + 1)
                    dve.tensor_tensor(v[:, :, g, 1, :], ctx_sb[:, :, g * HEAD_DIM:(g + 1) * HEAD_DIM],
                                      v[:, :, g, 0, :].bitcast(F32), ALU.subtract).then_inc(vlo_ready, 1)

                def copy_keys_swapped(b, g):
                    dve.wait_ge(kt_copied, G * b + g + 1)
                    for to, at in ((0, HEAD_DIM), (HEAD_DIM, 0)):
                        dve.tensor_copy(kT_swapped[to:to + HEAD_DIM, g, :], O_BANK[g % 2][at:at + HEAD_DIM, :]
                                        ).then_inc(kts_copied, 1)

                def maximum(i, h):
                    dve.wait_ge(scores_done, H * i + h + 1)
                    dve.tensor_reduce(neg_max[:, h:h + 1], S_BANK[h % 2][:, :], AX.X, ALU.max, negate=True
                                      ).then_inc(max_ready, 1)

                def invert(i, h):
                    dve.wait_ge(exp_ready, H * i + h + 1)
                    dve.reciprocal(row_inv[:, h:h + 1], row_sum[:, h:h + 1]).then_inc(inverse_ready, 1)

                def normalise_probs(i, h):
                    if h in ACT_HEADS:
                        return
                    dve.wait_ge(inverse_ready, H * i + h + 1)
                    dve.tensor_scalar(probs[h % 4][:, :], probs[h % 4][:, :], row_inv[:, h:h + 1], None, ALU.mult
                                      ).then_inc(probs_ready, 1)

                def copy_probs_lo(i, h):
                    g, k = divmod(h, GROUP_HEADS)
                    dve.wait_ge(pthi_copied, H * i + h + 1)
                    dve.tensor_tensor(pT_lo[g % 2][:, :, k, :], PT_BANK[h % 2][:, :].rearrange("p (c t) -> p c t", c=TC),
                                      pT_hi[g % 2][:, :, k, :].bitcast(F32), ALU.subtract).then_inc(ptlo_copied, 1)

                def sum_out(i, g):
                    dve.wait_ge(olow_copied, G * i + g + 1)
                    wait(dve, otlo_ready, G * i + g)
                    for r in range(2):
                        hi, low = (o.rearrange("p (a two t) -> p a two t", two=2, t=P)[:, :, r, :]
                                   for o in (O_BANK[g % 2][0:HEAD_DIM, :], o_low[:, :]))
                        dve.tensor_tensor(o_sum[HEAD_DIM * r:HEAD_DIM * (r + 1), :, :], hi, low, ALU.add).then_inc(osum_ready, 1)

                def split_out_lo(i, g):
                    dve.wait_ge(othi_ready, G * i + g + 1)
                    dve.tensor_tensor(oT_lo[:, 2 * g:2 * g + 2, :], o_sum[:, :, :], oT_hi[:, 2 * g:2 * g + 2, :].bitcast(F32),
                                      ALU.subtract).then_inc(otlo_ready, 1)

                def residual(j, n, s):
                    cols = slice(n * HALF, (n + 1) * HALF)
                    dve.wait_ge(wo_done, NH * j + n + 1)
                    if n == 0:
                        dve.wait_ge(xbias_ready, j + 1)
                        wait(dve, x2_stored, 16 * j)
                        wait(dve, xn2_ready, j)
                    dve.tensor_tensor(x2[:, cols], MISC[n][:, :], x_t[s][:, cols], ALU.add).then_inc(x2_ready, 1)

                def statistics2(j, n):
                    if n == 0:
                        wait(dve, ln2_ready, j)
                    dve.wait_ge(x2_ready, 2 * j + n + 1)
                    statistics(n, ln2_chain, 2 * j, bn2, mv2, x2, stats2)

                def copy_logits(j):
                    dve.wait_ge(router_done, j + 1)
                    dve.tensor_copy(logits[:, :], MISC[0][:, 0:E]).then_inc(logits_copied, 1)

                def choose(j):
                    chain = Chain(dve, back_chain, BACK_STEPS * j)
                    dve.wait_ge(logits_copied, j + 1)
                    dve.sem_inc(fence["dve"], 1)
                    chain.then(dve.max(top_v[:, :], logits[:, :]))
                    dve.tensor_scalar(neg_top[:, :], top_v[:, 0:1], -1.0, None, ALU.mult).then_inc(top_ready, 1)
                    chain.then(dve.max_index(top_i[:, :], top_v[:, :], logits[:, :]))
                    chain.then(dve.tensor_copy(top_f[:, :], top_i[:, :]))
                    assert chain.n == 3

                def mark(j):
                    chain = Chain(dve, back_chain, BACK_STEPS * j + 3)
                    chain.then(dve.tensor_tensor(hot[:, :, :], top_f[:, :].unsqueeze(2).to_broadcast([P, TOP_K, E]),
                                                 iota_e[:, :].unsqueeze(1).to_broadcast([P, TOP_K, E]), ALU.is_equal))
                    with nc.allow_low_precision(reason="a sum of one 1 at most"):
                        dve.tensor_reduce(chosen[:, :], hot[:, :, :].rearrange("p k e -> p e k"), AX.X, ALU.add
                                          ).then_inc(chosen_ready, 1)
                    assert chain.n == 1

                def place(j):
                    chain = Chain(dve, back_chain, BACK_STEPS * j + 4)
                    dve.wait_ge(rank_done, j + 1)
                    chain.then(dve.tensor_tensor(pos[:, :], MISC[1][:, 0:E], slot_base[:, :], ALU.add))
                    chain.then(dve.tensor_tensor(slot_base[:, :], MISC[1][:, E:2 * E], slot_base[:, :], ALU.add))
                    dve.sem_inc(rank_copied, 1)
                    chain.then(dve.tensor_tensor(hot_pos[:, :, :], hot[:, :, :],
                                                 pos[:, :].unsqueeze(1).to_broadcast([P, TOP_K, E]), ALU.mult))
                    wait(dve, table_written, 16 * TOP_K * j)
                    with nc.allow_low_precision(reason="one whole number below 2 ** 24 and zeros, summed in float32"):
                        chain.then(dve.tensor_reduce(slot_i[:, :], hot_pos[:, :, :], AX.X, ALU.add))
                    assert chain.n == 4

                def enter(j):
                    chain = Chain(dve, back_chain, BACK_STEPS * j + 8)
                    chain.then(dve.tensor_copy(entry[:, :, 0], token_id[:, :].to_broadcast([P, TOP_K])))
                    chain.then(dve.tensor_scalar(token_id[:, :], token_id[:, :], float(P), None, ALU.add))
                    dve.wait_ge(topexp_ready, j + 1)
                    chain.then(dve.reciprocal(top_inv[:, :], top_s[:, :]))
                    chain.then(dve.tensor_scalar(entry[:, :, 1].bitcast(F32), top_e[:, :], top_inv[:, :], None, ALU.mult))
                    dve.sem_inc(entry_ready, 1)
                    assert chain.n == 4

                def tile(t):
                    i = t.i
                    for h in range(H):
                        if h == CHOOSE[0] and t.back2:
                            copy_logits(i - 2)
                        if h + AHEAD < H:
                            maximum(i, h + AHEAD)
                        elif t.next:
                            maximum(i + 1, h + AHEAD - H)
                        if h + 2 < H:
                            invert(i, h + 2)
                        elif t.next:
                            invert(i + 1, h + 2 - H)
                        if h + 1 < H:
                            normalise_probs(i, h + 1)
                        elif t.next:
                            normalise_probs(i + 1, 0)
                        if t.back2:
                            if h == CHOOSE[0]:
                                choose(i - 2)
                            if h == CHOOSE[1]:
                                mark(i - 2)
                        copy_probs_lo(i, h)
                        if h in OUT_SUM and (t.back1 or not OUT_SUM[h][0]):
                            sum_out(i - OUT_SUM[h][0], OUT_SUM[h][1])
                        if h in OUT_SPLIT and (t.back1 or not OUT_SPLIT[h][0]):
                            split_out_lo(i - OUT_SPLIT[h][0], OUT_SPLIT[h][1])
                        for b, g, is_values in values_and_keys_at(t, h):
                            if is_values:
                                values_lo(b, g)
                            else:
                                copy_keys_swapped(b, g)
                        if t.back2:
                            if h == PLACE[0]:
                                place(i - 2)
                            if h == PLACE[1]:
                                enter(i - 2)
                        if h in NEXT_STATS and t.next:
                            statistics1(i + 1, t.next_s, NEXT_STATS.index(h))
                        if t.back1 and h in RESIDUAL:
                            residual(i - 1, RESIDUAL.index(h), (t.s - 1) % SC)
                        if t.back1 and h in STATS2:
                            statistics2(i - 1, STATS2.index(h))

                for n in range(2):
                    statistics1(0, 0, n)
                values_lo(0, 0)
                values_lo(0, 1)
                copy_keys_swapped(0, 0)
                copy_keys_swapped(0, 1)
                for h in range(AHEAD):
                    maximum(0, h)
                invert(0, 0)
                invert(0, 1)
                normalise_probs(0, 0)
                all_tiles(dve, tile)
                for step in (copy_logits, choose, mark, place, enter):
                    step(TILES - 2)
                for g in (G - 2, G - 1):
                    sum_out(TILES - 1, g)
                    split_out_lo(TILES - 1, g)
                for n in range(2):
                    residual(TILES - 1, n, SC - 1)
                for n in range(2):
                    statistics2(TILES - 1, n)
                for step in (copy_logits, choose, mark, place, enter):
                    step(TILES - 1)

            @block.tensor
            def _(pe):
                def transpose_queries(i, n):
                    pe.wait_ge(xq_ready, i + 1)
                    if n >= 2:
                        pe.wait_ge(qt_copied, 4 * i + n - 1)
                    elif isinstance(i, int) and i == 1:
                        pe.wait_ge(qt_copied, n + 3)
                    else:
                        wait(pe, x2_ready, 2 * (i - 2) + n + 1)
                    for k in range(4):
                        last = nc.tensor.transpose(MISC[n % 2][:, k * P:(k + 1) * P].bitcast(F32R),
                                                   xq[:, 4 * n + k, :, :].rearrange("p two d -> p (two d)"), ident_r[:, :])
                    last.then_inc(qt_done, 1)

                def transpose_keys(b, g):
                    pe.wait_ge(vlo_ready, G * b + g + 1)
                    wait(pe, osum_ready, 2 * (G * (SC * b - 1) + g + 1))
                    for c in range(TC):
                        last = nc.tensor.transpose(O_BANK[g % 2][:, c * P:(c + 1) * P].bitcast(F32R),
                                                   v[:, c, g, :, :].rearrange("p two d -> p (two d)"), ident_r[:, :])
                    last.then_inc(kt_done, 1)

                def scores(b, s, i, h):
                    g = h // GROUP_HEADS
                    if h % 4 == 0:
                        pe.wait_ge(qt_copied, 4 * i + h // 4 + 1)
                    if h % 4 == 0 and s == 0:
                        pe.wait_ge(kt_copied, G * b + g + 1)
                        pe.wait_ge(kts_copied, 2 * (G * b + g + 1))
                    wait(pe, exp_ready, H * i + h - 1)
                    nc.tensor.matmul(S_BANK[h % 2][:, :], qT[s % 2][:, h, :], kT[:, g, :], start=True, stop=False)
                    nc.tensor.matmul(S_BANK[h % 2][:, :], qT[s % 2][:, h, :], kT_swapped[:, g, :], start=False, stop=True
                                     ).then_inc(scores_done, 1)

                def transpose_probs(i, h):
                    if h in ACT_HEADS:
                        pe.wait_ge(probs_ready_act, len(ACT_HEADS) * i + ACT_HEADS.index(h) + 1)
                    else:
                        before = sum(k not in ACT_HEADS for k in range(h))
                        pe.wait_ge(probs_ready, (H - len(ACT_HEADS)) * i + before + 1)
                    wait(pe, ptlo_copied, H * i + h - 1)
                    for c in range(TC):
                        last = nc.tensor.transpose(PT_BANK[h % 2][:, c * P:(c + 1) * P], probs[h % 4][:, c * P:(c + 1) * P],
                                                   ident[:, :])
                    last.then_inc(pt_done, 1)

                def values(b, s, i, g, cs):
                    if cs[0] == 0:
                        pe.wait_ge(ptlo_copied, H * i + GROUP_HEADS * (g + 1))
                        wait(pe, osum_ready, 2 * (G * i + g - 1))
                        keys = None
                        if s == 0 and g < 2:
                            keys = G * b + g + 3
                        elif s == SC - 1 and g >= 2 and not (isinstance(b, int) and b == B - 1):
                            keys = G * (b + 1) + g - 1
                        if keys is not None:
                            pe.wait_ge(kt_copied, keys)
                            pe.wait_ge(kts_copied, 2 * keys)
                    for c in cs:
                        for p in (pT_hi, pT_lo):
                            last = nc.tensor.matmul(O_BANK[g % 2][:, :], v[:, c, g, :, :].rearrange("p two d -> p (two d)"),
                                                    p[g % 2][:, c, :, :].rearrange("p h t -> p (h t)"),
                                                    start=(c == 0 and p is pT_hi), stop=(c == TC - 1 and p is pT_lo))
                    if cs[-1] == TC - 1:
                        last.then_inc(pv_done, 1)

                def project(j, n, cs):
                    if cs[0] == 0:
                        if not (isinstance(j, int) and j == TILES - 1):
                            pe.wait_ge(qt_copied, 4 * (j + 1) + 3 + n)
                        wait(pe, (logits_copied, rank_copied)[n], j)
                    for c in cs:
                        if c % 2 == 0:
                            pe.wait_ge(otlo_ready, G * j + c // 2 + 1)
                        for o, w in ((oT_hi, WcT_hi), (oT_hi, WcT_lo), (oT_lo, WcT_hi)):
                            last = nc.tensor.matmul(MISC[n][:, :], o[:, c, :], w[:, c, n * HALF:(n + 1) * HALF],
                                                    start=(c == 0 and w is WcT_hi and o is oT_hi),
                                                    stop=(c == DC - 1 and o is oT_lo))
                    if cs[-1] == DC - 1:
                        last.then_inc(wo_done, 1)

                def transpose_xn2(j, n):
                    pe.wait_ge(xn2_ready, j + 1)
                    if not (isinstance(j, int) and j >= TILES - 2):
                        pe.wait_ge(qt_copied, 4 * (j + 2) + 3 + n)
                    for k in range(4):
                        c = 4 * n + k
                        last = nc.tensor.transpose(MISC[n][:, k * P:(k + 1) * P], xn2[:, c * P:(c + 1) * P], ident[:, :])
                    last.then_inc(xt2_done, 1)

                def router(j):
                    pe.wait_ge(xt2_copied, 2 * j + 2)
                    for c in range(DC):
                        last = nc.tensor.matmul(MISC[0][:, 0:E], xn2T[:, c, :], gate_sb[:, c, :], start=(c == 0), stop=(c == DC - 1))
                    last.then_inc(router_done, 1)

                def ranks(j):
                    pe.wait_ge(chosen_ready, j + 1)
                    nc.tensor.matmul(MISC[1][:, 0:E], before_bf[:, :], chosen[:, :], start=True, stop=True)
                    nc.tensor.matmul(MISC[1][:, E:2 * E], ones_bf[:, :], chosen[:, :], start=True, stop=True
                                     ).then_inc(rank_done, 1)

                def tile(t):
                    i = t.i
                    for h in range(H):
                        if h + AHEAD < H:
                            scores(t.b, t.s, i, h + AHEAD)
                        elif t.next:
                            scores(t.next_b, t.next_s, i + 1, h + AHEAD - H)
                        transpose_probs(i, h)
                        if h >= 4:
                            values(t.b, t.s, i, h // 4 - 1, (h % 4,))
                        elif t.back1:
                            last_b, last_s = (t.b, t.s - 1) if t.s else (t.b - 1, SC - 1)
                            values(last_b, last_s, i - 1, G - 1, (h,))
                        for b, g, is_values in values_and_keys_at(t, h):
                            if not is_values:
                                transpose_keys(b, g)
                        if h == RANKS and t.back2:
                            ranks(i - 2)
                        if t.back1:
                            for n, c0, c1 in PROJECT.get(h, ()):
                                project(i - 1, n, list(range(c0, c1)))
                        if h in NEXT_QUERIES and t.next:
                            transpose_queries(i + 1, NEXT_QUERIES.index(h))
                        if h in TRANSPOSE2 and t.back1:
                            transpose_xn2(i - 1, TRANSPOSE2.index(h))
                        if h == ROUTER and t.back1:
                            router(i - 1)

                transpose_keys(0, 0)
                transpose_keys(0, 1)
                for n in range(4):
                    transpose_queries(0, n)
                for h in range(AHEAD):
                    scores(0, 0, 0, h)
                all_tiles(pe, tile)
                ranks(TILES - 2)
                values(B - 1, SC - 1, TILES - 1, G - 1, range(TC))
                for n in range(NH):
                    project(TILES - 1, n, list(range(DC)))
                for n in range(2):
                    transpose_xn2(TILES - 1, n)
                router(TILES - 1)
                ranks(TILES - 1)

        sched_row = sb(top, "sched_row", [1, SCHED * 4], I32)
        tiles_used = sb(top, "tiles_used", [P, 1], I32)
        schedule_stage(nc, sb, sem, slot_base, expert_base, sched_dram, sched_row, tiles_used, T=T, E=E,
                       SCHED_COLS=SCHED_COLS, TABLE_PAD=TABLE_PAD)
        experts_stage(nc, sb, sem, banks, sched_row, tiles_used, xn_dram, table, gate_proj, up_proj, down_v, out,
                      T=T, D=D, DC=DC, M=M, MC=MC, E=E, TABLE_PAD=TABLE_PAD, MOST_TILES=MOST_TILES)


def setup_stage(nc, sb, sem, banks, Wc, bc, gate_w, xn_dram, table, out, ident, ident_r, before_bf, ones_bf, gate_sb,
                bias_row, iota_e, token_id, slot_base, expert_base, WcT_hi, WcT_lo, *, D, DC, E, T, TABLE_ROWS):
    ROWS = TABLE_ROWS // P
    assert ROWS * P == TABLE_ROWS and T % SLOT_ROWS == 0
    mem = ExitStack()
    with mem:
        Wc_sb = sb(mem, "Wc_sb", [P, DC, D], F32)
        row_i = sb(mem, "row_i", [P, ROWS], I32)
        row_m = sb(mem, "row_m", [P, ROWS], I32)
        empty = sb(mem, "empty", [P, ROWS, 2], I32)
        zeros = sb(mem, "zeros", [P, D], F32)
        before_f = sb(mem, "before_f", [P, P], F32)
        wc_loaded, small_loaded, stored = sem("wc_loaded"), sem("small_loaded"), sem("setup_stored")
        made, ident_made, ident_r_made, empty_made = sem("made"), sem("ident_made"), sem("ident_r_made"), sem("empty_made")
        wct_done, wct_hi, wct_lo = sem("wct_done"), sem("wct_hi"), sem("wct_lo")
        block = mem.enter_context(nc.Block())
        GROUPS = [(c, n) for c in range(DC) for n in range(DC // 4)]

        @block.sync
        def _(sp):
            sp.dma_start(Wc_sb[:, :, :], Wc.rearrange("(n p) c -> p n c", p=P)).then_inc(wc_loaded, 16)
            sp.dma_start(gate_sb[:, :, :], gate_w.rearrange("(c p) e -> p c e", p=P)).then_inc(small_loaded, 16)
            sp.dma_start(bias_row[:, :], bc.unsqueeze(0).to_broadcast([P, D])).then_inc(small_loaded, 16)
            sp.wait_ge(empty_made, 2)
            sp.dma_start(table.rearrange("(p r) two -> p (r two)", p=P), empty[:, :, :].rearrange("p r two -> p (r two)")
                         ).then_inc(stored, 16)
            for rows in (xn_dram[T:T + SLOT_ROWS, :], out[T:T + SLOT_ROWS, :]):
                for q in range(SLOT_ROWS // P):
                    sp.dma_start(rows[q * P:(q + 1) * P, :], zeros[:, :]).then_inc(stored, 16)
            sp.wait_ge(small_loaded, 32)
            sp.wait_ge(stored, 16 * (1 + 2 * SLOT_ROWS // P))

        @block.gpsimd
        def _(pool):
            pool.memset(ident[:, :], 0.0).then_inc(made, 1)
            pool.memset(before_f[:, :], 1.0).then_inc(made, 1)
            pool.wait_ge(made, 2)
            pool.affine_select(out=ident[:, :], in_=ident[:, :], compare_op=ALU.not_equal, fill=1.0, base=0,
                               pattern=[[-1, P]], channel_multiplier=1).then_inc(ident_made, 1)
            pool.affine_select(out=before_f[:, :], in_=before_f[:, :], compare_op=ALU.is_gt, fill=0.0, base=0,
                               pattern=[[1, P]], channel_multiplier=-1).then_inc(made, 1)
            pool.memset(ones_bf[:, :], 1.0)
            pool.iota(iota_e[:, :], [[1, E]], base=0, channel_multiplier=0, allow_small_or_imprecise_dtypes=True)
            pool.iota(token_id[:, :], [[0, 1]], base=0, channel_multiplier=1, allow_small_or_imprecise_dtypes=True)
            pool.iota(slot_base[:, :], [[T, E]], base=0, channel_multiplier=0, allow_small_or_imprecise_dtypes=True)
            pool.iota(expert_base[:, :], [[T, E]], base=0, channel_multiplier=0, allow_small_or_imprecise_dtypes=True)
            pool.iota(row_i[:, :], [[1, ROWS]], base=0, channel_multiplier=ROWS % SLOT_ROWS).then_inc(made, 1)
            pool.wait_ge(made, 4)
            pool.tensor_copy(before_bf[:, :], before_f[:, :])

        @block.vector
        def _(dve):
            dve.memset(zeros[:, :], 0.0).then_inc(empty_made, 1)
            dve.memset(empty[:, :, 1], 0)
            dve.wait_ge(ident_made, 1)
            dve.tensor_copy(ident_r[:, :], ident[:, :]).then_inc(ident_r_made, 1)
            dve.wait_ge(made, 4)
            dve.tensor_single_scalar(row_m[:, :], row_i[:, :], SLOT_ROWS - 1, ALU.bitwise_and).then_inc(ident_r_made, 1)
            dve.wait_ge(ident_r_made, 2)
            dve.tensor_scalar(empty[:, :, 0], row_m[:, :], float(T), None, ALU.add).then_inc(empty_made, 1)
            for k, (c, n) in enumerate(GROUPS):
                dve.wait_ge(wct_hi, k + 1)
                dve.tensor_tensor(WcT_lo[:, c, n * 512:(n + 1) * 512], banks[k % 2][:, :],
                                  WcT_hi[:, c, n * 512:(n + 1) * 512].bitcast(F32), ALU.subtract).then_inc(wct_lo, 1)

        @block.scalar
        def _(act):
            for k, (c, n) in enumerate(GROUPS):
                act.wait_ge(wct_done, k + 1)
                act.activation(WcT_hi[:, c, n * 512:(n + 1) * 512], banks[k % 2][:, :], ACT.Copy).then_inc(wct_hi, 1)

        @block.tensor
        def _(pe):
            pe.wait_ge(ident_made, 1)
            pe.wait_ge(wc_loaded, 16)
            for k, (c, n) in enumerate(GROUPS):
                if k >= 2:
                    pe.wait_ge(wct_lo, k - 1)
                for m in range(4):
                    last = nc.tensor.transpose(banks[k % 2][:, m * P:(m + 1) * P], Wc_sb[:, 4 * n + m, c * P:(c + 1) * P],
                                               ident[:, :])
                last.then_inc(wct_done, 1)


def schedule_stage(nc, sb, sem, slot_base, expert_base, sched_dram, sched_row, tiles_used, *, T, E, SCHED_COLS, TABLE_PAD):
    SIZES = T // SLOT_ROWS
    mem = ExitStack()
    with mem:
        steps = sb(mem, "steps", [P, SIZES], F32)
        upto = sb(mem, "upto", [P, E, E], F32)
        tile_no = sb(mem, "tile_no", [P, 2, SCHED_COLS], F32)
        count = sb(mem, "count", [P, E], F32)
        more = sb(mem, "more", [P, E, SIZES], F32)
        tiles = sb(mem, "tiles", [P, E], F32)
        part = sb(mem, "part", [P, E, E], F32)
        ends = sb(mem, "ends", [P, E], F32)
        passed = sb(mem, "passed", [P, 2 * SCHED_COLS, E], F32)
        expert = sb(mem, "expert", [P, 2, SCHED_COLS], F32)
        taken = sb(mem, "taken", [P, SCHED_COLS, E], F32)
        first = sb(mem, "first", [P, SCHED_COLS], F32)
        offset = sb(mem, "offset", [P, SCHED_COLS], F32)
        offset2 = sb(mem, "offset2", [P, SCHED_COLS], F32)
        clamped = sb(mem, "clamped", [P, 2, SCHED_COLS], F32)
        expert_no = sb(mem, "expert_no", [P, E], F32)
        own = sb(mem, "own", [P, SCHED_COLS, E], F32)
        own_count = sb(mem, "own_count", [P, SCHED_COLS, E], F32)
        rows = sb(mem, "rows", [P, SCHED_COLS], F32)
        left = sb(mem, "left", [P, SCHED_COLS], F32)
        fits_short = sb(mem, "fits_short", [P, SCHED_COLS], F32)
        fits_half = sb(mem, "fits_half", [P, SCHED_COLS], F32)
        sched = sb(mem, "sched", [P, SCHED_COLS, 4], I32)
        consts, chain_sem, ready, stored = sem("sched_consts"), sem("sched_chain"), sem("sched_ready"), sem("sched_stored")
        block = mem.enter_context(nc.Block())

        @block.gpsimd
        def _(pool):
            pool.iota(steps[:, :], [[SLOT_ROWS, SIZES]], base=0, channel_multiplier=0,
                      allow_small_or_imprecise_dtypes=True).then_inc(consts, 1)
            pool.iota(tile_no[:, :, :], [[-1, 2], [P, SCHED_COLS]], base=0, channel_multiplier=1,
                      allow_small_or_imprecise_dtypes=True).then_inc(consts, 1)
            pool.iota(expert_no[:, :], [[1, E]], base=0, channel_multiplier=0,
                      allow_small_or_imprecise_dtypes=True).then_inc(consts, 1)
            pool.memset(upto[:, :, :], 1.0).then_inc(consts, 1)
            pool.wait_ge(consts, 4)
            pool.affine_select(out=upto[:, :, :], in_=upto[:, :, :], compare_op=ALU.is_ge, fill=0.0, base=0,
                               pattern=[[1, E], [-1, E]], channel_multiplier=0).then_inc(consts, 1)

        @block.vector
        def _(dve):
            chain = Chain(dve, chain_sem, 0)
            do = chain.then
            do(dve.tensor_tensor(count[:, :], slot_base[:, :], expert_base[:, :], ALU.subtract))
            dve.wait_ge(consts, 5)
            do(dve.tensor_tensor(more[:, :, :], count[:, :].unsqueeze(2).to_broadcast([P, E, SIZES]),
                                 steps[:, :].unsqueeze(1).to_broadcast([P, E, SIZES]), ALU.is_gt))
            do(dve.tensor_reduce(tiles[:, :], more[:, :, :], AX.X, ALU.add))
            do(dve.tensor_tensor(part[:, :, :], upto[:, :, :], tiles[:, :].unsqueeze(1).to_broadcast([P, E, E]), ALU.mult))
            do(dve.tensor_reduce(ends[:, :], part[:, :, :], AX.X, ALU.add))
            do(dve.tensor_copy(tiles_used[:, :], ends[:, E - 1:E]))
            do(dve.tensor_tensor(passed[:, :, :],
                                 tile_no[:, :, :].rearrange("p a c -> p (a c)").unsqueeze(2).to_broadcast([P, 2 * SCHED_COLS, E]),
                                 ends[:, :].unsqueeze(1).to_broadcast([P, 2 * SCHED_COLS, E]), ALU.is_ge))
            do(dve.tensor_reduce(expert[:, :, :].rearrange("p a c -> p (a c)"), passed[:, :, :], AX.X, ALU.add))
            do(dve.tensor_tensor(taken[:, :, :], passed[:, 0:SCHED_COLS, :],
                                 tiles[:, :].unsqueeze(1).to_broadcast([P, SCHED_COLS, E]), ALU.mult))
            do(dve.tensor_reduce(first[:, :], taken[:, :, :], AX.X, ALU.add))
            do(dve.tensor_tensor(offset[:, :], tile_no[:, 0, :], first[:, :], ALU.subtract))
            do(dve.tensor_scalar(offset2[:, :], offset[:, :], float(SLOT_ROWS), None, ALU.mult))
            do(dve.scalar_tensor_tensor(out=offset[:, :], in0=expert[:, 0, :], scalar=float(T), in1=offset2[:, :],
                                        op0=ALU.mult, op1=ALU.add))
            do(dve.tensor_tensor(own[:, :, :], expert[:, 0, :].unsqueeze(2).to_broadcast([P, SCHED_COLS, E]),
                                 expert_no[:, :].unsqueeze(1).to_broadcast([P, SCHED_COLS, E]), ALU.is_equal))
            do(dve.tensor_tensor(own_count[:, :, :], own[:, :, :],
                                 count[:, :].unsqueeze(1).to_broadcast([P, SCHED_COLS, E]), ALU.mult))
            do(dve.tensor_reduce(rows[:, :], own_count[:, :, :], AX.X, ALU.add))
            do(dve.tensor_tensor(left[:, :], rows[:, :], offset2[:, :], ALU.subtract))
            do(dve.tensor_scalar(fits_short[:, :], left[:, :], float(SHORT), None, ALU.is_le))
            do(dve.tensor_scalar(fits_half[:, :], left[:, :], float(HALF_TILE), None, ALU.is_le))
            do(dve.tensor_tensor(sched[:, :, 3], fits_short[:, :], fits_half[:, :], ALU.add))
            do(dve.tensor_scalar(sched[:, :, 0], offset[:, :], float(TABLE_PAD), None, ALU.min))
            do(dve.tensor_scalar(clamped[:, :, :], expert[:, :, :], float(E - 1), None, ALU.min))
            do(dve.tensor_copy(sched[:, :, 1], clamped[:, 0, :]))
            do(dve.tensor_tensor(sched[:, :, 2], clamped[:, 0, :], clamped[:, 1, :], ALU.not_equal))
            dve.sem_inc(ready, 1)

        @block.sync
        def _(sp):
            sp.wait_ge(ready, 1)
            sp.dma_start(sched_dram.rearrange("(c p) k -> p c k", p=P), sched[:, :, :]).then_inc(stored, 16)
            sp.wait_ge(stored, 16)
            sp.dma_start(sched_row[:, :], sched_dram.rearrange("t k -> (t k)").unsqueeze(0)).then_inc(stored, 16)
            sp.wait_ge(stored, 32)


def experts_stage(nc, sb, sem, banks, sched_row, tiles_used, xn_dram, table, gate_proj, up_proj, down_v, out, *,
                  T, D, DC, M, MC, E, TABLE_PAD, MOST_TILES):
    Q = SLOT_ROWS // P
    NH = D // 512
    OUT_GROUPS = Q * NH
    QUAD = 32
    KQ = P // QUAD
    RUNS = SLOT_ROWS // QUAD
    QUARTER_ROW = D // KQ
    assert QUARTER_ROW == DC * QUAD
    quarter_rows = xn_dram.rearrange("t (k d) -> (t k) d", k=KQ)
    weights_v = [w.rearrange("e (k c r) m -> e k r c m", k=KQ, r=QUAD) for w in (gate_proj, up_proj)]

    mem = ExitStack()
    with mem:
        gu_raw = sb(mem, "gu_raw", [P, 2, DC, M], F32)
        d_raw = sb(mem, "d_raw", [P, MC, D], F32)
        gu_hi = sb(mem, "gu_hi", [P, DC, 2, M], F32R)
        gu_lo = sb(mem, "gu_lo", [P, DC, 2, M], F32R)
        d_hi = sb(mem, "d_hi", [P, MC, D], F32R)
        d_lo = sb(mem, "d_lo", [P, MC, D], F32R)
        xg = sb(mem, "xg", [P, RUNS, QUARTER_ROW], F32)
        xT = sb(mem, "xT", [P, DC, SLOT_ROWS], F32)
        xT_hi = sb(mem, "xT_hi", [P, DC, SLOT_ROWS], F32R)
        xT_lo = sb(mem, "xT_lo", [P, DC, SLOT_ROWS], F32R)
        gated = [sb(mem, f"gated{n}", [P, SLOT_ROWS], F32) for n in range(2)]
        h = sb(mem, "h", [P, SLOT_ROWS], F32)
        h_hi = sb(mem, "h_hi", [P, MC, SLOT_ROWS], F32R)
        h_lo = sb(mem, "h_lo", [P, MC, SLOT_ROWS], F32R)
        rows_out = sb(mem, "rows_out", [P, Q, D], F32)
        entry_in = sb(mem, "entry_in", [P, RUNS, 2], I32)
        entry_next = sb(mem, "entry_next", [P, RUNS, 2], I32)
        entry_now = sb(mem, "entry_now", [P, Q, 2], I32)
        quarter_no = sb(mem, "quarter_no", [P, 1], F32)
        gather_row = sb(mem, "gather_row", [P, RUNS], I32)
        GU_BANK, D_BANK = banks[0:6], banks[6:8]
        ROWS_AFTER = (0, 2, 5)

        gu_loaded, d_loaded, entry_loaded = sem("gu_loaded"), sem("d_loaded"), sem("entry_loaded")
        gathered, scattered = sem("gathered"), sem("scattered")
        quarter_made, rows_made, entry_taken, entry_kept = sem("quarter_made"), sem("rows_made"), sem("entry_taken"), sem("entry_kept")
        xt_ready, xt_hi, xt_lo = sem("xt_ready"), sem("xt_hi"), sem("xt_lo")
        guhi_ready, gulo_ready, dhi_ready, dlo_ready = sem("guhi_ready"), sem("gulo_ready"), sem("dhi_ready"), sem("dlo_ready")
        gu_done, silu_ready, h_ready, hhi_ready, hlo_ready = sem("gu_done"), sem("silu_ready"), sem("h_ready"), sem("hhi_ready"), sem("hlo_ready")
        down_done, left_ready, right_ready = sem("down_done"), sem("left_ready"), sem("right_ready")
        fence = {n: sem(f"fence2_{n}") for n in ("pool", "sp")}

        def all_tiles(eng, tile):
            used = eng.value_load(tiles_used[0:1, 0:1], min_val=1, max_val=MOST_TILES)
            tile(0)
            with eng.Fori(1, MOST_TILES) as t:
                with eng.If(t < used):
                    tile(t)

        block = mem.enter_context(nc.Block())

        @block.sync
        def _(sp):
            def hold(semaphore, value):
                sp.wait_ge(semaphore, value)
                sp.sem_inc(fence["sp"], 1)

            def load_entries(t):
                first_row = sp.value_load(sched_row[0:1, bass.ds(4 * t, 1)], min_val=0, max_val=TABLE_PAD)
                wait(sp, entry_taken, t)
                for k in range(KQ):
                    sp.dma_start(entry_in[k * QUAD:(k + 1) * QUAD, :, :].rearrange("r (q m) two -> r q (m two)", q=Q),
                                 table[bass.ds(first_row, SLOT_ROWS), :].rearrange("(q r m) two -> r q (m two)", q=Q, r=QUAD)
                                 ).then_inc(entry_loaded, 16)

            def load_weights(t):
                e = sp.value_load(sched_row[0:1, bass.ds(4 * t + 1, 1)], min_val=0, max_val=E - 1)
                first = isinstance(t, int) and t == 0
                only = {} if first else {"cond": sp.value_load(sched_row[0:1, bass.ds(4 * t + 2, 1)], min_val=0, max_val=1)}
                wait(sp, gulo_ready, MC * t)
                for n, w in enumerate(weights_v):
                    for k in range(KQ):
                        sp.dma_start(gu_raw[k * QUAD:(k + 1) * QUAD, n, :, :],
                                     w[bass.ds(e, 1), k, :, :, :].rearrange("e r c m -> r (e c) m"), **only
                                     ).then_inc(gu_loaded, 16)
                wait(sp, dlo_ready, MC * t)
                sp.dma_start(d_raw[:, :, :], down_v[bass.ds(e, 1), :, :, :].rearrange("e p c d -> p (e c) d"), **only
                             ).then_inc(d_loaded, 16)

            def tile(t):
                load_entries(t + 2)
                load_weights(t + 1)
                hold(d_loaded, 16 * (t + 2))

            load_entries(0)
            load_weights(0)
            load_entries(1)
            all_tiles(sp, tile)

        @block.gpsimd
        def _(pool):
            def hold(semaphore, value):
                if isinstance(value, int) and value <= 0:
                    return
                pool.wait_ge(semaphore, value)
                pool.sem_inc(fence["pool"], 1)

            def gather(t):
                hold(entry_loaded, 16 * KQ * (t + 1))
                pool.tensor_scalar(gather_row[:, :], entry_in[:, :, 0], float(KQ), quarter_no[:, :], ALU.mult, ALU.add
                                   ).then_inc(rows_made, 1)
                hold(rows_made, t + 1)
                hold(xt_ready, DC * t)
                for m in range(RUNS):
                    pool.indirect_dma_start(
                        out=xg[:, m, :], out_offset=None, in_=quarter_rows,
                        in_offset=bass.IndirectOffsetOnAxis(ap=gather_row[:, m:m + 1], axis=0),
                        bounds_check=KQ * (T + SLOT_ROWS) - 1, oob_is_err=True).then_inc(gathered, 16)

            def keep(t):
                pool.tensor_copy(entry_next[:, :, :], entry_in[:, :, :]).then_inc(entry_taken, 1)
                hold(entry_taken, t + 1)

            def tile(t):
                for k in range(KQ):
                    quad = slice(k * QUAD, (k + 1) * QUAD)
                    pool.tensor_copy(entry_now[quad, :, :],
                                     entry_next[quad, :, :].rearrange("r (q k) two -> r q k two", k=KQ)[:, :, k, :]
                                     ).then_inc(entry_kept, 1)
                hold(entry_kept, KQ * (t + 1))
                keep(t + 1)
                gather(t + 2)
                for q in range(Q):
                    hold(left_ready, Q * t + q + 1)
                    hold(right_ready, Q * t + q + 1)
                    pool.indirect_dma_start(
                        out=out, out_offset=bass.IndirectOffsetOnAxis(ap=entry_now[:, q, 0:1], axis=0),
                        in_=rows_out[:, q, :], in_offset=None, bounds_check=T + SLOT_ROWS - 1, oob_is_err=True,
                        compute_op=ALU.add).then_inc(scattered, 16)
                hold(gathered, 16 * RUNS * (t + 3))
                hold(scattered, 16 * Q * (t + 1))

            for k in range(KQ):
                pool.memset(quarter_no[k * QUAD:(k + 1) * QUAD, :], float(k)).then_inc(quarter_made, 1)
            pool.wait_ge(quarter_made, KQ)
            gather(0)
            keep(0)
            hold(gathered, 16 * RUNS)
            gather(1)
            hold(gathered, 16 * RUNS * 2)
            all_tiles(pool, tile)

        @block.scalar
        def _(act):
            def x_hi(t, c):
                act.wait_ge(xt_ready, DC * t + c + 1)
                wait(act, gu_done, MC * t)
                act.activation(xT_hi[:, c, :], xT[:, c, :], ACT.Copy).then_inc(xt_hi, 1)

            def gate_up_hi(t, j):
                cols = slice(j * P, (j + 1) * P)
                act.wait_ge(gu_loaded, 16 * 2 * KQ * (t + 1))
                wait(act, gu_done, MC * (t - 1) + j + 1)
                act.activation(gu_hi[:, :, :, cols], gu_raw[:, :, :, cols].rearrange("p n c m -> p c n m"), ACT.Copy
                               ).then_inc(guhi_ready, 1)

            def down_hi(t, k):
                act.wait_ge(d_loaded, 16 * (t + 1))
                wait(act, down_done, OUT_GROUPS * t)
                act.activation(d_hi[:, k, :], d_raw[:, k, :], ACT.Copy).then_inc(dhi_ready, 1)

            def silu(t, j):
                act.wait_ge(gu_done, MC * t + j + 1)
                wait(act, h_ready, MC * t + j - (1 if j else 2 - MC % 2))
                act.activation(gated[j % 2][:, :], GU_BANK[2 * j][:, :], ACT.Silu).then_inc(silu_ready, 1)

            def left_rows(t, q):
                act.wait_ge(down_done, OUT_GROUPS * t + NH * q + 1)
                if q == 0:
                    act.wait_ge(entry_kept, KQ * (t + 1))
                    wait(act, scattered, 16 * Q * t)
                act.activation(rows_out[:, q, 0:512], D_BANK[0][:, :], ACT.Copy,
                               scale=entry_now[:, q, 1:2].bitcast(F32)).then_inc(left_ready, 1)

            def tile(t):
                for k in range(MC):
                    down_hi(t, k)
                    silu(t, k)
                left_rows(t, 0)
                gate_up_hi(t + 1, 0)
                for c in range(DC):
                    x_hi(t + 1, c)
                    if c in ROWS_AFTER:
                        left_rows(t, 1 + ROWS_AFTER.index(c))
                for j in range(1, MC):
                    gate_up_hi(t + 1, j)

            gate_up_hi(0, 0)
            for c in range(DC):
                x_hi(0, c)
            for j in range(1, MC):
                gate_up_hi(0, j)
            all_tiles(act, tile)

        @block.vector
        def _(dve):
            def transpose_rows(t, c):
                if c == 0:
                    dve.wait_ge(gathered, 16 * RUNS * (t + 1))
                    wait(dve, xt_lo, DC * t)
                dve.transpose(xT[:, c, :].rearrange("p (m r) -> p m r", r=QUAD), xg[:, :, c * QUAD:(c + 1) * QUAD]
                              ).then_inc(xt_ready, 1)

            def x_lo(t, c):
                dve.wait_ge(xt_hi, DC * t + c + 1)
                dve.tensor_tensor(xT_lo[:, c, :], xT[:, c, :], xT_hi[:, c, :].bitcast(F32), ALU.subtract
                                  ).then_inc(xt_lo, 1)

            def gate_up_lo(t, j):
                cols = slice(j * P, (j + 1) * P)
                dve.wait_ge(guhi_ready, MC * t + j + 1)
                dve.tensor_tensor(gu_lo[:, :, :, cols], gu_raw[:, :, :, cols].rearrange("p n c m -> p c n m"),
                                  gu_hi[:, :, :, cols].bitcast(F32), ALU.subtract).then_inc(gulo_ready, 1)

            def down_lo(t, k):
                dve.wait_ge(dhi_ready, MC * t + k + 1)
                dve.tensor_tensor(d_lo[:, k, :], d_raw[:, k, :], d_hi[:, k, :].bitcast(F32), ALU.subtract
                                  ).then_inc(dlo_ready, 1)

            def hidden(t, j):
                dve.wait_ge(silu_ready, MC * t + j + 1)
                wait(dve, hlo_ready, MC * t + j)
                dve.tensor_tensor(h[:, :], GU_BANK[2 * j + 1][:, :], gated[j % 2][:, :], ALU.mult).then_inc(h_ready, 1)
                dve.wait_ge(h_ready, MC * t + j + 1)
                wait(dve, down_done, OUT_GROUPS * t)
                dve.tensor_copy(h_hi[:, j, :], h[:, :]).then_inc(hhi_ready, 1)
                dve.wait_ge(hhi_ready, MC * t + j + 1)
                dve.tensor_tensor(h_lo[:, j, :], h[:, :], h_hi[:, j, :].bitcast(F32), ALU.subtract).then_inc(hlo_ready, 1)

            def right_rows(t, q):
                dve.wait_ge(down_done, OUT_GROUPS * t + NH * q + 2)
                if q == 0:
                    dve.wait_ge(entry_kept, KQ * (t + 1))
                    wait(dve, scattered, 16 * Q * t)
                dve.tensor_scalar(rows_out[:, q, 512:1024], D_BANK[1][:, :], entry_now[:, q, 1:2].bitcast(F32), None,
                                  ALU.mult).then_inc(right_ready, 1)

            def tile(t):
                for k in range(MC):
                    down_lo(t, k)
                    hidden(t, k)
                    for c in ((0, 1, 2, 3), (4, 5, 6, 7), ())[k]:
                        transpose_rows(t + 1, c)
                right_rows(t, 0)
                gate_up_lo(t + 1, 0)
                for c in range(DC):
                    x_lo(t + 1, c)
                    if c in ROWS_AFTER:
                        right_rows(t, 1 + ROWS_AFTER.index(c))
                for j in range(1, MC):
                    gate_up_lo(t + 1, j)

            gate_up_lo(0, 0)
            for c in range(DC):
                transpose_rows(0, c)
                x_lo(0, c)
            for j in range(1, MC):
                gate_up_lo(0, j)
            all_tiles(dve, tile)

        @block.tensor
        def _(pe):
            def gate_up(t, j, cols):
                pe.wait_ge(gulo_ready, MC * t + j + 1)
                wait(pe, h_ready, MC * (t - 1) + j + 1)
                for n, bank in enumerate(GU_BANK[2 * j:2 * j + 2]):
                    for c in range(DC):
                        if j == 0 and n == 0:
                            pe.wait_ge(xt_lo, DC * t + c + 1)
                        for w, v in ((gu_hi, xT_hi), (gu_hi, xT_lo), (gu_lo, xT_hi)):
                            last = nc.tensor.matmul(bank[:, 0:cols], w[:, c, n, j * P:(j + 1) * P], v[:, c, 0:cols],
                                                    start=(c == 0 and w is gu_hi and v is xT_hi),
                                                    stop=(c == DC - 1 and w is gu_lo))
                last.then_inc(gu_done, 1)

            def down(t, g, ks, cols=512):
                q, n = divmod(g, NH)
                if ks[0] == 0:
                    wait(pe, (left_ready, right_ready)[n], Q * t + q)
                for k in ks:
                    if g == 0:
                        pe.wait_ge(dlo_ready, MC * t + k + 1)
                        pe.wait_ge(hlo_ready, MC * t + k + 1)
                    for v, w in ((h_hi, d_hi), (h_hi, d_lo), (h_lo, d_hi)):
                        last = nc.tensor.matmul(D_BANK[n][:, 0:cols], v[:, k, q * P:(q + 1) * P],
                                                w[:, k, n * 512:n * 512 + cols],
                                                start=(k == ks[0] == 0 and v is h_hi and w is d_hi),
                                                stop=(k == MC - 1 and v is h_lo))
                if ks[-1] == MC - 1:
                    last.then_inc(down_done, 1)

            def products(t, cols):
                for j in range(MC):
                    gate_up(t, j, cols)
                early, late = list(range(MC - 1)), [MC - 1]
                down(t, 0, early)
                down(t, 1, early)
                down(t, 0, late)
                down(t, 1, late)
                for g in range(2, OUT_GROUPS):
                    if g // NH * P < cols:
                        down(t, g, early + late)
                    else:
                        empty_group(t, g)

            def empty_group(t, g):
                q, n = divmod(g, NH)
                wait(pe, (left_ready, right_ready)[n], Q * t + q)
                nc.tensor.matmul(D_BANK[n][:, 0:P], h_hi[:, 0, 0:P], d_hi[:, 0, 0:P], start=True, stop=True
                                 ).then_inc(down_done, 1)

            def tile(t):
                size = pe.value_load(sched_row[0:1, bass.ds(4 * t + 3, 1)], min_val=0, max_val=2)
                with pe.If(size > 1):
                    products(t, HALF_TILE)
                with pe.Else():
                    with pe.If(size > 0):
                        products(t, SHORT)
                    with pe.Else():
                        products(t, SLOT_ROWS)

            all_tiles(pe, tile)


_INS = ["x", "ctx_512", "L0_xattn_Wc", "L0_xattn_bc", "L0_ffn_gate_kernel", "L0_ffn_gate_proj", "L0_ffn_up_proj",
        "L0_ffn_down_proj"]


def kernel(**inputs):
    import numpy as _np
    import concourse.bacc as _bacc
    from concourse import mybir as _mybir
    from concourse.bass_utils import run_bass_kernel_spmd as _run

    nc = _bacc.Bacc("TRN2", target_bir_lowering=False, num_devices=1, dynamic_dma_scratch_size=DMA_RING)
    arrays, args = {}, []
    for name in _INS:
        a = _np.ascontiguousarray(inputs[name])
        arrays[f"in_{name}"] = a
        args.append(nc.dram_tensor(f"in_{name}", a.shape, _mybir.dt.from_np(a.dtype), kind="ExternalInput").ap())
    B, S, D = inputs["x"].shape
    out = nc.dram_tensor("out_rows", (B * S + SLOT_ROWS, D), F32, kind="ExternalOutput").ap()
    moe_block(nc, *args, out)
    r = _run(nc, [arrays], core_ids=[0])
    return r.results[0]["out_rows"][:B * S].reshape(B, S, D)
```
